# Optimizing a Trainium2 kernel written in Bass

```python
import numpy as np
import jax
import jax.numpy as jnp

def _softmax(x, axis=-1):
    return jax.nn.softmax(x, axis=axis)

def _gelu(x):
    return jax.nn.gelu(x, approximate=True)

def _silu(x):
    return jax.nn.silu(x)

def _sigmoid(x):
    return jax.nn.sigmoid(x)

def _layernorm(x, axis=-1, eps=1e-05):
    m = jnp.mean(x, axis=axis, keepdims=True)
    v = jnp.var(x, axis=axis, keepdims=True)
    return (x - m) / jnp.sqrt(v + eps)

def _scatter_add(tgt, idx, src, axis=0):
    return tgt.at[idx].add(src)

def _segment_sum(src, seg, n):
    return jax.ops.segment_sum(src, seg, n)
kernel_name = 'mk_hybrid_d1_jaxref_r8_44caf8'

def setup_inputs(seed: int=0):
    np.random.seed(seed)
    _w = jnp.asarray

    def _L0_attn_a_setup():
        import jax, jax.numpy as jnp
        import numpy as np
        H = 16
        NOPE = 128
        ROPE = 64
        VD = 128
        KVR = 64
        QKD = NOPE + ROPE
        EPS = 1e-06

        def rms_norm(x, w):
            nrm = jax.lax.rsqrt(jnp.mean(x.astype(jnp.float32) ** 2, axis=-1, keepdims=True) + EPS)
            return (x.astype(jnp.float32) * nrm).astype(x.dtype) * w

        def rope_cos_sin(T, dim, base=10000.0):
            inv = 1.0 / base ** (jnp.arange(0, dim, 2, dtype=jnp.float32) / dim)
            f = jnp.outer(jnp.arange(T, dtype=jnp.float32), inv)
            emb = jnp.concatenate([f, f], axis=-1)
            return (jnp.cos(emb), jnp.sin(emb))

        def rotate_half(x):
            x1, x2 = jnp.split(x, 2, axis=-1)
            return jnp.concatenate([-x2, x1], axis=-1)

        def apply_rope(x, cos, sin):
            return x * cos[None, None] + rotate_half(x) * sin[None, None]
        key = jax.random.key(seed)
        ks = jax.random.split(key, 6)
        B, T, D = (2, 256, 256)
        s = 0.02
        return {'x': jax.random.normal(ks[0], (B, T, D), jnp.float32), 'wq': jax.random.normal(ks[1], (D, H * QKD), jnp.float32) * s, 'wkv_a': jax.random.normal(ks[2], (D, KVR + ROPE), jnp.float32) * s, 'wkv_b': jax.random.normal(ks[3], (KVR, H * (NOPE + VD)), jnp.float32) * s, 'wo': jax.random.normal(ks[4], (H * VD, D), jnp.float32) * s, 'kv_norm_w': jnp.ones((KVR,), jnp.float32)}
    _L0_attn_a_in = _L0_attn_a_setup()

    def _L0_attn_b_setup():
        import jax, jax.numpy as jnp
        import numpy as np
        import math
        H = 256
        NH = 16
        HD = H // NH
        THETA = 10000.0

        def rotate_half(x):
            x1, x2 = (x[..., :HD // 2], x[..., HD // 2:])
            return jnp.concatenate((-x2, x1), axis=-1)

        def rope_tables(seq_len, dtype):
            inv_freq = 1.0 / THETA ** (np.arange(0, HD, 2, dtype=np.float32) / HD)
            t = np.arange(seq_len, dtype=np.float32)
            freqs = np.einsum('i,j->ij', t, inv_freq)
            emb = np.concatenate((freqs, freqs), axis=-1)
            return (jnp.asarray(np.cos(emb), dtype), jnp.asarray(np.sin(emb), dtype))
        key = jax.random.key(seed)
        ks = jax.random.split(key, 5)
        B, S = (2, 256)
        scale = 1.0 / math.sqrt(H)
        return {'hidden_states': jax.random.normal(ks[0], (B, S, H), jnp.float32), 'Wq': jax.random.normal(ks[1], (H, H), jnp.float32) * scale, 'Wk': jax.random.normal(ks[2], (H, H), jnp.float32) * scale, 'Wv': jax.random.normal(ks[3], (H, H), jnp.float32) * scale, 'Wo': jax.random.normal(ks[4], (H, H), jnp.float32) * scale}
    _L0_attn_b_in = _L0_attn_b_setup()

    def _L0_ffn_setup():
        import jax, jax.numpy as jnp
        import numpy as np
        TOP_K = 4
        key = jax.random.key(seed)
        ks = jax.random.split(key, 8)
        B, S, H = (1, 128, 256)
        E, I = (60, 176)
        I_SH = 704
        s = 0.02
        return {'hidden_states': jax.random.normal(ks[0], (B, S, H), jnp.float32), 'gate_w': jax.random.normal(ks[1], (E, H), jnp.float32) * s, 'shared_gate_w': jax.random.normal(ks[2], (1, H), jnp.float32) * s, 'w13': jax.random.normal(ks[3], (E, 2 * I, H), jnp.float32) * s, 'w2': jax.random.normal(ks[4], (E, H, I), jnp.float32) * s, 'se_gate_up_w': jax.random.normal(ks[5], (2 * I_SH, H), jnp.float32) * s, 'se_down_w': jax.random.normal(ks[6], (H, I_SH), jnp.float32) * s}
    _L0_ffn_in = _L0_ffn_setup()
    _d = {'L0_attn_a_x': _L0_attn_a_in['x'], 'L0_attn_a_wq': _L0_attn_a_in['wq'], 'L0_attn_a_wkv_a': _L0_attn_a_in['wkv_a'], 'L0_attn_a_wkv_b': _L0_attn_a_in['wkv_b'], 'L0_attn_a_wo': _L0_attn_a_in['wo'], 'L0_attn_a_kv_norm_w': _L0_attn_a_in['kv_norm_w'], 'L0_attn_b_Wq': _L0_attn_b_in['Wq'], 'L0_attn_b_Wk': _L0_attn_b_in['Wk'], 'L0_attn_b_Wv': _L0_attn_b_in['Wv'], 'L0_attn_b_Wo': _L0_attn_b_in['Wo'], 'L0_ffn_gate_w': _L0_ffn_in['gate_w'], 'L0_ffn_shared_gate_w': _L0_ffn_in['shared_gate_w'], 'L0_ffn_w13': _L0_ffn_in['w13'], 'L0_ffn_w2': _L0_ffn_in['w2'], 'L0_ffn_se_gate_up_w': _L0_ffn_in['se_gate_up_w'], 'L0_ffn_se_down_w': _L0_ffn_in['se_down_w']}
    _x0 = _d['L0_attn_a_x']
    _d['L0_attn_a_x'] = jax.random.normal(jax.random.fold_in(jax.random.key(seed), 1), (4, 256, 256), dtype=_x0.dtype)
    del _x0
    return _d

def reference(L0_attn_a_x, L0_attn_a_wq, L0_attn_a_wkv_a, L0_attn_a_wkv_b, L0_attn_a_wo, L0_attn_a_kv_norm_w, L0_attn_b_Wq, L0_attn_b_Wk, L0_attn_b_Wv, L0_attn_b_Wo, L0_ffn_gate_w, L0_ffn_shared_gate_w, L0_ffn_w13, L0_ffn_w2, L0_ffn_se_gate_up_w, L0_ffn_se_down_w):

    def _L0_attn_a_ref(x, wq, wkv_a, wkv_b, wo, kv_norm_w):
        import jax, jax.numpy as jnp
        import numpy as np
        H = 16
        NOPE = 128
        ROPE = 64
        VD = 128
        KVR = 64
        QKD = NOPE + ROPE
        EPS = 1e-06

        def rms_norm(x, w):
            nrm = jax.lax.rsqrt(jnp.mean(x.astype(jnp.float32) ** 2, axis=-1, keepdims=True) + EPS)
            return (x.astype(jnp.float32) * nrm).astype(x.dtype) * w

        def rope_cos_sin(T, dim, base=10000.0):
            inv = 1.0 / base ** (jnp.arange(0, dim, 2, dtype=jnp.float32) / dim)
            f = jnp.outer(jnp.arange(T, dtype=jnp.float32), inv)
            emb = jnp.concatenate([f, f], axis=-1)
            return (jnp.cos(emb), jnp.sin(emb))

        def rotate_half(x):
            x1, x2 = jnp.split(x, 2, axis=-1)
            return jnp.concatenate([-x2, x1], axis=-1)

        def apply_rope(x, cos, sin):
            return x * cos[None, None] + rotate_half(x) * sin[None, None]
        B, T, D = x.shape
        q = (x @ wq).reshape(B, T, H, QKD)
        q_nope, q_rope = (q[..., :NOPE], q[..., NOPE:])
        kvc = x @ wkv_a
        kv_latent = rms_norm(kvc[..., :KVR], kv_norm_w)
        k_rope_raw = kvc[..., KVR:]
        cos, sin = rope_cos_sin(T, ROPE)
        q_rope = apply_rope(jnp.transpose(q_rope, (0, 2, 1, 3)), cos, sin)
        k_rope = apply_rope(k_rope_raw[:, None], cos, sin)
        kv_full = (kv_latent @ wkv_b).reshape(B, T, H, NOPE + VD)
        k_nope = jnp.transpose(kv_full[..., :NOPE], (0, 2, 1, 3))
        v = jnp.transpose(kv_full[..., NOPE:], (0, 2, 1, 3))
        k = jnp.concatenate([k_nope, jnp.broadcast_to(k_rope, (B, H, T, ROPE))], axis=-1)
        qf = jnp.concatenate([jnp.transpose(q_nope, (0, 2, 1, 3)), q_rope], axis=-1)
        scale = QKD ** (-0.5)
        att = jnp.einsum('bhqd,bhkd->bhqk', qf, k) * scale
        causal = jnp.triu(jnp.full((T, T), -jnp.inf, jnp.float32), k=1)
        att = att + causal[None, None]
        att = jax.nn.softmax(att.astype(jnp.float32), axis=-1).astype(x.dtype)
        y = jnp.einsum('bhqk,bhkd->bhqd', att, v)
        y = jnp.transpose(y, (0, 2, 1, 3)).reshape(B, T, H * VD)
        return y @ wo

    def _L0_attn_b_ref(hidden_states, Wq, Wk, Wv, Wo):
        import jax, jax.numpy as jnp
        import numpy as np
        import math
        H = 256
        NH = 16
        HD = H // NH
        THETA = 10000.0

        def rotate_half(x):
            x1, x2 = (x[..., :HD // 2], x[..., HD // 2:])
            return jnp.concatenate((-x2, x1), axis=-1)

        def rope_tables(seq_len, dtype):
            inv_freq = 1.0 / THETA ** (np.arange(0, HD, 2, dtype=np.float32) / HD)
            t = np.arange(seq_len, dtype=np.float32)
            freqs = np.einsum('i,j->ij', t, inv_freq)
            emb = np.concatenate((freqs, freqs), axis=-1)
            return (jnp.asarray(np.cos(emb), dtype), jnp.asarray(np.sin(emb), dtype))
        B, S, _ = hidden_states.shape

        def proj(W):
            y = jnp.einsum('bsh,oh->bso', hidden_states, W)
            return y.reshape(B, S, NH, HD).transpose(0, 2, 1, 3)
        q, k, v = (proj(Wq), proj(Wk), proj(Wv))
        cos, sin = rope_tables(S, hidden_states.dtype)
        cos, sin = (cos[None, None], sin[None, None])
        q = q * cos + rotate_half(q) * sin
        k = k * cos + rotate_half(k) * sin
        scores = jnp.einsum('bhqd,bhkd->bhqk', q, k) / math.sqrt(HD)
        causal = jnp.triu(jnp.ones((S, S), bool), k=1)
        scores = jnp.where(causal, -jnp.inf, scores)
        attn = jax.nn.softmax(scores, axis=-1)
        out = jnp.einsum('bhqk,bhkd->bhqd', attn, v)
        out = out.transpose(0, 2, 1, 3).reshape(B, S, H)
        return jnp.einsum('bsh,oh->bso', out, Wo)

    def _L0_ffn_ref(hidden_states, gate_w, shared_gate_w, w13, w2, se_gate_up_w, se_down_w):
        import jax, jax.numpy as jnp
        import numpy as np
        TOP_K = 4
        orig_shape = hidden_states.shape
        E, H = gate_w.shape
        I = w2.shape[2]
        x = hidden_states.reshape(-1, H)
        M = x.shape[0]
        gu = x @ se_gate_up_w.T
        I_sh = se_down_w.shape[1]
        shared = jax.nn.silu(gu[:, :I_sh]) * gu[:, I_sh:] @ se_down_w.T
        shared = shared * jax.nn.sigmoid(x @ shared_gate_w.T)
        logits = x @ gate_w.T
        probs = jax.nn.softmax(logits.astype(jnp.float32), axis=-1)
        weights, sel = jax.lax.top_k(probs, TOP_K)
        cw = jnp.zeros((M, E), jnp.float32).at[jnp.arange(M)[:, None], sel].add(weights)

        def step(acc, ews):
            w13_e, w2_e, cw_e = ews
            gu_e = x @ w13_e.T
            h = jax.nn.silu(gu_e[:, :I]) * gu_e[:, I:]
            return (acc + cw_e[:, None] * (h @ w2_e.T), None)
        sparse, _ = jax.lax.scan(step, jnp.zeros((M, H), jnp.float32), (w13, w2, cw.T))
        return (shared + sparse).reshape(orig_shape)
    x = L0_attn_a_x
    x = x + _L0_attn_a_ref(_layernorm(x, axis=-1), L0_attn_a_wq, L0_attn_a_wkv_a, L0_attn_a_wkv_b, L0_attn_a_wo, L0_attn_a_kv_norm_w)
    x = x + _L0_ffn_ref(_layernorm(x, axis=-1), L0_ffn_gate_w, L0_ffn_shared_gate_w, L0_ffn_w13, L0_ffn_w2, L0_ffn_se_gate_up_w, L0_ffn_se_down_w)
    x = x + _L0_attn_b_ref(_layernorm(x, axis=-1), L0_attn_b_Wq, L0_attn_b_Wk, L0_attn_b_Wv, L0_attn_b_Wo)
    x = x + _L0_ffn_ref(_layernorm(x, axis=-1), L0_ffn_gate_w, L0_ffn_shared_gate_w, L0_ffn_w13, L0_ffn_w2, L0_ffn_se_gate_up_w, L0_ffn_se_down_w)
    return x

_drawn_inputs = setup_inputs


def setup_inputs(seed=0):
    import zlib

    import numpy as np

    out = dict(_drawn_inputs(seed))
    spreads = {'L0_attn_a_kv_norm_w': (1.0, 0.6)}
    factors = {'L0_attn_a_wq': 8.0,
     'L0_ffn_gate_w': 8.0,
     'L0_ffn_shared_gate_w': 39.685,
     'L0_ffn_w13': 8.0,
     'L0_ffn_w2': 8.0,
     'L0_ffn_se_gate_up_w': 3.981,
     'L0_ffn_se_down_w': 4.191}
    for name, (base, spread) in spreads.items():
        noise = np.random.default_rng([zlib.crc32(name.encode()), seed]).standard_normal(out[name].shape)
        drawn = base * np.exp(spread * noise) if base else spread * noise
        out[name] = jnp.asarray(drawn.astype(out[name].dtype))
    for name, factor in factors.items():
        out[name] = (out[name] * factor).astype(out[name].dtype)
    return out
```

```python
from contextlib import ExitStack

import numpy as np

import concourse.bass as bass
from concourse import mybir

F32 = mybir.dt.float32
BF16 = mybir.dt.bfloat16
I32 = mybir.dt.int32
U32 = mybir.dt.uint32
ALU = mybir.AluOpType
ACT = mybir.ActivationFunctionType
AX = mybir.AxisListType.X

P = 128
BATCH, SEQ, D = 4, 256, 256
TOK = BATCH * SEQ
NT = TOK // P
DC = D // P
HEADS = 16
PAIRS = HEADS // 2
NOPE, ROPE, VD, KVR = 128, 64, 128, 64
HD = D // HEADS
EXPERTS, TOP, INTER = 60, 4, 176
IC = 96
SHARED_CHUNKS = 6
SLOTS = TOP * TOK // P + EXPERTS
SLOT_DEPTH = 4
GATHER_DEPTH = 8
TURNS = SLOTS // SLOT_DEPTH
LN_EPS, RMS_EPS = 1e-5, 1e-6


def build(nc, a, out):
    with ExitStack() as ctx:
        def sb(name, shape, dt=F32):
            return ctx.enter_context(nc.sbuf_tensor(name, shape, dt))

        def sem(name):
            return ctx.enter_context(nc.semaphore(name))

        g = {"sem": sem}
        g["x"] = sb("x", [P, NT, D])
        g["xn"] = sb("xn", [P, NT, D])
        g["xnT"] = sb("xnT", [P, DC, TOK])
        g["ident"] = sb("ident", [P, P])
        g["mask"] = sb("mask", [P, 2, P], BF16)
        g["halves"] = sb("halves", [P, NT])
        g["loaded_x"] = sem("loaded_x")
        names = {}
        for name in LOADS:
            shape = list(a[name].shape)
            g[name] = sb("w_" + name, shape)
            names[name] = sem("loaded_" + name)
        g["loaded"] = names
        g["norm_sems"] = {name: sem(name) for name in Norm.TOTALS}
        for name, n in (("w_loaded", SLOT_DEPTH), ("x_gathered", SLOT_DEPTH), ("y_stored", SLOT_DEPTH), ("y_gathered", GATHER_DEPTH)):
            g[name] = [sem(f"{name}{j}") for j in range(n)]
        g["xn_dram"] = nc.dram_tensor("xn_rows", (TOK, D), F32, kind="Internal").ap()
        g["y_dram"] = nc.dram_tensor("y_rows", (SLOTS * P, D), F32, kind="Internal").ap()

        with nc.Block() as block:
            @block.sync
            def _(sp):
                sp.dma_start(g["x"][:, :, :], a["x"].rearrange("(n p) d -> p n d", p=P)).then_inc(g["loaded_x"], 16)
                sp.dma_start(g["ident"][:, :], a["ident"]).then_inc(g["loaded_x"], 16)
                sp.dma_start(g["mask"][:, :, :], a["mask"]).then_inc(g["loaded_x"], 16)
                sp.wait_ge(g["loaded_x"], 48)
                for name in LOADS:
                    whole = (slice(None),) * len(a[name].shape)
                    sp.dma_start(g[name][whole], a[name][whole]).then_inc(names[name], 16)

            @block.gpsimd
            def _(pool):
                pool.memset(g["halves"][:, :], -0.5)

        for n, phase in enumerate(PHASES):
            if phase in ("latent", "rotary"):
                attention(nc, g, a, str(n), n, phase == "latent")
            else:
                experts(nc, g, a, str(n), n, PHASES[:n].count("experts"))

        stored = sem("stored")
        with nc.Block() as block:
            @block.sync
            def _(sp):
                sp.dma_start(out.rearrange("(n p) d -> p n d", p=P), g["x"][:, :, :]).then_inc(stored, 16)
                sp.wait_ge(stored, 16)


PHASES = ["latent", "experts", "rotary", "experts"]
LOADS = ["wq_nopeT", "wkT", "wkv_a", "kv_w", "rope_k", "rope_q", "wq_rope", "wvT", "wo_a", "gate", "se_up", "se_down",
         "count", "w_rot", "rope_b", "wo_b"]


class Norm:

    TOTALS = {"ln_stats_done": NT, "ln_mv_done": NT, "ln_var_done": 1, "ln_rstd_done": 1, "ln_xn_done": NT,
              "ln_turned": NT // 2}

    def __init__(self, ctx, nc, g, tag, before):
        sb = lambda name, shape: ctx.enter_context(nc.sbuf_tensor(name + tag, shape, F32))
        self.stats = sb("ln_stats", [P, NT, 6])
        self.mv = sb("ln_mv", [P, NT, 2])
        self.var = sb("ln_var", [P, NT])
        self.rstd = sb("ln_rstd", [P, NT])
        self.sems = g["norm_sems"]
        self.before = before

    def sem(self, name):
        return self.sems["ln_" + name]

    def count(self, name, n):
        return self.before * self.TOTALS["ln_" + name] + n

    def vector(self, dve, g):
        dve.wait_ge(g["loaded_x"], 48)
        for t in range(NT):
            dve.bn_stats(self.stats[:, t, :], g["x"][:, t, :]).then_inc(self.sem("stats_done"), 1)
        for t in range(NT):
            dve.wait_ge(self.sem("stats_done"), self.count("stats_done", t + 1))
            dve.bn_aggr(self.mv[:, t, :], self.stats[:, t, :]).then_inc(self.sem("mv_done"), 1)
        dve.wait_ge(self.sem("mv_done"), self.count("mv_done", NT))
        dve.tensor_scalar(self.var[:, :], self.mv[:, :, 1], LN_EPS, None, ALU.add).then_inc(self.sem("var_done"), 1)
        dve.wait_ge(self.sem("rstd_done"), self.count("rstd_done", 1))
        for t in range(NT):
            dve.tensor_scalar(g["xn"][:, t, :], g["x"][:, t, :], self.mv[:, t, 0:1], self.rstd[:, t:t + 1],
                              ALU.subtract, ALU.mult).then_inc(self.sem("xn_done"), 1)

    def gpsimd(self, pool, g):
        pool.wait_ge(self.sem("var_done"), self.count("var_done", 1))
        pool.tensor_tensor(self.rstd[:, :], self.var[:, :], g["halves"][:, :], ALU.pow).then_inc(self.sem("rstd_done"), 1)

    def tensor(self, pe, g, banks):
        for m in range(NT // 2):
            pe.wait_ge(self.sem("xn_done"), self.count("xn_done", 2 * m + 2))
            for c in range(DC):
                for t in (2 * m, 2 * m + 1):
                    last = pe.transpose(banks[m][:, c * 256 + (t % 2) * P:c * 256 + (t % 2 + 1) * P],
                                        g["xn"][:, t, c * P:(c + 1) * P], g["ident"][:, :])
            last.then_inc(self.sem("turned"), 1)

    def scalar(self, act, g, banks, done):
        for m in range(NT // 2):
            act.wait_ge(self.sem("turned"), self.count("turned", m + 1))
            act.activation(g["xnT"][:, :, m * 256:(m + 1) * 256],
                           banks[m][:, :].rearrange("p (c n) -> p c n", c=DC), ACT.Copy).then_inc(done, 1)


def attention(nc, g, a, tag, before, latent):
    vd = KVR if latent else HD
    KG = 1 if latent else 2
    SCALE = float(NOPE + ROPE) ** -0.5 if latent else float(HD) ** -0.5
    ROT = ROPE if latent else HD
    QUSE = 5 if latent else 3
    TUSE = 4 + PAIRS + (2 if latent else 1) + (0 if latent else 1)
    OC = HEADS * vd // P

    with ExitStack() as ctx:
        def sb(name, shape, dt=F32):
            return ctx.enter_context(nc.sbuf_tensor(name + tag, shape, dt))

        def sem(name):
            return g["sem"](name + tag)

        def psum(name, shape):
            return ctx.enter_context(nc.psum_tensor(name + tag, shape, F32))

        norm = Norm(ctx, nc, g, tag, before)
        T = [psum(f"T{i}", [P, 512]) for i in range(2)]
        Q = [psum(f"Q{i}", [P, 512]) for i in range(2)]
        S = [psum(f"S{i}", [P, 512]) for i in range(2)]
        O = [psum(f"O{i}", [P, 512]) for i in range(2)]

        xs = sb("xs", [P, 2, DC, P])
        q = sb("q", [P, 2, HEADS, P])
        qT = sb("qT", [P, 2, HEADS, P])
        rot1 = sb("rot1", [P, 2, 8 * ROPE])
        rot2 = sb("rot2", [P, 2, 8 * ROPE])
        nmax = sb("nmax", [P, 2, HEADS])
        rsum = sb("rsum", [P, 2, HEADS])
        rinv = sb("rinv", [P, 2, HEADS])
        prob = sb("prob", [P, 2, 2, 2 * P])
        probT = sb("probT", [P, 2, 4 * P])
        o = sb("o", [P, 2, HEADS * vd])
        oT = sb("oT", [P, 2, OC, P])
        if latent:
            wqn = sb("wqn", [P, DC, HEADS * KVR])
            wvo = sb("wvo", [P, PAIRS, D])
            kvc = sb("kvc", [P, NT, P])
            sq = sb("sq", [P, NT, KVR])
            ms = sb("ms", [P, NT])
            ms2 = sb("ms2", [P, NT])
            rr = sb("rr", [P, NT])
            kv = sb("kv", [P, NT, P])
            kT = sb("kT", [P, TOK])
        else:
            kr = sb("kr", [P, D])
            kT = sb("kT", [P, 2, SEQ])
            v = sb("v", [P, 2, D])

        xnT_done = sem("xnT_done")
        staged = sem("staged")
        projected = sem("projected")
        q_read = [sem(f"q_read{i}") for i in range(2)]
        turned = sem("turned")
        t_read = [sem(f"t_read{i}") for i in range(2)]
        q_ready = sem("q_ready")
        kr_ready = sem("kr_ready")
        scored = sem("scored")
        max_done = sem("max_done")
        exp_done = sem("exp_done")
        summed = sem("summed")
        recip = sem("recip")
        o_done = sem("o_done")
        pre_pe = sem("pre_pe")
        pre_act = sem("pre_act")
        pre_dve = sem("pre_dve")
        pre_pool = sem("pre_pool")
        zeroed = sem("zeroed")
        loaded = g["loaded"]
        TB, QB = 2 * TUSE, 2 * QUSE
        WQN_USES = DC * HEADS * KVR // 512
        WVO_USES = PAIRS * D // 512

        def k_slice(b, i, gr):
            if latent:
                return kT[:, bass.ds(b * SEQ, (i + 1) * P)]
            return kT[:, gr, 0:(i + 1) * P]

        def qi(i, n):
            return QUSE * i + n

        def ti(i, n):
            return TUSE * i + n

        START = 1

        T_Q = 0 if latent else 1
        T_P = T_Q + 4
        T_O = T_P + PAIRS

        with nc.Block() as block:
            @block.tensor
            def _(pe):
                for counter in (*q_read, *t_read, summed, turned):
                    pe.sem_inc(counter, START)
                if latent:
                    pe.wait_ge(g["loaded_x"], 48)
                    pe.wait_ge(loaded["wq_nopeT"], 16)
                    pe.wait_ge(loaded["wkT"], 16)
                    n = 0
                    for c in range(DC):
                        for half in range(2):
                            if n >= 2:
                                pe.wait_ge(pre_act, n - 1)
                            for k in range(8):
                                h = 8 * half + k
                                last = pe.matmul(Q[n % 2][:, k * KVR:(k + 1) * KVR],
                                                 g["wq_nopeT"][:, h, c * P:(c + 1) * P],
                                                 g["wkT"][:, h, :], start=True, stop=True)
                            last.then_inc(pre_pe, 1)
                            n += 1
                    pe.wait_ge(loaded["wvT"], 16)
                    pe.wait_ge(loaded["wo_a"], 16)
                    for m in range(WVO_USES):
                        pe.wait_ge(pre_act, n - 1)
                        for j in range(2):
                            for half in range(2):
                                h = 4 * m + 2 * j + half
                                last = pe.matmul(Q[n % 2][half * KVR:(half + 1) * KVR, j * D:(j + 1) * D],
                                                 g["wvT"][:, h, :], g["wo_a"][:, h, :], start=True, stop=True)
                        last.then_inc(pre_pe, 1)
                        n += 1
                norm.tensor(pe, g, [T[0], T[1], S[0], S[1]])
                if latent:
                    pe.wait_ge(loaded["wkv_a"], 16)
                    for m in range(2):
                        pe.wait_ge(xnT_done, 2 * m + 2)
                        for t in range(4):
                            for c in range(DC):
                                last = pe.matmul(O[m][:, t * P:(t + 1) * P],
                                                 g["xnT"][:, c, (4 * m + t) * P:(4 * m + t + 1) * P],
                                                 g["wkv_a"][:, c, :], start=(c == 0), stop=(c == DC - 1))
                        last.then_inc(pre_pe, 1)
                    pe.wait_ge(pre_dve, 7)
                    for m in range(2):
                        for t in range(4):
                            last = pe.transpose(T[m][:, t * P:(t + 1) * P], kv[:, 4 * m + t, :], g["ident"][:, :])
                        last.then_inc(pre_pe, 1)
                    pe.wait_ge(pre_act, WQN_USES + WVO_USES + 4)
                    pe.wait_ge(loaded["wq_rope"], 16)
                else:
                    pe.wait_ge(xnT_done, NT // 2)
                    pe.wait_ge(loaded["w_rot"], 16)
                pe.wait_ge(loaded["wo_b" if not latent else "wo_a"], 16)

                with pe.Fori(0, BATCH) as b:
                    def project(i, n, w, cols, width):
                        u = qi(i, n)
                        pe.wait_ge(q_read[u % 2], START + b * (QB // 2) + u // 2)
                        for c in range(DC):
                            last = pe.matmul(Q[u % 2][:, 0:width], xs[:, i, c, :], w[:, c, cols:cols + width],
                                             start=(c == 0), stop=(c == DC - 1))
                        last.then_inc(projected, 1)

                    def turn_queries(i, gr):
                        u = ti(i, T_Q + gr)
                        pe.wait_ge(t_read[u % 2], START + b * (TB // 2) + u // 2)
                        if latent:
                            at = qi(i, 2 * (gr // 2))
                            pe.wait_ge(q_read[at % 2], START + b * (QB // 2) + at // 2 + 1)
                        pe.wait_ge(q_ready, b * 4 + 2 * i + gr // 2 + 1)
                        for k in range(4):
                            last = pe.transpose(T[u % 2][:, k * P:(k + 1) * P], q[:, i, 4 * gr + k, :], g["ident"][:, :])
                        last.then_inc(turned, 1)

                    def scores(i, p):
                        n = PAIRS * i + p
                        pe.wait_ge(exp_done, START + b * 2 * PAIRS + max(n - 1, 0))
                        at = ti(i, T_Q + p // 2)
                        pe.wait_ge(t_read[at % 2], START + b * (TB // 2) + at // 2 + 1)
                        w = (i + 1) * P
                        for j in range(2):
                            h = 2 * p + j
                            to = S[n % 2][:, j * 256:j * 256 + w]
                            pe.matmul(to, qT[:, i, h, :], k_slice(b, i, h // 8), start=True, stop=True)
                            last = pe.matmul(S[n % 2][:, j * 256 + i * P:j * 256 + w], g["mask"][:, 0, :],
                                             g["mask"][:, 1, :], start=False, stop=True, skip_group_check=True)
                        last.then_inc(scored, 1)

                    def turn_probs(i, p):
                        n, u = PAIRS * i + p, ti(i, T_P + p)
                        pe.wait_ge(exp_done, START + b * 2 * PAIRS + n + 1)
                        pe.wait_ge(t_read[u % 2], START + b * (TB // 2) + u // 2)
                        for j in range(2):
                            for kb in range(i + 1):
                                at = (j * (i + 1) + kb) * P
                                last = pe.transpose(T[u % 2][:, at:at + P], prob[:, n % 2, j, kb * P:(kb + 1) * P],
                                                    g["ident"][:, :])
                        last.then_inc(turned, 1)

                    def values(i, p):
                        n = PAIRS * i + p
                        at = ti(i, T_P + p)
                        pe.wait_ge(t_read[at % 2], START + b * (TB // 2) + at // 2 + 1)
                        if p % 4 == 0:
                            pe.wait_ge(o_done, START + b * 4 + max(2 * i + p // 4 - 1, 0))
                        for j in range(2):
                            h = 2 * p + j
                            for kb in range(i + 1):
                                at = (j * (i + 1) + kb) * P
                                if latent:
                                    val = kv[:, bass.ds(b * 2 + kb, 1), 0:KVR].rearrange("p a n -> p (a n)")
                                else:
                                    val = v[:, kb, h * HD:(h + 1) * HD]
                                last = pe.matmul(O[p // 4][:, (h % 8) * vd:(h % 8 + 1) * vd],
                                                 probT[:, n % 2, at:at + P], val,
                                                 start=(kb == 0), stop=(kb == i))
                        last.then_inc(summed, 1)

                    def turn_outputs(i):
                        for m in range((OC + 3) // 4):
                            u = ti(i, T_O + m)
                            pe.wait_ge(t_read[u % 2], START + b * (TB // 2) + u // 2)
                            pe.wait_ge(o_done, START + b * 4 + 2 * i + (m + 1 if latent else 2))
                            for k in range(min(4, OC)):
                                last = pe.transpose(T[u % 2][:, k * P:(k + 1) * P],
                                                    o[:, i, (4 * m + k) * P:(4 * m + k + 1) * P], g["ident"][:, :])
                            last.then_inc(turned, 1)

                    def output(i):
                        u = qi(i, QUSE - 1)
                        pe.wait_ge(q_read[u % 2], START + b * (QB // 2) + u // 2)
                        for m in range((OC + 3) // 4):
                            at = ti(i, T_O + m)
                            pe.wait_ge(t_read[at % 2], START + b * (TB // 2) + at // 2 + 1)
                        w = wvo if latent else g["wo_b"]
                        for c in range(OC):
                            last = pe.matmul(Q[u % 2][:, 0:D], oT[:, i, c, :], w[:, c, :],
                                             start=(c == 0), stop=(c == OC - 1))
                        last.then_inc(projected, 1)

                    for i in range(2):
                        pe.wait_ge(staged, b * 2 + i + 1)
                        if latent:
                            project(i, 0, wqn, 0, 512)
                            project(i, 1, g["wq_rope"], 0, 512)
                            project(i, 2, wqn, 512, 512)
                            turn_queries(i, 0)
                            project(i, 3, g["wq_rope"], 512, 512)
                            for gr in range(1, 4):
                                turn_queries(i, gr)
                        else:
                            project(i, 0, g["w_rot"], 0, 512)
                            project(i, 1, g["w_rot"], 512, 256)
                            u = ti(i, 0)
                            pe.wait_ge(t_read[u % 2], START + b * (TB // 2) + u // 2)
                            pe.wait_ge(kr_ready, b * 2 + i + 1)
                            for k in range(2):
                                last = pe.transpose(T[u % 2][:, k * P:(k + 1) * P], kr[:, k * P:(k + 1) * P],
                                                    g["ident"][:, :])
                            last.then_inc(turned, 1)
                            for gr in range(4):
                                turn_queries(i, gr)
                            pe.wait_ge(t_read[u % 2], START + b * (TB // 2) + u // 2 + 1)
                            at = qi(i, 1)
                            pe.wait_ge(q_read[at % 2], START + b * (QB // 2) + at // 2 + 1)
                        scores(i, 0)
                        scores(i, 1)
                        for p in range(PAIRS + 1):
                            if p < PAIRS:
                                turn_probs(i, p)
                            if p + 2 < PAIRS:
                                scores(i, p + 2)
                            if p > 0:
                                values(i, p - 1)
                        turn_outputs(i)
                        output(i)

            @block.scalar
            def _(act):
                act.sem_inc(exp_done, START)
                n = 0
                if latent:
                    for c in range(DC):
                        for half in range(2):
                            act.wait_ge(pre_pe, n + 1)
                            act.activation(wqn[:, c, half * 512:(half + 1) * 512], Q[n % 2][:, :],
                                           ACT.Copy).then_inc(pre_act, 1)
                            n += 1
                    for m in range(WVO_USES):
                        act.wait_ge(pre_pe, n + 1)
                        act.activation(wvo[:, 2 * m:2 * m + 2, :],
                                       Q[n % 2][:, :].rearrange("p (j d) -> p j d", j=2),
                                       ACT.Copy).then_inc(pre_act, 1)
                        n += 1
                norm.scalar(act, g, [T[0], T[1], S[0], S[1]], xnT_done)
                if latent:
                    for m in range(2):
                        act.wait_ge(pre_pe, n + 1)
                        act.activation(kvc[:, 4 * m:4 * m + 4, :], O[m][:, :].rearrange("p (t n) -> p t n", t=4),
                                       ACT.Copy).then_inc(pre_act, 1)
                        n += 1
                    for m in range(2):
                        act.wait_ge(pre_pe, n + 1)
                        act.activation(kT[:, m * 512:(m + 1) * 512], T[m][:, :], ACT.Copy).then_inc(pre_act, 1)
                        n += 1

                with act.Fori(0, BATCH) as b:
                    def unrotated(i, half):
                        u = qi(i, 2 * half)
                        act.wait_ge(projected, b * QB + u + 1)
                        act.activation(q[:, i, 8 * half:8 * half + 8, 0:KVR],
                                       Q[u % 2][:, :].rearrange("p (h n) -> p h n", h=8),
                                       ACT.Copy, scale=SCALE).then_inc(q_read[u % 2], 1)

                    def queries(i, gr):
                        u = ti(i, T_Q + gr)
                        act.wait_ge(turned, START + b * TB + u + 1)
                        act.activation(qT[:, i, 4 * gr:4 * gr + 4, :],
                                       T[u % 2][:, :].rearrange("p (h n) -> p h n", h=4),
                                       ACT.Copy).then_inc(t_read[u % 2], 1)

                    def softmax(i, p):
                        n = PAIRS * i + p
                        act.wait_ge(max_done, b * 2 * PAIRS + n + 1)
                        act.wait_ge(turned, START + b * TB + (ti((n - 2) // PAIRS, T_P + (n - 2) % PAIRS) + 1 if n >= 2 else 0))
                        w = (i + 1) * P
                        for j in range(2):
                            h = 2 * p + j
                            last = act.activation(prob[:, n % 2, j, 0:w], S[n % 2][:, j * 256:j * 256 + w], ACT.Exp,
                                                  bias=nmax[:, i, h:h + 1], scale=1.0,
                                                  accum_out=rsum[:, i, h:h + 1])
                        last.then_inc(exp_done, 1)

                    def outputs(i):
                        for m in range((OC + 3) // 4):
                            u = ti(i, T_O + m)
                            act.wait_ge(turned, START + b * TB + u + 1)
                            k = min(4, OC)
                            act.activation(oT[:, i, 4 * m:4 * m + k, :],
                                           T[u % 2][:, 0:k * P].rearrange("p (c n) -> p c n", c=k),
                                           ACT.Copy).then_inc(t_read[u % 2], 1)

                    for i in range(2):
                        if latent:
                            unrotated(i, 0)
                            unrotated(i, 1)
                        for gr in range(4):
                            queries(i, gr)
                        for p in range(PAIRS):
                            softmax(i, p)
                        outputs(i)

            @block.gpsimd
            def _(pool):
                if not latent:
                    pool.memset(q[:, :, :, :], 0.0).then_inc(zeroed, 1)
                norm.gpsimd(pool, g)
                if latent:
                    pool.wait_ge(pre_dve, 3)
                    pool.tensor_tensor(rr[:, :], ms2[:, :], g["halves"][:, :], ALU.pow).then_inc(pre_pool, 1)
                for i in range(2):
                    pool.wait_ge(xnT_done, 1)
                    pool.tensor_copy(xs[:, i, :, :], g["xnT"][:, :, i * P:(i + 1) * P]).then_inc(staged, 1)
                pool.wait_ge(xnT_done, NT // 2)
                with pool.Fori(0, BATCH - 1) as b:
                    for i in range(2):
                        pool.wait_ge(projected, b * QB + qi(i, QUSE - 1))
                        pool.tensor_copy(xs[:, i, :, :],
                                         g["xnT"][:, :, bass.ds(b * SEQ + SEQ + i * P, P)]).then_inc(staged, 1)

            @block.vector
            def _(dve):
                dve.sem_inc(o_done, START)
                norm.vector(dve, g)
                if latent:
                    step = 0

                    def own(ins):
                        nonlocal step
                        ins.then_inc(pre_dve, 1)
                        step += 1
                        dve.wait_ge(pre_dve, step)

                    dve.wait_ge(pre_act, WQN_USES + WVO_USES + 2)
                    own(dve.tensor_tensor(sq[:, :, :], kvc[:, :, 0:KVR], kvc[:, :, 0:KVR], ALU.mult))
                    own(dve.tensor_reduce(ms[:, :], sq[:, :, :], AX, ALU.add))
                    own(dve.tensor_scalar(ms2[:, :], ms[:, :], 1.0 / KVR, RMS_EPS, ALU.mult, ALU.add))
                    dve.wait_ge(pre_pool, 1)
                    dve.wait_ge(loaded["kv_w"], 16)
                    dve.wait_ge(loaded["rope_k"], 16)
                    own(dve.tensor_tensor(sq[:, :, :], kvc[:, :, 0:KVR],
                                          rr[:, :].unsqueeze(2).broadcast_to([P, NT, KVR]), ALU.mult))
                    own(dve.tensor_tensor(kv[:, :, 0:KVR], sq[:, :, :],
                                          g["kv_w"][:, :].unsqueeze(1).broadcast_to([P, NT, KVR]), ALU.mult))
                    raw = kvc[:, :, KVR:P].rearrange("p (b i) n -> p b i n", i=2)
                    r1 = rot1[:, 0, :].rearrange("p (b i n) -> p b i n", b=BATCH, i=2)
                    r2 = rot2[:, 0, :].rearrange("p (b i n) -> p b i n", b=BATCH, i=2)
                    H = ROPE // 2
                    for i in range(2):
                        cos, sin = (g["rope_k"][:, i, s, :].unsqueeze(1) for s in range(2))
                        dve.tensor_tensor(r1[:, :, i, :], raw[:, :, i, :], cos.broadcast_to([P, BATCH, ROPE]), ALU.mult)
                        for lo, hi in ((0, H), (H, 0)):
                            last = dve.tensor_tensor(r2[:, :, i, lo:lo + H], raw[:, :, i, hi:hi + H],
                                                     sin[:, :, lo:lo + H].broadcast_to([P, BATCH, H]), ALU.mult)
                    own(last)
                    own(dve.tensor_tensor(kv[:, :, KVR:P], rot1[:, 0, :].rearrange("p (t n) -> p t n", t=NT),
                                          rot2[:, 0, :].rearrange("p (t n) -> p t n", t=NT), ALU.add))
                    dve.wait_ge(loaded["rope_q"], 16)
                else:
                    dve.wait_ge(loaded["rope_b"], 16)
                    dve.wait_ge(zeroed, 1)

                with dve.Fori(0, BATCH) as b:
                    def rotate_latent(i, half):
                        u = qi(i, 1 + 2 * half)
                        dve.wait_ge(projected, b * QB + u + 1)
                        src = Q[u % 2][:, :].rearrange("p (h n) -> p h n", h=8)
                        r1 = rot1[:, half, :].rearrange("p (h n) -> p h n", h=8)
                        r2 = rot2[:, half, :].rearrange("p (h n) -> p h n", h=8)
                        cos, sin = (g["rope_q"][:, i, s, :].unsqueeze(1) for s in range(2))
                        H = ROPE // 2
                        dve.tensor_tensor(r1, src, cos.broadcast_to([P, 8, ROPE]), ALU.mult)
                        for lo, hi in ((0, H), (H, 0)):
                            last = dve.tensor_tensor(r2[:, :, lo:lo + H], src[:, :, hi:hi + H],
                                                     sin[:, :, lo:lo + H].broadcast_to([P, 8, H]), ALU.mult)
                        last.then_inc(q_read[u % 2], 1)
                        dve.wait_ge(q_read[u % 2], START + b * (QB // 2) + u // 2 + 1)
                        dve.tensor_tensor(q[:, i, 8 * half:8 * half + 8, KVR:P], r1, r2, ALU.add).then_inc(q_ready, 1)

                    def rotate_all(i):
                        u = qi(i, 0)
                        dve.wait_ge(projected, b * QB + u + 1)
                        src = Q[u % 2][:, :].rearrange("p (s h n) -> p s h n", s=2, h=HEADS)
                        r1 = rot1[:, 0, :].rearrange("p (s h n) -> p s h n", s=2, h=HEADS)
                        r2 = rot2[:, 0, :].rearrange("p (s h n) -> p s h n", s=2, h=HEADS)
                        H = HD // 2
                        for s in range(2):
                            cos, sin = (g["rope_b"][:, i, s, f, :].unsqueeze(1) for f in range(2))
                            dve.tensor_tensor(r1[:, s], src[:, s], cos.broadcast_to([P, HEADS, HD]), ALU.mult)
                            for lo, hi in ((0, H), (H, 0)):
                                last = dve.tensor_tensor(r2[:, s, :, lo:lo + H], src[:, s, :, hi:hi + H],
                                                         sin[:, :, lo:lo + H].broadcast_to([P, HEADS, H]), ALU.mult)
                        last.then_inc(q_read[u % 2], 1)
                        dve.wait_ge(q_read[u % 2], START + b * (QB // 2) + u // 2 + 1)
                        dve.tensor_tensor(kr[:, :], rot1[:, 0, D:2 * D], rot2[:, 0, D:2 * D], ALU.add).then_inc(kr_ready, 1)
                        for half in range(2):
                            start = (i * HEADS + 8 * half) * P
                            diagonal = bass.AP(q, start, [[2 * HEADS * P, P], [P + HD, 8], [1, HD]])
                            at = slice(half * P, (half + 1) * P)
                            dve.tensor_tensor(diagonal, rot1[:, 0, at].rearrange("p (h n) -> p h n", h=8),
                                              rot2[:, 0, at].rearrange("p (h n) -> p h n", h=8),
                                              ALU.add).then_inc(q_ready, 1)

                    def keys_values(i):
                        u = qi(i, 1)
                        dve.wait_ge(projected, b * QB + u + 1)
                        dve.tensor_copy(v[:, i, :], Q[u % 2][:, 0:D]).then_inc(q_read[u % 2], 1)
                        u = ti(i, 0)
                        dve.wait_ge(turned, START + b * TB + u + 1)
                        dve.tensor_copy(kT[:, :, i * P:(i + 1) * P],
                                        T[u % 2][:, 0:2 * P].rearrange("p (k n) -> p k n", k=2)).then_inc(t_read[u % 2], 1)

                    def maxima(i, p):
                        n = PAIRS * i + p
                        dve.wait_ge(scored, b * 2 * PAIRS + n + 1)
                        dve.tensor_reduce(nmax[:, i, 2 * p:2 * p + 2],
                                          S[n % 2][:, :].rearrange("p (j n) -> p j n", j=2)[:, :, 0:(i + 1) * P],
                                          AX, ALU.max, negate=True).then_inc(max_done, 1)

                    def probs(i, p):
                        n, u = PAIRS * i + p, ti(i, T_P + p)
                        dve.wait_ge(turned, START + b * TB + u + 1)
                        dve.wait_ge(summed, START + b * 2 * PAIRS + max(n - 1, 0))
                        w = 2 * (i + 1) * P
                        dve.tensor_copy(probT[:, n % 2, 0:w], T[u % 2][:, 0:w]).then_inc(t_read[u % 2], 1)

                    def normalise(i, m):
                        dve.wait_ge(exp_done, START + b * 2 * PAIRS + PAIRS * i + 4 * m + 4)
                        dve.reciprocal(rinv[:, i, 8 * m:8 * m + 8], rsum[:, i, 8 * m:8 * m + 8]).then_inc(recip, 1)
                        dve.wait_ge(recip, b * 4 + 2 * i + m + 1)
                        dve.wait_ge(summed, START + b * 2 * PAIRS + PAIRS * i + 4 * m + 4)
                        dve.tensor_tensor(o[:, i, m * 8 * vd:(m + 1) * 8 * vd].rearrange("p (h n) -> p h n", h=8),
                                          O[m][:, 0:8 * vd].rearrange("p (h n) -> p h n", h=8),
                                          rinv[:, i, 8 * m:8 * m + 8].unsqueeze(2).broadcast_to([P, 8, vd]),
                                          ALU.mult).then_inc(o_done, 1)

                    def add(i):
                        u = qi(i, QUSE - 1)
                        dve.wait_ge(projected, b * QB + u + 1)
                        x = g["x"][:, bass.ds(b * 2 + i, 1), :].rearrange("p a d -> p (a d)")
                        dve.tensor_tensor(x, Q[u % 2][:, 0:D], x, ALU.add).then_inc(q_read[u % 2], 1)

                    for i in range(2):
                        if latent:
                            rotate_latent(i, 0)
                            rotate_latent(i, 1)
                        else:
                            rotate_all(i)
                            keys_values(i)
                        maxima(i, 0)
                        maxima(i, 1)
                        for p in range(PAIRS):
                            probs(i, p)
                            if p + 2 < PAIRS:
                                maxima(i, p + 2)
                            if p == 5:
                                normalise(i, 0)
                        normalise(i, 1)
                        add(i)


def experts(nc, g, a, tag, before, run):
    with ExitStack() as ctx:
        def sb(name, shape, dt=F32):
            return ctx.enter_context(nc.sbuf_tensor(name + tag, shape, dt))

        def sem(name):
            return g["sem"](name + tag)

        E, K = EXPERTS, TOP
        bank = [ctx.enter_context(nc.psum_tensor(f"bank{i}" + tag, [P, 512], F32)) for i in range(8)]
        norm = Norm(ctx, nc, g, tag, before)
        loaded = g["loaded"]
        ids = sb("ids", [P, SLOTS], U32)
        wts = sb("wts", [P, SLOTS])
        row = sb("row", [1, P], U32)
        place = sb("place", [P, NT * K], I32)

        count = g["count"]
        iota, tri, ones = (count[:, n * P:(n + 1) * P] for n in range(3))
        full = count[:, 3 * P:3 * P + 8]
        tokens = count[:, 3 * P + 8:3 * P + 16]
        index = iota_p = count[:, 3 * P + 16:3 * P + 17]

        with ExitStack() as inner:
            def sb(name, shape, dt=F32):
                return inner.enter_context(nc.sbuf_tensor(name + tag, shape, dt))

            lg = sb("lg", [P, NT, E + 1])
            lgs = sb("lgs", [P, NT, E])
            pr = sb("pr", [P, NT, E])
            small = sb("small", [P, 6, NT])
            top = sb("top", [P, NT, 8])
            best = sb("best", [P, NT, 8], U32)
            bestf = sb("bestf", [P, NT * K])
            onehot = sb("onehot", [P, NT * K, E])
            work = sb("work", [P, NT * K, E])
            chosen = sb("chosen", [P, NT, E])
            base = sb("base", [P, NT + 1, E])
            pos = sb("pos", [P, NT, E])
            over = sb("over", [P, E, 8])
            tiles = sb("tiles", [P, E])
            cum = sb("cum", [P, E])
            begin = sb("begin", [P, E])
            junk = sb("junk", [P, E])
            slot_expert = sb("slot_expert", [P, 2])
            placef = sb("placef", [P, NT * K])
            part = sb("part", [P, 2, NT * K], I32)
            partf = sb("partf", [P, 2, NT * K])
            in_row = sb("in_row", [P, 2, K, P])
            in_slot = sb("in_slot", [P, 2, 3, K, SLOTS])
            sg = sb("sg", [P, 2, 512])
            up = sb("up", [P, 2, 512])
            hT = sb("hT", [P, SHARED_CHUNKS, TOK])

            xnT_done = sem("xnT_done")
            stored = sem("xn_stored")
            logits = sem("logits")
            lg_done = sem("lg_done")
            chain = sem("chain")
            ex_done = sem("ex_done")
            chosen_ready = sem("chosen_ready")
            counted = sem("counted")
            expert_ready = sem("expert_ready")
            expert_turned = sem("expert_turned")
            in_ready = sem("in_ready")
            listed = sem("listed")
            gu = sem("gu")
            gu_read = sem("gu_read")
            sgu_read = sem("sgu_read")
            h_done = sem("h_done")
            shared = sem("shared")
            added = sem("added")
            routed = sem("routed")
            DONE = {}

            with nc.Block() as block:
                @block.sync
                def _(sp):
                    sp.wait_ge(norm.sem("xn_done"), norm.count("xn_done", NT))
                    sp.dma_start(g["xn_dram"].rearrange("(n p) d -> p n d", p=P), g["xn"][:, :, :]).then_inc(stored, 16)
                    sp.wait_ge(stored, 16)

                @block.gpsimd
                def _(pool):
                    norm.gpsimd(pool, g)
                    for n in range(2 * SHARED_CHUNKS):
                        pool.wait_ge(gu_read, 2 * n + 2)
                        pool.tensor_tensor(hT[:, n // 2, (n % 2) * 512:(n % 2 + 1) * 512], sg[:, n % 2, :],
                                           up[:, n % 2, :], ALU.mult).then_inc(h_done, 1)

                @block.tensor
                def _(pe):
                    pe.wait_ge(g["loaded_x"], 48)
                    norm.tensor(pe, g, bank[0:4])
                    pe.wait_ge(xnT_done, NT // 2)
                    pe.wait_ge(loaded["gate"], 16)
                    for t in range(NT):
                        for c in range(DC):
                            last = pe.matmul(bank[0][:, t * (E + 1):(t + 1) * (E + 1)],
                                             g["xnT"][:, c, t * P:(t + 1) * P], g["gate"][:, c, :],
                                             start=(c == 0), stop=(c == DC - 1))
                    last.then_inc(logits, 1)

                    def shared_up(n):
                        ch, half = n // 2, n % 2
                        if n >= 2:
                            pe.wait_ge(gu_read, 2 * (n - 1))
                        for s in range(2):
                            for c in range(DC):
                                col = (s * SHARED_CHUNKS + ch) * P
                                last = pe.matmul(bank[4 + 2 * (n % 2) + s][:, :], g["se_up"][:, c, col:col + P],
                                                 g["xnT"][:, c, half * 512:(half + 1) * 512],
                                                 start=(c == 0), stop=(c == DC - 1))
                        last.then_inc(gu, 1)

                    pe.wait_ge(loaded["se_up"], 16)
                    pe.wait_ge(loaded["count"], 16)
                    for n in range(4):
                        shared_up(n)
                    pe.wait_ge(chosen_ready, 1)
                    pe.matmul(bank[1][:, 0:NT * E], tri, chosen[:, :, :], start=True, stop=True)
                    pe.matmul(bank[2][:, 0:NT * E], ones, chosen[:, :, :], start=True, stop=True).then_inc(counted, 1)
                    for n in range(4, 2 * SHARED_CHUNKS):
                        shared_up(n)
                    pe.wait_ge(expert_ready, 1)
                    pe.matmul(bank[0][0:1, 0:P], slot_expert[:, 1:2], g["ident"][:, :],
                              start=True, stop=True).then_inc(expert_turned, 1)
                    pe.wait_ge(h_done, 2 * SHARED_CHUNKS)
                    pe.wait_ge(gu_read, 4 * SHARED_CHUNKS)
                    pe.wait_ge(loaded["se_down"], 16)
                    for t in range(NT):
                        for c in range(SHARED_CHUNKS):
                            last = pe.matmul(bank[4 + t // 2][:, (t % 2) * D:(t % 2 + 1) * D],
                                             hT[:, c, t * P:(t + 1) * P], g["se_down"][:, c, :],
                                             start=(c == 0), stop=(c == SHARED_CHUNKS - 1))
                        if t % 2:
                            last.then_inc(shared, 1)
                    for t in range(NT):
                        pe.wait_ge(in_ready, t + 1)
                        for k in range(K):
                            last = pe.matmul(bank[3][:, 0:2 * SLOTS].rearrange("p (v s) -> p v s", v=2),
                                             in_row[:, t % 2, k, :], in_slot[:, t % 2, 1:3, k, :],
                                             start=(t == 0 and k == 0), stop=(t == NT - 1 and k == K - 1))
                        last.then_inc(listed, 1)

                @block.scalar
                def _(act):
                    norm.scalar(act, g, bank[0:4], xnT_done)
                    act.wait_ge(logits, 1)
                    act.activation(lg[:, :, :], bank[0][:, 0:NT * (E + 1)].rearrange("p (t e) -> p t e", t=NT),
                                   ACT.Copy).then_inc(lg_done, 1)
                    act.wait_ge(chain, 2)
                    act.activation(pr[:, :, :], lgs[:, :, :], ACT.Exp).then_inc(ex_done, 1)
                    act.activation(small[:, 3, :], lg[:, :, E], ACT.Exp, scale=-1.0).then_inc(ex_done, 1)
                    for n in range(2 * SHARED_CHUNKS):
                        act.wait_ge(gu, n + 1)
                        if n >= 2:
                            act.wait_ge(h_done, n - 1)
                        act.activation(sg[:, n % 2, :], bank[4 + 2 * (n % 2)][:, :], ACT.Silu).then_inc(gu_read, 1)
                        act.activation(up[:, n % 2, :], bank[5 + 2 * (n % 2)][:, :], ACT.Copy).then_inc(gu_read, 1)

                @block.vector
                def _(dve):
                    norm.vector(dve, g)
                    step = 0

                    def own(ins):
                        nonlocal step
                        ins.then_inc(chain, 1)
                        step += 1
                        dve.wait_ge(chain, step)

                    def over_experts(ap):
                        return ap.unsqueeze(2).broadcast_to([P, NT, E])

                    dve.wait_ge(loaded["count"], 16)
                    dve.memset(base[:, 0, :], 0.0)
                    dve.wait_ge(lg_done, 1)
                    own(dve.tensor_reduce(small[:, 0, :], lg[:, :, 0:E], AX, ALU.max, negate=True))
                    own(dve.tensor_tensor(lgs[:, :, :], lg[:, :, 0:E], over_experts(small[:, 0, :]), ALU.add))
                    dve.wait_ge(ex_done, 2)
                    own(dve.tensor_reduce(small[:, 1, :], pr[:, :, :], AX, ALU.add))
                    own(dve.reciprocal(small[:, 2, :], small[:, 1, :]))
                    own(dve.tensor_tensor(lgs[:, :, :], pr[:, :, :], over_experts(small[:, 2, :]), ALU.mult))
                    own(dve.tensor_scalar(small[:, 4, :], small[:, 3, :], 1.0, None, ALU.add))
                    dve.reciprocal(small[:, 5, :], small[:, 4, :])
                    for t in range(NT):
                        last = dve.max(top[:, t, :], lgs[:, t, :])
                    own(last)
                    for t in range(NT):
                        last = dve.max_index(best[:, t, :], top[:, t, :], lgs[:, t, :])
                    own(last)
                    own(dve.tensor_copy(bestf[:, :].rearrange("p (t k) -> p t k", t=NT), best[:, :, 0:K]))
                    own(dve.tensor_tensor(onehot[:, :, :], iota[:, 0:E].unsqueeze(1).broadcast_to([P, NT * K, E]),
                                          bestf[:, :].unsqueeze(2).broadcast_to([P, NT * K, E]), ALU.is_equal))
                    dve.tensor_reduce(chosen[:, :, :], onehot[:, :, :].rearrange("p (t k) e -> p t e k", t=NT),
                                      AX, ALU.add).then_inc(chosen_ready, 1)
                    dve.wait_ge(counted, 1)
                    for t in range(NT):
                        own(dve.tensor_tensor(base[:, t + 1, :], bank[2][:, t * E:(t + 1) * E], base[:, t, :], ALU.add))
                    own(dve.tensor_tensor(pos[:, :, :], bank[1][:, 0:NT * E].rearrange("p (t e) -> p t e", t=NT),
                                          base[:, 0:NT, :], ALU.add))
                    own(dve.tensor_tensor(over[:, :, :], base[:, NT, :].unsqueeze(2).broadcast_to([P, E, 8]),
                                          full.unsqueeze(1).broadcast_to([P, E, 8]), ALU.is_gt))
                    own(dve.tensor_reduce(tiles[:, :], over[:, :, :], AX, ALU.add))
                    own(dve.tensor_tensor_scan(cum[:, :], ones[:, 0:E], tiles[:, :], 0.0, ALU.mult, ALU.add))
                    own(dve.tensor_tensor(begin[:, :], cum[:, :], tiles[:, :], ALU.subtract))
                    own(dve.tensor_scalar(junk[:, :], cum[:, :], index, 0.0, ALU.is_le, ALU.add,
                                          accum_out=slot_expert[:, 0:1]))
                    dve.tensor_scalar(slot_expert[:, 1:2], slot_expert[:, 0:1], float(E - 1), None,
                                      ALU.min).then_inc(expert_ready, 1)
                    own(dve.scalar_tensor_tensor(pos[:, :, :], begin[:, :].unsqueeze(1).broadcast_to([P, NT, E]),
                                                 float(P), pos[:, :, :], ALU.mult, ALU.add))
                    own(dve.tensor_tensor(work[:, :, :].rearrange("p (t k) e -> p t k e", t=NT),
                                          onehot[:, :, :].rearrange("p (t k) e -> p t k e", t=NT),
                                          pos[:, :, :].unsqueeze(2).broadcast_to([P, NT, K, E]), ALU.mult))
                    own(dve.tensor_reduce(placef[:, :], work[:, :, :], AX, ALU.add))
                    own(dve.tensor_copy(place[:, :], placef[:, :]))
                    dve.tensor_scalar(part[:, 0, :], place[:, :], P - 1, None, ALU.bitwise_and)
                    own(dve.tensor_scalar(part[:, 1, :], place[:, :], 7, None, ALU.logical_shift_right))
                    own(dve.tensor_copy(partf[:, :, :], part[:, :, :]))
                    for t in range(NT):
                        at = slice(t * K, (t + 1) * K)
                        if t >= 2:
                            dve.wait_ge(listed, t - 1)
                        dve.tensor_tensor(in_row[:, t % 2, :, :], iota.unsqueeze(1).broadcast_to([P, K, P]),
                                          partf[:, 0, at].unsqueeze(2).broadcast_to([P, K, P]), ALU.is_equal)
                        own(dve.tensor_tensor(in_slot[:, t % 2, 0], iota[:, 0:SLOTS].unsqueeze(1).broadcast_to([P, K, SLOTS]),
                                              partf[:, 1, at].unsqueeze(2).broadcast_to([P, K, SLOTS]), ALU.is_equal))
                        dve.tensor_scalar(in_slot[:, t % 2, 1], in_slot[:, t % 2, 0], tokens[:, t:t + 1], None, ALU.mult)
                        dve.tensor_tensor(in_slot[:, t % 2, 2], in_slot[:, t % 2, 0],
                                          top[:, t, 0:K].unsqueeze(2).broadcast_to([P, K, SLOTS]),
                                          ALU.mult).then_inc(in_ready, 1)
                    dve.wait_ge(expert_turned, 1)
                    dve.tensor_copy(row[:, :], bank[0][0:1, 0:P])
                    for t in range(NT):
                        dve.wait_ge(shared, t // 2 + 1)
                        dve.scalar_tensor_tensor(g["x"][:, t, :], bank[4 + t // 2][:, (t % 2) * D:(t % 2 + 1) * D],
                                                 small[:, 5, t:t + 1], g["x"][:, t, :], ALU.mult, ALU.add)
                    dve.wait_ge(listed, NT)
                    dve.tensor_copy(ids[:, :], bank[3][:, 0:SLOTS])
                    dve.tensor_copy(wts[:, :], bank[3][:, SLOTS:2 * SLOTS])

        with ExitStack() as inner:
            def sb(name, shape, dt=F32):
                return inner.enter_context(nc.sbuf_tensor(name + tag, shape, dt))

            DEPTH = SLOT_DEPTH
            assert TURNS * DEPTH == SLOTS
            w13 = sb("w13", [P, DEPTH, DC, 2 * INTER])
            w2 = sb("w2", [IC, DEPTH, 2, D])
            who = sb("who", [P, DEPTH], U32)
            xg = sb("xg", [P, DEPTH, D])
            xgT = sb("xgT", [P, 2, DC, P])
            act_g = sb("act_g", [P, 2, INTER])
            h = sb("h", [P, 2, 2 * IC])
            hT = sb("hTs", [IC, 2, 2, P])
            y = sb("y", [P, DEPTH, D])
            w_loaded = g["w_loaded"]
            x_gathered = g["x_gathered"]
            y_stored = g["y_stored"]
            who_ready = sem("who_ready")
            who_seen = sem("who_seen")
            cleared = sem("cleared")
            x_turned = sem("x_turned")
            xgT_done = sem("xgT_done")
            gu_done = sem("gu_done")
            silu_done = sem("silu_done")
            h_done = sem("h_done_s")
            h_turned = sem("h_turned")
            hT_done = sem("hT_done")
            down_done = sem("down_done")
            y_done = sem("y_done")
            TX, TH, G, Y = bank[0:2], bank[2:4], bank[4:6], bank[6:8]

            with nc.Block() as block:
                @block.sync
                def _(sp):
                    def load(j, s):
                        e = sp.value_load(row[0:1, bass.ds(s, 1)], min_val=0, max_val=EXPERTS - 1)
                        sp.dma_start(w13[:, j, :, :], a["w13"][bass.ds(e, 1)].rearrange("a p c n -> p (a c) n")).then_inc(w_loaded[j], 16)
                        sp.dma_start(w2[:, j, :, :], a["w2"][bass.ds(e, 1)].rearrange("a p c n -> p (a c) n")).then_inc(w_loaded[j], 16)

                    def store(turn, j):
                        s = turn * DEPTH + j
                        sp.wait_ge(y_done, s + 1)
                        sp.dma_start(g["y_dram"][bass.ds(s * P, P), :], y[:, j, :]).then_inc(y_stored[j], 16)

                    for j in range(DEPTH):
                        load(j, j)
                    with sp.Fori(0, TURNS - 1) as turn:
                        for j in range(DEPTH):
                            sp.wait_ge(down_done, turn * DEPTH + j + 1)
                            load(j, turn * DEPTH + DEPTH + j)
                            store(turn, j)
                    for j in range(DEPTH):
                        store(TURNS - 1, j)
                    for j in range(DEPTH):
                        sp.wait_ge(y_stored[j], 16 * TURNS * (run + 1))

                @block.gpsimd
                def _(pool):
                    pool.memset(h[:, :, :], 0.0).then_inc(cleared, 1)

                    def gather(s, j):
                        pool.tensor_copy(who[:, j:j + 1], ids[:, bass.ds(s, 1)]).then_inc(who_ready, 1)
                        pool.wait_ge(who_ready, s + 1)
                        pool.sem_inc(who_seen, 1)
                        pool.indirect_dma_start(xg[:, j, :], None, g["xn_dram"],
                                                bass.IndirectOffsetOnAxis(ap=who[:, j:j + 1], axis=0),
                                                ).then_inc(x_gathered[j], 16)

                    for j in range(DEPTH):
                        gather(j, j)
                    with pool.Fori(0, TURNS - 1) as turn:
                        for j in range(DEPTH):
                            pool.wait_ge(x_turned, turn * DEPTH + j + 1)
                            gather(turn * DEPTH + DEPTH + j, j)

                @block.tensor
                def _(pe):
                    def turn_x(turn, j):
                        s = turn * DEPTH + j
                        pe.wait_ge(x_gathered[j], 16 * (turn + 1 + run * TURNS))
                        if not (isinstance(turn, int) and s < 2):
                            pe.wait_ge(xgT_done, s - 1)
                        for c in range(DC):
                            last = pe.transpose(TX[j % 2][:, c * P:(c + 1) * P], xg[:, j, c * P:(c + 1) * P],
                                                g["ident"][:, :])
                        last.then_inc(x_turned, 1)

                    def gate_up(turn, j):
                        s = turn * DEPTH + j
                        pe.wait_ge(w_loaded[j], 32 * (turn + 1 + run * TURNS))
                        pe.wait_ge(xgT_done, s + 1)
                        if not (isinstance(turn, int) and s < 2):
                            pe.wait_ge(h_done, s - 1)
                        for c in range(DC):
                            last = pe.matmul(G[j % 2][:, 0:2 * INTER], xgT[:, j % 2, c, :], w13[:, j, c, :],
                                             start=(c == 0), stop=(c == DC - 1))
                        last.then_inc(gu_done, 1)

                    def turn_h(turn, j):
                        s = turn * DEPTH + j
                        pe.wait_ge(h_done, s + 1)
                        if not (isinstance(turn, int) and s < 2):
                            pe.wait_ge(hT_done, s - 1)
                        for c in range(2):
                            last = pe.transpose(TH[j % 2][0:IC, c * P:(c + 1) * P], h[:, j % 2, c * IC:(c + 1) * IC],
                                                g["ident"][:, :])
                        last.then_inc(h_turned, 1)

                    def down(turn, j):
                        s = turn * DEPTH + j
                        pe.wait_ge(hT_done, s + 1)
                        if not (isinstance(turn, int) and s < 2):
                            pe.wait_ge(y_done, s - 1)
                        for c in range(2):
                            last = pe.matmul(Y[j % 2][:, 0:D], hT[:, j % 2, c, :], w2[:, j, c, :],
                                             start=(c == 0), stop=(c == 1))
                        last.then_inc(down_done, 1)

                    def slots(turn, first=False, final=False):
                        for j in range(DEPTH):
                            before = (turn, j - 1) if j > 0 else (turn - 1, DEPTH - 1)
                            if j > 0 or not first:
                                turn_h(*before)
                            if j < DEPTH - 1:
                                turn_x(turn, j + 1)
                            elif not final:
                                turn_x(turn + 1, 0)
                            gate_up(turn, j)
                            if j > 0 or not first:
                                down(*before)

                    turn_x(0, 0)
                    slots(0, first=True)
                    with pe.Fori(1, TURNS - 1) as turn:
                        slots(turn)
                    slots(TURNS - 1, final=True)
                    turn_h(TURNS - 1, DEPTH - 1)
                    down(TURNS - 1, DEPTH - 1)

                @block.scalar
                def _(act):
                    def silu(turn, j):
                        act.wait_ge(gu_done, turn * DEPTH + j + 1)
                        act.activation(act_g[:, j % 2, :], G[j % 2][:, 0:INTER], ACT.Silu).then_inc(silu_done, 1)

                    def weigh(turn, j):
                        s = turn * DEPTH + j
                        act.wait_ge(down_done, s + 1)
                        if not (isinstance(turn, int) and turn + run == 0):
                            act.wait_ge(y_stored[j], 16 * (turn + run * TURNS))
                        act.activation(y[:, j, :], Y[j % 2][:, 0:D], ACT.Copy,
                                       scale=wts[:, bass.ds(s, 1)]).then_inc(y_done, 1)

                    def slots(turn, first=False):
                        for j in range(DEPTH):
                            silu(turn, j)
                            if j > 0:
                                weigh(turn, j - 1)
                            elif not first:
                                weigh(turn - 1, DEPTH - 1)

                    slots(0, first=True)
                    with act.Fori(1, TURNS) as turn:
                        slots(turn)
                    weigh(TURNS - 1, DEPTH - 1)

                @block.vector
                def _(dve):
                    dve.wait_ge(cleared, 1)

                    def copy_x(turn, j):
                        dve.wait_ge(x_turned, turn * DEPTH + j + 1)
                        dve.tensor_copy(xgT[:, j % 2, :, :],
                                        TX[j % 2][:, 0:D].rearrange("p (c n) -> p c n", c=DC)).then_inc(xgT_done, 1)

                    def gate(turn, j):
                        s = turn * DEPTH + j
                        dve.wait_ge(silu_done, s + 1)
                        dve.tensor_tensor(h[:, j % 2, 0:INTER], G[j % 2][:, INTER:2 * INTER], act_g[:, j % 2, :],
                                          ALU.mult).then_inc(h_done, 1)

                    def copy_h(turn, j):
                        dve.wait_ge(h_turned, turn * DEPTH + j + 1)
                        dve.tensor_copy(hT[:, j % 2, :, :],
                                        TH[j % 2][0:IC, 0:D].rearrange("p (c n) -> p c n", c=2)).then_inc(hT_done, 1)

                    def slots(turn, first=False, final=False):
                        for j in range(DEPTH):
                            if j > 0:
                                copy_h(turn, j - 1)
                            elif not first:
                                copy_h(turn - 1, DEPTH - 1)
                            if j < DEPTH - 1:
                                copy_x(turn, j + 1)
                            elif not final:
                                copy_x(turn + 1, 0)
                            gate(turn, j)

                    copy_x(0, 0)
                    slots(0, first=True)
                    with dve.Fori(1, TURNS - 1) as turn:
                        slots(turn)
                    slots(TURNS - 1, final=True)
                    copy_h(TURNS - 1, DEPTH - 1)

        with ExitStack() as inner:
            DEPTH = GATHER_DEPTH
            yg = inner.enter_context(nc.sbuf_tensor("yg" + tag, [P, DEPTH, D], F32))
            gathered = g["y_gathered"]
            summed = sem("y_summed")
            with nc.Block() as block:
                @block.gpsimd
                def _(pool):
                    for n in range(NT * K):
                        if n >= DEPTH:
                            pool.wait_ge(summed, n - DEPTH + 1)
                        pool.indirect_dma_start(yg[:, n % DEPTH, :], None, g["y_dram"],
                                                bass.IndirectOffsetOnAxis(ap=place[:, n:n + 1].bitcast(U32), axis=0),
                                                ).then_inc(gathered[n % DEPTH], 16)

                @block.vector
                def _(dve):
                    for n in range(NT * K):
                        dve.wait_ge(gathered[n % DEPTH], 16 * (n // DEPTH + 1 + run * NT * K // DEPTH))
                        if n % K:
                            dve.wait_ge(summed, n)
                        dve.tensor_tensor(g["x"][:, n // K, :], g["x"][:, n // K, :], yg[:, n % DEPTH, :],
                                          ALU.add).then_inc(summed, 1)


def _rope(dim, scale):
    inv = (1.0 / 10000.0 ** (np.arange(0, dim, 2, dtype=np.float32) / np.float32(dim))).astype(np.float32)
    f = np.outer(np.arange(SEQ, dtype=np.float32), inv).astype(np.float32)
    f = np.concatenate([f, f], axis=1)
    sign = np.where(np.arange(dim) < dim // 2, -1.0, 1.0)
    both = np.stack([np.cos(f), np.sin(f) * sign], axis=1) * scale
    return np.ascontiguousarray(both.reshape(2, P, 2, dim).transpose(1, 0, 2, 3).astype(np.float32))


def _chunks(w):
    return np.ascontiguousarray(w.reshape(-1, P, w.shape[-1]).transpose(1, 0, 2))


def kernel(**inputs):
    import ml_dtypes
    import concourse.bacc as bacc
    from concourse.bass_utils import run_bass_kernel_spmd

    x = {k.replace("L0_", ""): np.asarray(v) for k, v in inputs.items()}
    wq = x["attn_a_wq"].reshape(D, HEADS, NOPE + ROPE)
    wkv = x["attn_a_wkv_b"].reshape(KVR, HEADS, NOPE + VD)
    se_up = np.zeros((D, 2, SHARED_CHUNKS * P), np.float32)
    se_up[:, :, 0:704] = x["ffn_se_gate_up_w"].T.reshape(D, 2, 704)
    se_down = np.zeros((SHARED_CHUNKS * P, D), np.float32)
    se_down[0:704] = x["ffn_se_down_w"].T
    w2 = np.zeros((EXPERTS, 2 * IC, D), np.float32)
    w2[:, 0:INTER] = x["ffn_w2"].transpose(0, 2, 1)
    p = np.arange(P)
    count = np.concatenate([
        np.broadcast_to(p, (P, P)), p[:, None] < p[None, :], np.ones((P, P)),
        np.broadcast_to(np.arange(8) * P, (P, 8)), np.arange(8) * P + p[:, None], p[:, None],
    ], axis=1).astype(np.float32)
    mask = np.stack([np.eye(P), np.where(p[None, :] > p[:, None], -3e38, 0.0)], axis=1).astype(ml_dtypes.bfloat16)
    arrays = {
        "x": x["attn_a_x"].reshape(TOK, D),
        "ident": np.eye(P, dtype=np.float32),
        "mask": mask,
        "wq_nopeT": wq[:, :, 0:NOPE].transpose(2, 1, 0),
        "wq_rope": _chunks(wq[:, :, NOPE:].reshape(D, HEADS * ROPE)),
        "wkT": wkv[:, :, 0:NOPE].transpose(2, 1, 0),
        "wvT": wkv[:, :, NOPE:].transpose(2, 1, 0),
        "wo_a": x["attn_a_wo"].reshape(HEADS, VD, D).transpose(1, 0, 2),
        "wkv_a": _chunks(x["attn_a_wkv_a"]),
        "kv_w": np.broadcast_to(x["attn_a_kv_norm_w"], (P, KVR)),
        "rope_k": _rope(ROPE, 1.0),
        "rope_q": _rope(ROPE, float(NOPE + ROPE) ** -0.5),
        "gate": _chunks(np.concatenate([x["ffn_gate_w"], x["ffn_shared_gate_w"]]).T),
        "se_up": _chunks(se_up.reshape(D, -1)),
        "se_down": _chunks(se_down),
        "count": count,
        "w_rot": _chunks(np.concatenate([x["attn_b_Wq"], x["attn_b_Wk"], x["attn_b_Wv"]]).T),
        "rope_b": np.stack([_rope(HD, float(HD) ** -0.5), _rope(HD, 1.0)], axis=2),
        "wo_b": _chunks(x["attn_b_Wo"].T),
        "w13": x["ffn_w13"].transpose(0, 2, 1).reshape(EXPERTS, DC, P, 2 * INTER).transpose(0, 2, 1, 3),
        "w2": w2.reshape(EXPERTS, 2, IC, D).transpose(0, 2, 1, 3),
    }
    arrays = {k: np.ascontiguousarray(v) for k, v in arrays.items()}
    nc = bacc.Bacc("TRN2", target_bir_lowering=False, num_devices=1)
    aps = {k: nc.dram_tensor(k + "_dram", v.shape, mybir.dt.from_np(v.dtype), kind="ExternalInput").ap()
           for k, v in arrays.items()}
    out = nc.dram_tensor("out_dram", (TOK, D), F32, kind="ExternalOutput").ap()
    build(nc, aps, out)
    r = run_bass_kernel_spmd(nc, [{k + "_dram": v for k, v in arrays.items()}], core_ids=[0])
    return r.results[0]["out_dram"].reshape(BATCH, SEQ, D)
```

```python
from contextlib import ExitStack

import numpy as np

import concourse.bass as bass
from concourse import mybir

F32 = mybir.dt.float32
BF16 = mybir.dt.bfloat16
I32 = mybir.dt.int32
U32 = mybir.dt.uint32
ALU = mybir.AluOpType
ACT = mybir.ActivationFunctionType
AX = mybir.AxisListType.X

P = 128
BATCH, SEQ, D = 4, 256, 256
TOK = BATCH * SEQ
NT = TOK // P
DC = D // P
HEADS = 16
PAIRS = HEADS // 2
NOPE, ROPE, VD, KVR = 128, 64, 128, 64
HD = D // HEADS
EXPERTS, TOP, INTER = 60, 4, 176
IC = 96
SHARED_CHUNKS = 6
SLOTS = TOP * TOK // P + EXPERTS
SLOT_DEPTH = 4
GATHER_DEPTH = 8
TURNS = SLOTS // SLOT_DEPTH
LN_EPS, RMS_EPS = 1e-5, 1e-6


def build(nc, a, out):
    with ExitStack() as ctx:
        def sb(name, shape, dt=F32):
            return ctx.enter_context(nc.sbuf_tensor(name, shape, dt))

        def sem(name):
            return ctx.enter_context(nc.semaphore(name))

        g = {"sem": sem}
        g["x"] = sb("x", [P, NT, D])
        g["xn"] = sb("xn", [P, NT, D])
        g["xnT"] = sb("xnT", [P, DC, TOK])
        g["ident"] = sb("ident", [P, P])
        g["mask"] = sb("mask", [P, 2, P], BF16)
        g["halves"] = sb("halves", [P, NT])
        g["loaded_x"] = sem("loaded_x")
        names = {}
        for name in LOADS:
            shape = list(a[name].shape)
            g[name] = sb("w_" + name, shape)
            names[name] = sem("loaded_" + name)
        g["loaded"] = names
        g["norm_sems"] = {name: sem(name) for name in Norm.TOTALS}
        for name, n in (("w_loaded", SLOT_DEPTH), ("x_gathered", SLOT_DEPTH), ("y_stored", SLOT_DEPTH), ("y_gathered", GATHER_DEPTH)):
            g[name] = [sem(f"{name}{j}") for j in range(n)]
        g["xn_dram"] = nc.dram_tensor("xn_rows", (TOK, D), F32, kind="Internal").ap()
        g["y_dram"] = nc.dram_tensor("y_rows", (SLOTS * P, D), F32, kind="Internal").ap()

        with nc.Block() as block:
            @block.sync
            def _(sp):
                sp.dma_start(g["x"][:, :, :], a["x"].rearrange("(n p) d -> p n d", p=P)).then_inc(g["loaded_x"], 16)
                sp.dma_start(g["ident"][:, :], a["ident"]).then_inc(g["loaded_x"], 16)
                sp.dma_start(g["mask"][:, :, :], a["mask"]).then_inc(g["loaded_x"], 16)
                sp.wait_ge(g["loaded_x"], 48)
                for name in LOADS:
                    whole = (slice(None),) * len(a[name].shape)
                    sp.dma_start(g[name][whole], a[name][whole]).then_inc(names[name], 16)

            @block.gpsimd
            def _(pool):
                pool.memset(g["halves"][:, :], -0.5)

        for n, phase in enumerate(PHASES):
            if phase in ("latent", "rotary"):
                attention(nc, g, a, str(n), n, phase == "latent")
            else:
                experts(nc, g, a, str(n), n, PHASES[:n].count("experts"))

        stored = sem("stored")
        with nc.Block() as block:
            @block.sync
            def _(sp):
                sp.dma_start(out.rearrange("(n p) d -> p n d", p=P), g["x"][:, :, :]).then_inc(stored, 16)
                sp.wait_ge(stored, 16)


PHASES = ["latent", "experts", "rotary", "experts"]
LOADS = ["wq_nopeT", "wkT", "wkv_a", "kv_w", "rope_k", "rope_q", "wq_rope", "wvT", "wo_a", "gate", "se_up", "se_down",
         "count", "w_rot", "rope_b", "wo_b"]


class Norm:

    TOTALS = {"ln_stats_done": NT, "ln_mv_done": NT, "ln_var_done": 1, "ln_rstd_done": 1, "ln_xn_done": NT,
              "ln_turned": NT // 2}

    def __init__(self, ctx, nc, g, tag, before):
        sb = lambda name, shape: ctx.enter_context(nc.sbuf_tensor(name + tag, shape, F32))
        self.stats = sb("ln_stats", [P, NT, 6])
        self.mv = sb("ln_mv", [P, NT, 2])
        self.var = sb("ln_var", [P, NT])
        self.rstd = sb("ln_rstd", [P, NT])
        self.sems = g["norm_sems"]
        self.before = before

    def sem(self, name):
        return self.sems["ln_" + name]

    def count(self, name, n):
        return self.before * self.TOTALS["ln_" + name] + n

    def vector(self, dve, g):
        dve.wait_ge(g["loaded_x"], 48)
        for t in range(NT):
            dve.bn_stats(self.stats[:, t, :], g["x"][:, t, :]).then_inc(self.sem("stats_done"), 1)
        for t in range(NT):
            dve.wait_ge(self.sem("stats_done"), self.count("stats_done", t + 1))
            dve.bn_aggr(self.mv[:, t, :], self.stats[:, t, :]).then_inc(self.sem("mv_done"), 1)
        dve.wait_ge(self.sem("mv_done"), self.count("mv_done", NT))
        dve.tensor_scalar(self.var[:, :], self.mv[:, :, 1], LN_EPS, None, ALU.add).then_inc(self.sem("var_done"), 1)
        dve.wait_ge(self.sem("rstd_done"), self.count("rstd_done", 1))
        for t in range(NT):
            dve.tensor_scalar(g["xn"][:, t, :], g["x"][:, t, :], self.mv[:, t, 0:1], self.rstd[:, t:t + 1],
                              ALU.subtract, ALU.mult).then_inc(self.sem("xn_done"), 1)

    def gpsimd(self, pool, g):
        pool.wait_ge(self.sem("var_done"), self.count("var_done", 1))
        pool.tensor_tensor(self.rstd[:, :], self.var[:, :], g["halves"][:, :], ALU.pow).then_inc(self.sem("rstd_done"), 1)

    def tensor(self, pe, g, banks):
        for m in range(NT // 2):
            pe.wait_ge(self.sem("xn_done"), self.count("xn_done", 2 * m + 2))
            for c in range(DC):
                for t in (2 * m, 2 * m + 1):
                    last = pe.transpose(banks[m][:, c * 256 + (t % 2) * P:c * 256 + (t % 2 + 1) * P],
                                        g["xn"][:, t, c * P:(c + 1) * P], g["ident"][:, :])
            last.then_inc(self.sem("turned"), 1)

    def scalar(self, act, g, banks, done):
        for m in range(NT // 2):
            act.wait_ge(self.sem("turned"), self.count("turned", m + 1))
            act.activation(g["xnT"][:, :, m * 256:(m + 1) * 256],
                           banks[m][:, :].rearrange("p (c n) -> p c n", c=DC), ACT.Copy).then_inc(done, 1)


def attention(nc, g, a, tag, before, latent):
    VW = KVR if latent else 2 * HD
    SCALE = float(NOPE + ROPE) ** -0.5 if latent else float(HD) ** -0.5
    OC = HEADS * VW // P
    loaded = g["loaded"]

    if latent:
        FRONT = [("Q", 0), ("Q", 1), ("Q", 2), ("T", 0), ("Q", 3), ("T", 1), ("T", 2), ("T", 3)]
    else:
        FRONT = [("Q", 0), ("Q", 1), ("T", 0), ("T", 1), ("T", 2), ("T", 3), ("T", 4), None]
    KEYS = ("T", 4)

    T_ORDER, Q_ORDER = [], []
    for p in range(PAIRS):
        T_ORDER.append(("P", p))
        if FRONT[p]:
            (T_ORDER if FRONT[p][0] == "T" else Q_ORDER).append(FRONT[p])
    Q_ORDER.append("out")
    T_FRONT = [f for f in FRONT if f and f[0] == "T"]
    Q_FRONT = [f for f in FRONT if f and f[0] == "Q"]

    class Use:

        def __init__(self, kind, b, i, key, nxt):
            order, front = (T_ORDER, T_FRONT) if kind == "T" else (Q_ORDER, Q_FRONT)
            if not nxt:
                order = [k for k in order if k not in front]
            if b is None:
                v, b = front.index(key), 0
            else:
                v = len(front) + len(T_ORDER if kind == "T" else Q_ORDER) * i + order.index(key)
            per_bank = len(T_ORDER if kind == "T" else Q_ORDER)
            self.bank = v % 2
            self.before = b * per_bank + v // 2
            self.first = v < 2
            self.written = b * 2 * per_bank + v + 1

    with ExitStack() as ctx:
        def sb(name, shape, dt=F32):
            return ctx.enter_context(nc.sbuf_tensor(name + tag, shape, dt))

        def sem(name):
            return g["sem"](name + tag)

        def psum(name, shape):
            return ctx.enter_context(nc.psum_tensor(name + tag, shape, F32))

        norm = Norm(ctx, nc, g, tag, before)
        T = [psum(f"T{i}", [P, 512]) for i in range(2)]
        Q = [psum(f"Q{i}", [P, 512]) for i in range(2)]
        S = [psum(f"S{i}", [P, 512]) for i in range(2)]
        O = [psum(f"O{i}", [P, 512]) for i in range(2)]

        xs = sb("xs", [P, 2, DC, P])
        q = sb("q", [P, 2, HEADS, P])
        qT = sb("qT", [P, 2, HEADS, P])
        rot1 = sb("rot1", [P, 2, 8 * ROPE])
        rot2 = sb("rot2", [P, 2, 8 * ROPE])
        nmax = sb("nmax", [P, 2, HEADS])
        rsum = sb("rsum", [P, 2, HEADS])
        rinv = sb("rinv", [P, 2, HEADS])
        prob = sb("prob", [P, 2, 2, 2 * P])
        probT = sb("probT", [P, 2, 2, 2, 4, P])
        oT = sb("oT", [P, 2, OC, P])
        if latent:
            wqn = sb("wqn", [P, DC, HEADS * KVR])
            wvo = sb("wvo", [P, PAIRS, D])
            kvc = sb("kvc", [P, NT, P])
            sq = rot1[:, 1, :].rearrange("p (t n) -> p t n", t=NT)
            ms = sb("ms", [P, NT])
            ms2 = sb("ms2", [P, NT])
            rr = sb("rr", [P, NT])
            kv = sb("kv", [P, NT, P])
            kT = sb("kT", [P, TOK])
            vals = sb("vals", [P, 2, KVR])
        else:
            kr = sb("kr", [P, D])
            kT = sb("kT", [P, 2, SEQ])
            v = sb("v", [P, 2, D])
            vals = sb("vals", [P, 2, HEADS, VW])

        xnT_done = sem("xnT_done")
        staged = sem("staged")
        projected = sem("projected")
        q_read = [sem(f"q_read{i}") for i in range(2)]
        turned = sem("turned")
        t_read = [sem(f"t_read{i}") for i in range(2)]
        q_ready = sem("q_ready")
        kr_ready = sem("kr_ready")
        vals_ready = sem("vals_ready")
        vals_free = sem("vals_free")
        scored = sem("scored")
        max_done = sem("max_done")
        exp_done = sem("exp_done")
        recip = sem("recip")
        normed = sem("normed")
        summed = sem("summed")
        o_done = sem("o_done")
        pre_pe = sem("pre_pe")
        pre_act = sem("pre_act")
        pre_dve = sem("pre_dve")
        pre_pool = sem("pre_pool")
        WQN_USES = DC * HEADS * KVR // 512
        WVO_USES = PAIRS * D // 512
        START = 2

        def pair(b, i, p):
            return b * 2 * PAIRS + PAIRS * i + p + 1

        def half(b, i, m):
            return b * 4 + 2 * i + m + 1 + START

        def k_slice(b, i, gr):
            if latent:
                return kT[:, bass.ds(b * SEQ, (i + 1) * P)]
            return kT[:, gr, 0:(i + 1) * P]

        def run(eng, slot):
            with eng.Fori(0, BATCH - 1) as b:
                slot(b, 0, True)
                slot(b, 1, True)
            slot(BATCH - 1, 0, True)
            slot(BATCH - 1, 1, False)

        def after(b, i):
            return (b, 1) if i == 0 else (b + 1, 0)

        with nc.Block() as block:
            @block.tensor
            def _(pe):
                pe.sem_inc(summed, START)
                if latent:
                    pe.wait_ge(g["loaded_x"], 48)
                    pe.wait_ge(loaded["wq_nopeT"], 16)
                    pe.wait_ge(loaded["wkT"], 16)
                    n = 0
                    for c in range(DC):
                        for side in range(2):
                            if n >= 2:
                                pe.wait_ge(pre_act, n - 1)
                            for k in range(8):
                                h = 8 * side + k
                                last = pe.matmul(Q[n % 2][:, k * KVR:(k + 1) * KVR],
                                                 g["wq_nopeT"][:, h, c * P:(c + 1) * P],
                                                 g["wkT"][:, h, :], start=True, stop=True)
                            last.then_inc(pre_pe, 1)
                            n += 1
                norm.tensor(pe, g, [T[0], T[1], S[0], S[1]])
                if latent:
                    pe.wait_ge(loaded["wkv_a"], 16)
                    for m in range(2):
                        pe.wait_ge(xnT_done, 2 * m + 2)
                        for t in range(4):
                            for c in range(DC):
                                last = pe.matmul(O[m][:, t * P:(t + 1) * P],
                                                 g["xnT"][:, c, (4 * m + t) * P:(4 * m + t + 1) * P],
                                                 g["wkv_a"][:, c, :], start=(c == 0), stop=(c == DC - 1))
                        last.then_inc(pre_pe, 1)
                    n += 2
                    pe.wait_ge(loaded["wvT"], 16)
                    pe.wait_ge(loaded["wo_a"], 16)
                    for m in range(WVO_USES):
                        if m < 2:
                            pe.wait_ge(pre_act, WQN_USES - 1 + m)
                        else:
                            pe.wait_ge(pre_act, n - 1)
                        for j in range(2):
                            for side in range(2):
                                h = 4 * m + 2 * j + side
                                last = pe.matmul(Q[n % 2][side * KVR:(side + 1) * KVR, j * D:(j + 1) * D],
                                                 g["wvT"][:, h, :], g["wo_a"][:, h, :], start=True, stop=True)
                        last.then_inc(pre_pe, 1)
                        n += 1
                    pe.wait_ge(pre_dve, 7)
                    for m in range(2):
                        for t in range(4):
                            last = pe.transpose(T[m][:, t * P:(t + 1) * P], kv[:, 4 * m + t, :], g["ident"][:, :])
                        last.then_inc(pre_pe, 1)
                    pe.wait_ge(pre_act, WQN_USES + 2 + WVO_USES + 2)
                    pe.wait_ge(loaded["wq_rope"], 16)
                else:
                    pe.wait_ge(xnT_done, NT // 2)
                    pe.wait_ge(loaded["w_rot"], 16)
                    pe.wait_ge(loaded["wo_b"], 16)

                def project(b, i, n, nxt):
                    if latent:
                        w, cols, width = (wqn, g["wq_rope"])[n % 2], 512 * (n // 2), 512
                    else:
                        w, cols, width = g["w_rot"], 512 * n, (512, 256)[n]
                    use = Use("Q", b, i, ("Q", n), nxt)
                    tile = 0 if b is None else 2 * b + i + 1
                    side = 0 if b is None else (i + 1) % 2
                    pe.wait_ge(staged, tile + 1)
                    if not use.first:
                        pe.wait_ge(q_read[use.bank], use.before)
                    for c in range(DC):
                        last = pe.matmul(Q[use.bank][:, 0:width], xs[:, side, c, :], w[:, c, cols:cols + width],
                                         start=(c == 0), stop=(c == DC - 1))
                    last.then_inc(projected, 1)

                def turn_front(b, i, n, nxt):
                    use = Use("T", b, i, ("T", n), nxt)
                    tile = 0 if b is None else 2 * b + i + 1
                    side = 0 if b is None else (i + 1) % 2
                    if not use.first:
                        pe.wait_ge(t_read[use.bank], use.before)
                    if ("T", n) == KEYS:
                        pe.wait_ge(kr_ready, tile + 1)
                        for k in range(2):
                            last = pe.transpose(T[use.bank][:, k * P:(k + 1) * P], kr[:, k * P:(k + 1) * P],
                                                g["ident"][:, :])
                    else:
                        if latent:
                            at = Use("Q", b, i, ("Q", 2 * (n // 2)), nxt)
                            pe.wait_ge(q_read[at.bank], at.before + 1)
                        pe.wait_ge(q_ready, tile * 2 + n // 2 + 1)
                        for k in range(4):
                            last = pe.transpose(T[use.bank][:, k * P:(k + 1) * P], q[:, side, 4 * n + k, :],
                                                g["ident"][:, :])
                    last.then_inc(turned, 1)

                def scores(b, i, p):
                    if not (isinstance(b, int) and b == i == 0 and p < 2):
                        pe.wait_ge(exp_done, pair(b, i, p) - 2)
                    w = (i + 1) * P
                    for j in range(2):
                        h = 2 * p + j
                        to = S[p % 2][:, j * 256:j * 256 + w]
                        pe.matmul(to, qT[:, i, h, :], k_slice(b, i, h // 8), start=True, stop=True)
                        last = pe.matmul(S[p % 2][:, j * 256 + i * P:j * 256 + w], g["mask"][:, 0, :],
                                         g["mask"][:, 1, :], start=False, stop=True, skip_group_check=True)
                    last.then_inc(scored, 1)

                def first_scores(b, i, nxt, at):
                    for key in (("T", 0), KEYS):
                        if key in T_FRONT:
                            use = Use("T", b, i, key, nxt)
                            pe.wait_ge(t_read[use.bank], use.before + 1)
                    scores(*at, 0)
                    scores(*at, 1)

                def turn_probs(b, i, p, nxt):
                    use = Use("T", b, i, ("P", p), nxt)
                    pe.wait_ge(normed, pair(b, i, p))
                    pe.wait_ge(t_read[use.bank], use.before)
                    for j in range(2):
                        for kb in range(i + 1):
                            at = (j * (i + 1) + kb) * P
                            last = pe.transpose(T[use.bank][:, at:at + P], prob[:, p % 2, j, kb * P:(kb + 1) * P],
                                                g["ident"][:, :])
                    last.then_inc(turned, 1)

                def values(b, i, m, nxt):
                    use = Use("T", b, i, ("P", 4 * m + 3), nxt)
                    pe.wait_ge(t_read[use.bank], use.before + 1)
                    pe.wait_ge(vals_ready, 2 * b + i + 1)
                    pe.wait_ge(o_done, half(b, i, m) - 2)
                    if latent:
                        for j in range(2):
                            for kb in range(i + 1):
                                last = pe.matmul(O[m][j * VW:(j + 1) * VW, :], vals[:, kb, :],
                                                 probT[:, m, j, kb, :, :], start=(kb == 0), stop=(kb == i))
                    else:
                        for s in range(4):
                            for j in range(2):
                                h = 8 * m + 2 * s + j
                                for kb in range(i + 1):
                                    last = pe.matmul(O[m][(h % 4) * VW:(h % 4 + 1) * VW, (s // 2) * P:(s // 2 + 1) * P],
                                                     vals[:, kb, h, :], probT[:, m, j, kb, s, :],
                                                     start=(kb == 0), stop=(kb == i))
                    last.then_inc(summed, 1)

                def output(b, i, nxt):
                    use = Use("Q", b, i, "out", nxt)
                    pe.wait_ge(q_read[use.bank], use.before)
                    pe.wait_ge(o_done, half(b, i, 1))
                    w = wvo if latent else g["wo_b"]
                    for c in range(OC):
                        last = pe.matmul(Q[use.bank][:, 0:D], oT[:, i, c, :], w[:, c, :],
                                         start=(c == 0), stop=(c == OC - 1))
                    last.then_inc(projected, 1)

                def front(b, i, step, nxt):
                    if step and step[0] == "Q":
                        project(b, i, step[1], nxt)
                    elif step:
                        turn_front(b, i, step[1], nxt)

                def slot(b, i, nxt):
                    for p in range(PAIRS):
                        if p + 2 < PAIRS:
                            scores(b, i, p + 2)
                        turn_probs(b, i, p, nxt)
                        if nxt:
                            front(b, i, FRONT[p], nxt)
                        if p == 4:
                            values(b, i, 0, nxt)
                    values(b, i, 1, nxt)
                    if nxt:
                        first_scores(b, i, nxt, after(b, i))
                    output(b, i, nxt)

                for step in FRONT:
                    front(None, 0, step, True)
                first_scores(None, 0, True, (0, 0))
                run(pe, slot)

            @block.scalar
            def _(act):
                act.sem_inc(o_done, START)
                n = 0
                if latent:
                    for c in range(DC):
                        for side in range(2):
                            act.wait_ge(pre_pe, n + 1)
                            act.activation(wqn[:, c, side * 512:(side + 1) * 512], Q[n % 2][:, :],
                                           ACT.Copy).then_inc(pre_act, 1)
                            n += 1
                norm.scalar(act, g, [T[0], T[1], S[0], S[1]], xnT_done)
                if latent:
                    for m in range(2):
                        act.wait_ge(pre_pe, n + 1)
                        act.activation(kvc[:, 4 * m:4 * m + 4, :], O[m][:, :].rearrange("p (t n) -> p t n", t=4),
                                       ACT.Copy).then_inc(pre_act, 1)
                        n += 1
                    for m in range(WVO_USES):
                        act.wait_ge(pre_pe, n + 1)
                        act.activation(wvo[:, 2 * m:2 * m + 2, :],
                                       Q[n % 2][:, :].rearrange("p (j d) -> p j d", j=2),
                                       ACT.Copy).then_inc(pre_act, 1)
                        n += 1
                    for m in range(2):
                        act.wait_ge(pre_pe, n + 1)
                        act.activation(kT[:, m * 512:(m + 1) * 512], T[m][:, :], ACT.Copy).then_inc(pre_act, 1)
                        n += 1

                def copy_front(b, i, step, nxt):
                    side = 0 if b is None else (i + 1) % 2
                    if latent and step in (("Q", 0), ("Q", 2)):
                        use, h = Use("Q", b, i, step, nxt), 4 * step[1]
                        act.wait_ge(projected, use.written)
                        act.activation(q[:, side, h:h + 8, 0:KVR],
                                       Q[use.bank][:, :].rearrange("p (h n) -> p h n", h=8),
                                       ACT.Copy, scale=SCALE).then_inc(q_read[use.bank], 1)
                    elif not latent and step == ("Q", 1):
                        use = Use("Q", b, i, step, nxt)
                        act.wait_ge(projected, use.written)
                        act.activation(v[:, side, :], Q[use.bank][:, 0:D], ACT.Copy).then_inc(q_read[use.bank], 1)
                    elif step and step[0] == "T" and step != KEYS:
                        use, gr = Use("T", b, i, step, nxt), step[1]
                        act.wait_ge(turned, use.written)
                        act.activation(qT[:, side, 4 * gr:4 * gr + 4, :],
                                       T[use.bank][:, :].rearrange("p (h n) -> p h n", h=4),
                                       ACT.Copy).then_inc(t_read[use.bank], 1)

                def softmax(b, i, p, nxt):
                    act.wait_ge(max_done, pair(b, i, p))
                    if p >= 2:
                        act.wait_ge(turned, Use("T", b, i, ("P", p - 2), nxt).written)
                    elif i == 1:
                        act.wait_ge(turned, Use("T", b, 0, ("P", p + PAIRS - 2), True).written)
                    else:
                        act.wait_ge(turned, Use("T", b - 1, 1, ("P", p + PAIRS - 2), True).written)
                    w = (i + 1) * P
                    for j in range(2):
                        h = 2 * p + j
                        last = act.activation(prob[:, p % 2, j, 0:w], S[p % 2][:, j * 256:j * 256 + w], ACT.Exp,
                                              bias=nmax[:, i, h:h + 1], scale=1.0, accum_out=rsum[:, i, h:h + 1])
                    last.then_inc(exp_done, 1)

                def outputs(b, i, m):
                    act.wait_ge(summed, half(b, i, m))
                    n = OC // 2
                    act.activation(oT[:, i, n * m:n * (m + 1), :],
                                   O[m][:, 0:n * P].rearrange("p (c n) -> p c n", c=n), ACT.Copy).then_inc(o_done, 1)

                def slot(b, i, nxt):
                    softmax(b, i, 0, nxt)
                    softmax(b, i, 1, nxt)
                    for p in range(PAIRS):
                        if p + 2 < PAIRS:
                            softmax(b, i, p + 2, nxt)
                        if nxt:
                            copy_front(b, i, FRONT[p], nxt)
                        if p == 5:
                            outputs(b, i, 0)
                    outputs(b, i, 1)

                for step in FRONT:
                    copy_front(None, 0, step, True)
                run(act, slot)

            @block.gpsimd
            def _(pool):
                norm.gpsimd(pool, g)
                if latent:
                    pool.wait_ge(pre_dve, 3)
                    pool.tensor_tensor(rr[:, :], ms2[:, :], g["halves"][:, :], ALU.pow).then_inc(pre_pool, 1)
                else:
                    pool.memset(vals[:, :, :, :], 0.0).then_inc(pre_pool, 1)
                    pool.wait_ge(pre_pool, 1)
                for i in range(2):
                    pool.wait_ge(xnT_done, 1)
                    pool.tensor_copy(xs[:, i, :, :], g["xnT"][:, :, i * P:(i + 1) * P]).then_inc(staged, 1)
                pool.wait_ge(xnT_done, NT // 2)

                def normalise(b, i, p):
                    pool.wait_ge(recip, pair(b, i, p))
                    w = (i + 1) * P
                    pool.tensor_tensor(prob[:, p % 2, :, 0:w], prob[:, p % 2, :, 0:w],
                                       rinv[:, i, 2 * p:2 * p + 2].unsqueeze(2).broadcast_to([P, 2, w]),
                                       ALU.mult).then_inc(normed, 1)

                def slot(b, i, nxt):
                    more = not isinstance(b, int)
                    for p in range(PAIRS):
                        normalise(b, i, p)
                        if p == 2:
                            pool.wait_ge(summed, half(b, i, 0) - 1)
                            pool.sem_inc(vals_free, 1)
                            if latent:
                                src = kv[:, bass.ds(2 * b + i, 1), 0:KVR].rearrange("p a n -> p (a n)")
                                pool.tensor_copy(vals[:, i, :], src).then_inc(vals_ready, 1)
                            else:
                                pool.tensor_copy(vals[:, i, :, 0:HD],
                                                 v[:, i, :].rearrange("p (h n) -> p h n", h=HEADS)).then_inc(vals_ready, 1)
                        if p == 5 and more:
                            pool.tensor_copy(xs[:, i, :, :],
                                             g["xnT"][:, :, bass.ds(b * SEQ + SEQ + i * P, P)]).then_inc(staged, 1)

                run(pool, slot)

            @block.vector
            def _(dve):
                norm.vector(dve, g)
                step_n = 0

                def own(ins):
                    nonlocal step_n
                    ins.then_inc(pre_dve, 1)
                    step_n += 1
                    dve.wait_ge(pre_dve, step_n)

                if latent:
                    dve.wait_ge(pre_act, WQN_USES + 2)
                    own(dve.tensor_tensor(sq, kvc[:, :, 0:KVR], kvc[:, :, 0:KVR], ALU.mult))
                    own(dve.tensor_reduce(ms[:, :], sq, AX, ALU.add))
                    own(dve.tensor_scalar(ms2[:, :], ms[:, :], 1.0 / KVR, RMS_EPS, ALU.mult, ALU.add))
                    dve.wait_ge(loaded["rope_k"], 16)
                    raw = kvc[:, :, KVR:P].rearrange("p (b i) n -> p b i n", i=2)
                    r1 = rot1[:, 0, :].rearrange("p (b i n) -> p b i n", b=BATCH, i=2)
                    r2 = rot2[:, 0, :].rearrange("p (b i n) -> p b i n", b=BATCH, i=2)
                    H = ROPE // 2
                    for i in range(2):
                        cos, sin = (g["rope_k"][:, i, s, :].unsqueeze(1) for s in range(2))
                        dve.tensor_tensor(r1[:, :, i, :], raw[:, :, i, :], cos.broadcast_to([P, BATCH, ROPE]), ALU.mult)
                        for lo, hi in ((0, H), (H, 0)):
                            last = dve.tensor_tensor(r2[:, :, i, lo:lo + H], raw[:, :, i, hi:hi + H],
                                                     sin[:, :, lo:lo + H].broadcast_to([P, BATCH, H]), ALU.mult)
                    own(last)
                    own(dve.tensor_tensor(kv[:, :, KVR:P], rot1[:, 0, :].rearrange("p (t n) -> p t n", t=NT),
                                          rot2[:, 0, :].rearrange("p (t n) -> p t n", t=NT), ALU.add))
                    dve.wait_ge(pre_pool, 1)
                    dve.wait_ge(loaded["kv_w"], 16)
                    own(dve.tensor_tensor(sq, kvc[:, :, 0:KVR],
                                          rr[:, :].unsqueeze(2).broadcast_to([P, NT, KVR]), ALU.mult))
                    own(dve.tensor_tensor(kv[:, :, 0:KVR], sq,
                                          g["kv_w"][:, :].unsqueeze(1).broadcast_to([P, NT, KVR]), ALU.mult))
                    dve.wait_ge(loaded["rope_q"], 16)
                else:
                    own(dve.memset(q[:, :, :, :], 0.0))
                    dve.wait_ge(loaded["rope_b"], 16)

                def rotate_latent(b, i, step, nxt):
                    use, k = Use("Q", b, i, step, nxt), step[1] // 2
                    side = 0 if b is None else (i + 1) % 2
                    dve.wait_ge(projected, use.written)
                    src = Q[use.bank][:, :].rearrange("p (h n) -> p h n", h=8)
                    r1 = rot1[:, k, :].rearrange("p (h n) -> p h n", h=8)
                    r2 = rot2[:, k, :].rearrange("p (h n) -> p h n", h=8)
                    cos, sin = (g["rope_q"][:, side, s, :].unsqueeze(1) for s in range(2))
                    H = ROPE // 2
                    dve.tensor_tensor(r1, src, cos.broadcast_to([P, 8, ROPE]), ALU.mult)
                    for lo, hi in ((0, H), (H, 0)):
                        last = dve.tensor_tensor(r2[:, :, lo:lo + H], src[:, :, hi:hi + H],
                                                 sin[:, :, lo:lo + H].broadcast_to([P, 8, H]), ALU.mult)
                    last.then_inc(q_read[use.bank], 1)
                    dve.wait_ge(q_read[use.bank], use.before + 1)
                    dve.tensor_tensor(q[:, side, 8 * k:8 * k + 8, KVR:P], r1, r2, ALU.add).then_inc(q_ready, 1)

                def rotate_all(b, i, step, nxt):
                    use = Use("Q", b, i, step, nxt)
                    side = 0 if b is None else (i + 1) % 2
                    dve.wait_ge(projected, use.written)
                    src = Q[use.bank][:, :].rearrange("p (s h n) -> p s h n", s=2, h=HEADS)
                    r1 = rot1[:, 0, :].rearrange("p (s h n) -> p s h n", s=2, h=HEADS)
                    r2 = rot2[:, 0, :].rearrange("p (s h n) -> p s h n", s=2, h=HEADS)
                    H = HD // 2
                    for s in range(2):
                        cos, sin = (g["rope_b"][:, side, s, f, :].unsqueeze(1) for f in range(2))
                        dve.tensor_tensor(r1[:, s], src[:, s], cos.broadcast_to([P, HEADS, HD]), ALU.mult)
                        for lo, hi in ((0, H), (H, 0)):
                            last = dve.tensor_tensor(r2[:, s, :, lo:lo + H], src[:, s, :, hi:hi + H],
                                                     sin[:, :, lo:lo + H].broadcast_to([P, HEADS, H]), ALU.mult)
                    last.then_inc(q_read[use.bank], 1)
                    dve.wait_ge(q_read[use.bank], use.before + 1)
                    for k in range(2):
                        start = (side * HEADS + 8 * k) * P
                        diagonal = bass.AP(q, start, [[2 * HEADS * P, P], [P + HD, 8], [1, HD]])
                        at = slice(k * P, (k + 1) * P)
                        dve.tensor_tensor(diagonal, rot1[:, 0, at].rearrange("p (h n) -> p h n", h=8),
                                          rot2[:, 0, at].rearrange("p (h n) -> p h n", h=8),
                                          ALU.add).then_inc(q_ready, 1)
                    dve.tensor_tensor(kr[:, :], rot1[:, 0, D:2 * D], rot2[:, 0, D:2 * D], ALU.add).then_inc(kr_ready, 1)

                def keys(b, i, step, nxt):
                    use = Use("T", b, i, step, nxt)
                    side = 0 if b is None else (i + 1) % 2
                    dve.wait_ge(turned, use.written)
                    dve.tensor_copy(kT[:, :, side * P:(side + 1) * P],
                                    T[use.bank][:, 0:2 * P].rearrange("p (k n) -> p k n", k=2)).then_inc(t_read[use.bank], 1)

                def front(b, i, step, nxt):
                    if latent and step in (("Q", 1), ("Q", 3)):
                        rotate_latent(b, i, step, nxt)
                    elif not latent and step == ("Q", 0):
                        rotate_all(b, i, step, nxt)
                    elif step == KEYS:
                        keys(b, i, step, nxt)

                def maxima(b, i, p):
                    dve.wait_ge(scored, pair(b, i, p))
                    dve.tensor_reduce(nmax[:, i, 2 * p:2 * p + 2],
                                      S[p % 2][:, :].rearrange("p (j n) -> p j n", j=2)[:, :, 0:(i + 1) * P],
                                      AX, ALU.max, negate=True).then_inc(max_done, 1)

                def invert(b, i, p):
                    dve.wait_ge(exp_done, pair(b, i, p))
                    dve.reciprocal(rinv[:, i, 2 * p:2 * p + 2], rsum[:, i, 2 * p:2 * p + 2]).then_inc(recip, 1)

                def probs(b, i, p, nxt):
                    use, m = Use("T", b, i, ("P", p), nxt), p // 4
                    dve.wait_ge(turned, use.written)
                    if p % 4 == 0:
                        dve.wait_ge(summed, half(b, i, m) - 2)
                    w = 2 * (i + 1) * P
                    dve.tensor_copy(probT[:, m, :, 0:i + 1, p % 4, :],
                                    T[use.bank][:, 0:w].rearrange("p (j k n) -> p j k n", j=2, k=i + 1),
                                    ).then_inc(t_read[use.bank], 1)

                def add(b, i, nxt):
                    use = Use("Q", b, i, "out", nxt)
                    dve.wait_ge(projected, use.written)
                    x = g["x"][:, bass.ds(b * 2 + i, 1), :].rearrange("p a d -> p (a d)")
                    dve.tensor_tensor(x, Q[use.bank][:, 0:D], x, ALU.add).then_inc(q_read[use.bank], 1)

                def slot(b, i, nxt):
                    invert(b, i, 0)
                    for p in range(PAIRS):
                        if p + 1 < PAIRS:
                            invert(b, i, p + 1)
                        if p + 2 < PAIRS:
                            maxima(b, i, p + 2)
                        probs(b, i, p, nxt)
                        if nxt:
                            front(b, i, FRONT[p], nxt)
                    if nxt:
                        maxima(*after(b, i), 0)
                        maxima(*after(b, i), 1)
                    add(b, i, nxt)

                for step in FRONT:
                    front(None, 0, step, True)
                maxima(0, 0, 0)
                maxima(0, 0, 1)
                run(dve, slot)


def experts(nc, g, a, tag, before, run):
    with ExitStack() as ctx:
        def sb(name, shape, dt=F32):
            return ctx.enter_context(nc.sbuf_tensor(name + tag, shape, dt))

        def sem(name):
            return g["sem"](name + tag)

        E, K = EXPERTS, TOP
        bank = [ctx.enter_context(nc.psum_tensor(f"bank{i}" + tag, [P, 512], F32)) for i in range(8)]
        norm = Norm(ctx, nc, g, tag, before)
        loaded = g["loaded"]
        ids = sb("ids", [P, SLOTS], U32)
        wts = sb("wts", [P, SLOTS])
        row = sb("row", [1, P], U32)
        place = sb("place", [P, NT * K], I32)

        count = g["count"]
        iota, tri, ones = (count[:, n * P:(n + 1) * P] for n in range(3))
        full = count[:, 3 * P:3 * P + 8]
        tokens = count[:, 3 * P + 8:3 * P + 16]
        index = iota_p = count[:, 3 * P + 16:3 * P + 17]

        with ExitStack() as inner:
            def sb(name, shape, dt=F32):
                return inner.enter_context(nc.sbuf_tensor(name + tag, shape, dt))

            lg = sb("lg", [P, NT, E + 1])
            lgs = sb("lgs", [P, NT, E])
            pr = sb("pr", [P, NT, E])
            small = sb("small", [P, 6, NT])
            top = sb("top", [P, NT, 8])
            best = sb("best", [P, NT, 8], U32)
            bestf = sb("bestf", [P, NT * K])
            onehot = sb("onehot", [P, NT * K, E])
            work = sb("work", [P, NT * K, E])
            chosen = sb("chosen", [P, NT, E])
            base = sb("base", [P, NT + 1, E])
            pos = sb("pos", [P, NT, E])
            over = sb("over", [P, E, 8])
            tiles = sb("tiles", [P, E])
            cum = sb("cum", [P, E])
            begin = sb("begin", [P, E])
            junk = sb("junk", [P, E])
            slot_expert = sb("slot_expert", [P, 2])
            placef = sb("placef", [P, NT * K])
            part = sb("part", [P, 2, NT * K], I32)
            partf = sb("partf", [P, 2, NT * K])
            in_row = sb("in_row", [P, 2, K, P])
            in_slot = sb("in_slot", [P, 2, 3, K, SLOTS])
            sg = sb("sg", [P, 2, 512])
            up = sb("up", [P, 2, 512])
            hT = sb("hT", [P, SHARED_CHUNKS, TOK])

            xnT_done = sem("xnT_done")
            stored = sem("xn_stored")
            logits = sem("logits")
            lg_done = sem("lg_done")
            chain = sem("chain")
            ex_done = sem("ex_done")
            chosen_ready = sem("chosen_ready")
            counted = sem("counted")
            expert_ready = sem("expert_ready")
            expert_turned = sem("expert_turned")
            in_ready = sem("in_ready")
            listed = sem("listed")
            gu = sem("gu")
            gu_read = sem("gu_read")
            sgu_read = sem("sgu_read")
            h_done = sem("h_done")
            shared = sem("shared")
            added = sem("added")
            routed = sem("routed")
            DONE = {}

            with nc.Block() as block:
                @block.sync
                def _(sp):
                    sp.wait_ge(norm.sem("xn_done"), norm.count("xn_done", NT))
                    sp.dma_start(g["xn_dram"].rearrange("(n p) d -> p n d", p=P), g["xn"][:, :, :]).then_inc(stored, 16)
                    sp.wait_ge(stored, 16)

                @block.gpsimd
                def _(pool):
                    norm.gpsimd(pool, g)
                    for n in range(2 * SHARED_CHUNKS):
                        pool.wait_ge(gu_read, 2 * n + 2)
                        pool.tensor_tensor(hT[:, n // 2, (n % 2) * 512:(n % 2 + 1) * 512], sg[:, n % 2, :],
                                           up[:, n % 2, :], ALU.mult).then_inc(h_done, 1)

                @block.tensor
                def _(pe):
                    pe.wait_ge(g["loaded_x"], 48)
                    norm.tensor(pe, g, bank[0:4])
                    pe.wait_ge(xnT_done, NT // 2)
                    pe.wait_ge(loaded["gate"], 16)
                    for t in range(NT):
                        for c in range(DC):
                            last = pe.matmul(bank[0][:, t * (E + 1):(t + 1) * (E + 1)],
                                             g["xnT"][:, c, t * P:(t + 1) * P], g["gate"][:, c, :],
                                             start=(c == 0), stop=(c == DC - 1))
                    last.then_inc(logits, 1)

                    def shared_up(n):
                        ch, half = n // 2, n % 2
                        if n >= 2:
                            pe.wait_ge(gu_read, 2 * (n - 1))
                        for s in range(2):
                            for c in range(DC):
                                col = (s * SHARED_CHUNKS + ch) * P
                                last = pe.matmul(bank[4 + 2 * (n % 2) + s][:, :], g["se_up"][:, c, col:col + P],
                                                 g["xnT"][:, c, half * 512:(half + 1) * 512],
                                                 start=(c == 0), stop=(c == DC - 1))
                        last.then_inc(gu, 1)

                    pe.wait_ge(loaded["se_up"], 16)
                    pe.wait_ge(loaded["count"], 16)
                    for n in range(4):
                        shared_up(n)
                    pe.wait_ge(chosen_ready, 1)
                    pe.matmul(bank[1][:, 0:NT * E], tri, chosen[:, :, :], start=True, stop=True)
                    pe.matmul(bank[2][:, 0:NT * E], ones, chosen[:, :, :], start=True, stop=True).then_inc(counted, 1)
                    for n in range(4, 2 * SHARED_CHUNKS):
                        shared_up(n)
                    pe.wait_ge(expert_ready, 1)
                    pe.matmul(bank[0][0:1, 0:P], slot_expert[:, 1:2], g["ident"][:, :],
                              start=True, stop=True).then_inc(expert_turned, 1)
                    pe.wait_ge(h_done, 2 * SHARED_CHUNKS)
                    pe.wait_ge(gu_read, 4 * SHARED_CHUNKS)
                    pe.wait_ge(loaded["se_down"], 16)
                    for t in range(NT):
                        for c in range(SHARED_CHUNKS):
                            last = pe.matmul(bank[4 + t // 2][:, (t % 2) * D:(t % 2 + 1) * D],
                                             hT[:, c, t * P:(t + 1) * P], g["se_down"][:, c, :],
                                             start=(c == 0), stop=(c == SHARED_CHUNKS - 1))
                        if t % 2:
                            last.then_inc(shared, 1)
                    for t in range(NT):
                        pe.wait_ge(in_ready, t + 1)
                        for k in range(K):
                            last = pe.matmul(bank[3][:, 0:2 * SLOTS].rearrange("p (v s) -> p v s", v=2),
                                             in_row[:, t % 2, k, :], in_slot[:, t % 2, 1:3, k, :],
                                             start=(t == 0 and k == 0), stop=(t == NT - 1 and k == K - 1))
                        last.then_inc(listed, 1)

                @block.scalar
                def _(act):
                    norm.scalar(act, g, bank[0:4], xnT_done)
                    act.wait_ge(logits, 1)
                    act.activation(lg[:, :, :], bank[0][:, 0:NT * (E + 1)].rearrange("p (t e) -> p t e", t=NT),
                                   ACT.Copy).then_inc(lg_done, 1)
                    act.wait_ge(chain, 2)
                    act.activation(pr[:, :, :], lgs[:, :, :], ACT.Exp).then_inc(ex_done, 1)
                    act.activation(small[:, 3, :], lg[:, :, E], ACT.Exp, scale=-1.0).then_inc(ex_done, 1)
                    for n in range(2 * SHARED_CHUNKS):
                        act.wait_ge(gu, n + 1)
                        if n >= 2:
                            act.wait_ge(h_done, n - 1)
                        act.activation(sg[:, n % 2, :], bank[4 + 2 * (n % 2)][:, :], ACT.Silu).then_inc(gu_read, 1)
                        act.activation(up[:, n % 2, :], bank[5 + 2 * (n % 2)][:, :], ACT.Copy).then_inc(gu_read, 1)

                @block.vector
                def _(dve):
                    norm.vector(dve, g)
                    step = 0

                    def own(ins):
                        nonlocal step
                        ins.then_inc(chain, 1)
                        step += 1
                        dve.wait_ge(chain, step)

                    def over_experts(ap):
                        return ap.unsqueeze(2).broadcast_to([P, NT, E])

                    dve.wait_ge(loaded["count"], 16)
                    dve.memset(base[:, 0, :], 0.0)
                    dve.wait_ge(lg_done, 1)
                    own(dve.tensor_reduce(small[:, 0, :], lg[:, :, 0:E], AX, ALU.max, negate=True))
                    own(dve.tensor_tensor(lgs[:, :, :], lg[:, :, 0:E], over_experts(small[:, 0, :]), ALU.add))
                    dve.wait_ge(ex_done, 2)
                    own(dve.tensor_reduce(small[:, 1, :], pr[:, :, :], AX, ALU.add))
                    own(dve.reciprocal(small[:, 2, :], small[:, 1, :]))
                    own(dve.tensor_tensor(lgs[:, :, :], pr[:, :, :], over_experts(small[:, 2, :]), ALU.mult))
                    own(dve.tensor_scalar(small[:, 4, :], small[:, 3, :], 1.0, None, ALU.add))
                    dve.reciprocal(small[:, 5, :], small[:, 4, :])
                    for t in range(NT):
                        last = dve.max(top[:, t, :], lgs[:, t, :])
                    own(last)
                    for t in range(NT):
                        last = dve.max_index(best[:, t, :], top[:, t, :], lgs[:, t, :])
                    own(last)
                    own(dve.tensor_copy(bestf[:, :].rearrange("p (t k) -> p t k", t=NT), best[:, :, 0:K]))
                    own(dve.tensor_tensor(onehot[:, :, :], iota[:, 0:E].unsqueeze(1).broadcast_to([P, NT * K, E]),
                                          bestf[:, :].unsqueeze(2).broadcast_to([P, NT * K, E]), ALU.is_equal))
                    dve.tensor_reduce(chosen[:, :, :], onehot[:, :, :].rearrange("p (t k) e -> p t e k", t=NT),
                                      AX, ALU.add).then_inc(chosen_ready, 1)
                    dve.wait_ge(counted, 1)
                    for t in range(NT):
                        own(dve.tensor_tensor(base[:, t + 1, :], bank[2][:, t * E:(t + 1) * E], base[:, t, :], ALU.add))
                    own(dve.tensor_tensor(pos[:, :, :], bank[1][:, 0:NT * E].rearrange("p (t e) -> p t e", t=NT),
                                          base[:, 0:NT, :], ALU.add))
                    own(dve.tensor_tensor(over[:, :, :], base[:, NT, :].unsqueeze(2).broadcast_to([P, E, 8]),
                                          full.unsqueeze(1).broadcast_to([P, E, 8]), ALU.is_gt))
                    own(dve.tensor_reduce(tiles[:, :], over[:, :, :], AX, ALU.add))
                    own(dve.tensor_tensor_scan(cum[:, :], ones[:, 0:E], tiles[:, :], 0.0, ALU.mult, ALU.add))
                    own(dve.tensor_tensor(begin[:, :], cum[:, :], tiles[:, :], ALU.subtract))
                    own(dve.tensor_scalar(junk[:, :], cum[:, :], index, 0.0, ALU.is_le, ALU.add,
                                          accum_out=slot_expert[:, 0:1]))
                    dve.tensor_scalar(slot_expert[:, 1:2], slot_expert[:, 0:1], float(E - 1), None,
                                      ALU.min).then_inc(expert_ready, 1)
                    own(dve.scalar_tensor_tensor(pos[:, :, :], begin[:, :].unsqueeze(1).broadcast_to([P, NT, E]),
                                                 float(P), pos[:, :, :], ALU.mult, ALU.add))
                    own(dve.tensor_tensor(work[:, :, :].rearrange("p (t k) e -> p t k e", t=NT),
                                          onehot[:, :, :].rearrange("p (t k) e -> p t k e", t=NT),
                                          pos[:, :, :].unsqueeze(2).broadcast_to([P, NT, K, E]), ALU.mult))
                    own(dve.tensor_reduce(placef[:, :], work[:, :, :], AX, ALU.add))
                    own(dve.tensor_copy(place[:, :], placef[:, :]))
                    dve.tensor_scalar(part[:, 0, :], place[:, :], P - 1, None, ALU.bitwise_and)
                    own(dve.tensor_scalar(part[:, 1, :], place[:, :], 7, None, ALU.logical_shift_right))
                    own(dve.tensor_copy(partf[:, :, :], part[:, :, :]))
                    for t in range(NT):
                        at = slice(t * K, (t + 1) * K)
                        if t >= 2:
                            dve.wait_ge(listed, t - 1)
                        dve.tensor_tensor(in_row[:, t % 2, :, :], iota.unsqueeze(1).broadcast_to([P, K, P]),
                                          partf[:, 0, at].unsqueeze(2).broadcast_to([P, K, P]), ALU.is_equal)
                        own(dve.tensor_tensor(in_slot[:, t % 2, 0], iota[:, 0:SLOTS].unsqueeze(1).broadcast_to([P, K, SLOTS]),
                                              partf[:, 1, at].unsqueeze(2).broadcast_to([P, K, SLOTS]), ALU.is_equal))
                        dve.tensor_scalar(in_slot[:, t % 2, 1], in_slot[:, t % 2, 0], tokens[:, t:t + 1], None, ALU.mult)
                        dve.tensor_tensor(in_slot[:, t % 2, 2], in_slot[:, t % 2, 0],
                                          top[:, t, 0:K].unsqueeze(2).broadcast_to([P, K, SLOTS]),
                                          ALU.mult).then_inc(in_ready, 1)
                    dve.wait_ge(expert_turned, 1)
                    dve.tensor_copy(row[:, :], bank[0][0:1, 0:P])
                    for t in range(NT):
                        dve.wait_ge(shared, t // 2 + 1)
                        dve.scalar_tensor_tensor(g["x"][:, t, :], bank[4 + t // 2][:, (t % 2) * D:(t % 2 + 1) * D],
                                                 small[:, 5, t:t + 1], g["x"][:, t, :], ALU.mult, ALU.add)
                    dve.wait_ge(listed, NT)
                    dve.tensor_copy(ids[:, :], bank[3][:, 0:SLOTS])
                    dve.tensor_copy(wts[:, :], bank[3][:, SLOTS:2 * SLOTS])

        with ExitStack() as inner:
            def sb(name, shape, dt=F32):
                return inner.enter_context(nc.sbuf_tensor(name + tag, shape, dt))

            DEPTH = SLOT_DEPTH
            assert TURNS * DEPTH == SLOTS
            w13 = sb("w13", [P, DEPTH, DC, 2 * INTER])
            w2 = sb("w2", [IC, DEPTH, 2, D])
            who = sb("who", [P, DEPTH], U32)
            xg = sb("xg", [P, DEPTH, D])
            xgT = sb("xgT", [P, 2, DC, P])
            act_g = sb("act_g", [P, 2, INTER])
            h = sb("h", [P, 2, 2 * IC])
            hT = sb("hTs", [IC, 2, 2, P])
            y = sb("y", [P, DEPTH, D])
            w_loaded = g["w_loaded"]
            x_gathered = g["x_gathered"]
            y_stored = g["y_stored"]
            who_ready = sem("who_ready")
            who_seen = sem("who_seen")
            cleared = sem("cleared")
            x_turned = sem("x_turned")
            xgT_done = sem("xgT_done")
            gu_done = sem("gu_done")
            silu_done = sem("silu_done")
            h_done = sem("h_done_s")
            h_turned = sem("h_turned")
            hT_done = sem("hT_done")
            down_done = sem("down_done")
            y_done = sem("y_done")
            TX, TH, G, Y = bank[0:2], bank[2:4], bank[4:6], bank[6:8]

            with nc.Block() as block:
                @block.sync
                def _(sp):
                    def load(j, s):
                        e = sp.value_load(row[0:1, bass.ds(s, 1)], min_val=0, max_val=EXPERTS - 1)
                        sp.dma_start(w13[:, j, :, :], a["w13"][bass.ds(e, 1)].rearrange("a p c n -> p (a c) n")).then_inc(w_loaded[j], 16)
                        sp.dma_start(w2[:, j, :, :], a["w2"][bass.ds(e, 1)].rearrange("a p c n -> p (a c) n")).then_inc(w_loaded[j], 16)

                    def store(turn, j):
                        s = turn * DEPTH + j
                        sp.wait_ge(y_done, s + 1)
                        sp.dma_start(g["y_dram"][bass.ds(s * P, P), :], y[:, j, :]).then_inc(y_stored[j], 16)

                    for j in range(DEPTH):
                        load(j, j)
                    with sp.Fori(0, TURNS - 1) as turn:
                        for j in range(DEPTH):
                            sp.wait_ge(down_done, turn * DEPTH + j + 1)
                            load(j, turn * DEPTH + DEPTH + j)
                            store(turn, j)
                    for j in range(DEPTH):
                        store(TURNS - 1, j)
                    for j in range(DEPTH):
                        sp.wait_ge(y_stored[j], 16 * TURNS * (run + 1))

                @block.gpsimd
                def _(pool):
                    pool.memset(h[:, :, :], 0.0).then_inc(cleared, 1)

                    def gather(s, j):
                        pool.tensor_copy(who[:, j:j + 1], ids[:, bass.ds(s, 1)]).then_inc(who_ready, 1)
                        pool.wait_ge(who_ready, s + 1)
                        pool.sem_inc(who_seen, 1)
                        pool.indirect_dma_start(xg[:, j, :], None, g["xn_dram"],
                                                bass.IndirectOffsetOnAxis(ap=who[:, j:j + 1], axis=0),
                                                ).then_inc(x_gathered[j], 16)

                    for j in range(DEPTH):
                        gather(j, j)
                    with pool.Fori(0, TURNS - 1) as turn:
                        for j in range(DEPTH):
                            pool.wait_ge(x_turned, turn * DEPTH + j + 1)
                            gather(turn * DEPTH + DEPTH + j, j)

                @block.tensor
                def _(pe):
                    def turn_x(turn, j):
                        s = turn * DEPTH + j
                        pe.wait_ge(x_gathered[j], 16 * (turn + 1 + run * TURNS))
                        if not (isinstance(turn, int) and s < 2):
                            pe.wait_ge(xgT_done, s - 1)
                        for c in range(DC):
                            last = pe.transpose(TX[j % 2][:, c * P:(c + 1) * P], xg[:, j, c * P:(c + 1) * P],
                                                g["ident"][:, :])
                        last.then_inc(x_turned, 1)

                    def gate_up(turn, j):
                        s = turn * DEPTH + j
                        pe.wait_ge(w_loaded[j], 32 * (turn + 1 + run * TURNS))
                        pe.wait_ge(xgT_done, s + 1)
                        if not (isinstance(turn, int) and s < 2):
                            pe.wait_ge(h_done, s - 1)
                        for c in range(DC):
                            last = pe.matmul(G[j % 2][:, 0:2 * INTER], xgT[:, j % 2, c, :], w13[:, j, c, :],
                                             start=(c == 0), stop=(c == DC - 1))
                        last.then_inc(gu_done, 1)

                    def turn_h(turn, j):
                        s = turn * DEPTH + j
                        pe.wait_ge(h_done, s + 1)
                        if not (isinstance(turn, int) and s < 2):
                            pe.wait_ge(hT_done, s - 1)
                        for c in range(2):
                            last = pe.transpose(TH[j % 2][0:IC, c * P:(c + 1) * P], h[:, j % 2, c * IC:(c + 1) * IC],
                                                g["ident"][:, :])
                        last.then_inc(h_turned, 1)

                    def down(turn, j):
                        s = turn * DEPTH + j
                        pe.wait_ge(hT_done, s + 1)
                        if not (isinstance(turn, int) and s < 2):
                            pe.wait_ge(y_done, s - 1)
                        for c in range(2):
                            last = pe.matmul(Y[j % 2][:, 0:D], hT[:, j % 2, c, :], w2[:, j, c, :],
                                             start=(c == 0), stop=(c == 1))
                        last.then_inc(down_done, 1)

                    def slots(turn, first=False, final=False):
                        for j in range(DEPTH):
                            before = (turn, j - 1) if j > 0 else (turn - 1, DEPTH - 1)
                            if j > 0 or not first:
                                turn_h(*before)
                            if j < DEPTH - 1:
                                turn_x(turn, j + 1)
                            elif not final:
                                turn_x(turn + 1, 0)
                            gate_up(turn, j)
                            if j > 0 or not first:
                                down(*before)

                    turn_x(0, 0)
                    slots(0, first=True)
                    with pe.Fori(1, TURNS - 1) as turn:
                        slots(turn)
                    slots(TURNS - 1, final=True)
                    turn_h(TURNS - 1, DEPTH - 1)
                    down(TURNS - 1, DEPTH - 1)

                @block.scalar
                def _(act):
                    def silu(turn, j):
                        act.wait_ge(gu_done, turn * DEPTH + j + 1)
                        act.activation(act_g[:, j % 2, :], G[j % 2][:, 0:INTER], ACT.Silu).then_inc(silu_done, 1)

                    def weigh(turn, j):
                        s = turn * DEPTH + j
                        act.wait_ge(down_done, s + 1)
                        if not (isinstance(turn, int) and turn + run == 0):
                            act.wait_ge(y_stored[j], 16 * (turn + run * TURNS))
                        act.activation(y[:, j, :], Y[j % 2][:, 0:D], ACT.Copy,
                                       scale=wts[:, bass.ds(s, 1)]).then_inc(y_done, 1)

                    def slots(turn, first=False):
                        for j in range(DEPTH):
                            silu(turn, j)
                            if j > 0:
                                weigh(turn, j - 1)
                            elif not first:
                                weigh(turn - 1, DEPTH - 1)

                    slots(0, first=True)
                    with act.Fori(1, TURNS) as turn:
                        slots(turn)
                    weigh(TURNS - 1, DEPTH - 1)

                @block.vector
                def _(dve):
                    dve.wait_ge(cleared, 1)

                    def copy_x(turn, j):
                        dve.wait_ge(x_turned, turn * DEPTH + j + 1)
                        dve.tensor_copy(xgT[:, j % 2, :, :],
                                        TX[j % 2][:, 0:D].rearrange("p (c n) -> p c n", c=DC)).then_inc(xgT_done, 1)

                    def gate(turn, j):
                        s = turn * DEPTH + j
                        dve.wait_ge(silu_done, s + 1)
                        dve.tensor_tensor(h[:, j % 2, 0:INTER], G[j % 2][:, INTER:2 * INTER], act_g[:, j % 2, :],
                                          ALU.mult).then_inc(h_done, 1)

                    def copy_h(turn, j):
                        dve.wait_ge(h_turned, turn * DEPTH + j + 1)
                        dve.tensor_copy(hT[:, j % 2, :, :],
                                        TH[j % 2][0:IC, 0:D].rearrange("p (c n) -> p c n", c=2)).then_inc(hT_done, 1)

                    def slots(turn, first=False, final=False):
                        for j in range(DEPTH):
                            if j > 0:
                                copy_h(turn, j - 1)
                            elif not first:
                                copy_h(turn - 1, DEPTH - 1)
                            if j < DEPTH - 1:
                                copy_x(turn, j + 1)
                            elif not final:
                                copy_x(turn + 1, 0)
                            gate(turn, j)

                    copy_x(0, 0)
                    slots(0, first=True)
                    with dve.Fori(1, TURNS - 1) as turn:
                        slots(turn)
                    slots(TURNS - 1, final=True)
                    copy_h(TURNS - 1, DEPTH - 1)

        with ExitStack() as inner:
            DEPTH = GATHER_DEPTH
            yg = inner.enter_context(nc.sbuf_tensor("yg" + tag, [P, DEPTH, D], F32))
            gathered = g["y_gathered"]
            summed = sem("y_summed")
            with nc.Block() as block:
                @block.gpsimd
                def _(pool):
                    for n in range(NT * K):
                        if n >= DEPTH:
                            pool.wait_ge(summed, n - DEPTH + 1)
                        pool.indirect_dma_start(yg[:, n % DEPTH, :], None, g["y_dram"],
                                                bass.IndirectOffsetOnAxis(ap=place[:, n:n + 1].bitcast(U32), axis=0),
                                                ).then_inc(gathered[n % DEPTH], 16)

                @block.vector
                def _(dve):
                    for n in range(NT * K):
                        dve.wait_ge(gathered[n % DEPTH], 16 * (n // DEPTH + 1 + run * NT * K // DEPTH))
                        if n % K:
                            dve.wait_ge(summed, n)
                        dve.tensor_tensor(g["x"][:, n // K, :], g["x"][:, n // K, :], yg[:, n % DEPTH, :],
                                          ALU.add).then_inc(summed, 1)


def _rope(dim, scale):
    inv = (1.0 / 10000.0 ** (np.arange(0, dim, 2, dtype=np.float32) / np.float32(dim))).astype(np.float32)
    f = np.outer(np.arange(SEQ, dtype=np.float32), inv).astype(np.float32)
    f = np.concatenate([f, f], axis=1)
    sign = np.where(np.arange(dim) < dim // 2, -1.0, 1.0)
    both = np.stack([np.cos(f), np.sin(f) * sign], axis=1) * scale
    return np.ascontiguousarray(both.reshape(2, P, 2, dim).transpose(1, 0, 2, 3).astype(np.float32))


def _chunks(w):
    return np.ascontiguousarray(w.reshape(-1, P, w.shape[-1]).transpose(1, 0, 2))


def kernel(**inputs):
    import ml_dtypes
    import concourse.bacc as bacc
    from concourse.bass_utils import run_bass_kernel_spmd

    x = {k.replace("L0_", ""): np.asarray(v) for k, v in inputs.items()}
    wq = x["attn_a_wq"].reshape(D, HEADS, NOPE + ROPE)
    wkv = x["attn_a_wkv_b"].reshape(KVR, HEADS, NOPE + VD)
    se_up = np.zeros((D, 2, SHARED_CHUNKS * P), np.float32)
    se_up[:, :, 0:704] = x["ffn_se_gate_up_w"].T.reshape(D, 2, 704)
    se_down = np.zeros((SHARED_CHUNKS * P, D), np.float32)
    se_down[0:704] = x["ffn_se_down_w"].T
    w2 = np.zeros((EXPERTS, 2 * IC, D), np.float32)
    w2[:, 0:INTER] = x["ffn_w2"].transpose(0, 2, 1)
    wo_b = np.zeros((HEADS, 2 * HD, D), np.float32)
    wo_b[:, 0:HD] = x["attn_b_Wo"].T.reshape(HEADS, HD, D)
    p = np.arange(P)
    count = np.concatenate([
        np.broadcast_to(p, (P, P)), p[:, None] < p[None, :], np.ones((P, P)),
        np.broadcast_to(np.arange(8) * P, (P, 8)), np.arange(8) * P + p[:, None], p[:, None],
    ], axis=1).astype(np.float32)
    mask = np.stack([np.eye(P), np.where(p[None, :] > p[:, None], -3e38, 0.0)], axis=1).astype(ml_dtypes.bfloat16)
    arrays = {
        "x": x["attn_a_x"].reshape(TOK, D),
        "ident": np.eye(P, dtype=np.float32),
        "mask": mask,
        "wq_nopeT": wq[:, :, 0:NOPE].transpose(2, 1, 0),
        "wq_rope": _chunks(wq[:, :, NOPE:].reshape(D, HEADS * ROPE)),
        "wkT": wkv[:, :, 0:NOPE].transpose(2, 1, 0),
        "wvT": wkv[:, :, NOPE:].transpose(2, 1, 0),
        "wo_a": x["attn_a_wo"].reshape(HEADS, VD, D).transpose(1, 0, 2),
        "wkv_a": _chunks(x["attn_a_wkv_a"]),
        "kv_w": np.broadcast_to(x["attn_a_kv_norm_w"], (P, KVR)),
        "rope_k": _rope(ROPE, 1.0),
        "rope_q": _rope(ROPE, float(NOPE + ROPE) ** -0.5),
        "gate": _chunks(np.concatenate([x["ffn_gate_w"], x["ffn_shared_gate_w"]]).T),
        "se_up": _chunks(se_up.reshape(D, -1)),
        "se_down": _chunks(se_down),
        "count": count,
        "w_rot": _chunks(np.concatenate([x["attn_b_Wq"], x["attn_b_Wk"], x["attn_b_Wv"]]).T),
        "rope_b": np.stack([_rope(HD, float(HD) ** -0.5), _rope(HD, 1.0)], axis=2),
        "wo_b": wo_b.reshape(4, P, D).transpose(1, 0, 2),
        "w13": x["ffn_w13"].transpose(0, 2, 1).reshape(EXPERTS, DC, P, 2 * INTER).transpose(0, 2, 1, 3),
        "w2": w2.reshape(EXPERTS, 2, IC, D).transpose(0, 2, 1, 3),
    }
    arrays = {k: np.ascontiguousarray(v) for k, v in arrays.items()}
    nc = bacc.Bacc("TRN2", target_bir_lowering=False, num_devices=1)
    aps = {k: nc.dram_tensor(k + "_dram", v.shape, mybir.dt.from_np(v.dtype), kind="ExternalInput").ap()
           for k, v in arrays.items()}
    out = nc.dram_tensor("out_dram", (TOK, D), F32, kind="ExternalOutput").ap()
    build(nc, aps, out)
    r = run_bass_kernel_spmd(nc, [{k + "_dram": v for k, v in arrays.items()}], core_ids=[0])
    return r.results[0]["out_dram"].reshape(BATCH, SEQ, D)
```

```python
from contextlib import ExitStack

import numpy as np

import concourse.bass as bass
from concourse import mybir

F32 = mybir.dt.float32
BF16 = mybir.dt.bfloat16
I32 = mybir.dt.int32
U32 = mybir.dt.uint32
ALU = mybir.AluOpType
ACT = mybir.ActivationFunctionType
AX = mybir.AxisListType.X

P = 128
BATCH, SEQ, D = 4, 256, 256
TOK = BATCH * SEQ
NT = TOK // P
DC = D // P
HEADS = 16
PAIRS = HEADS // 2
NOPE, ROPE, VD, KVR = 128, 64, 128, 64
HD = D // HEADS
EXPERTS, TOP, INTER = 60, 4, 176
IC = 96
SHARED_CHUNKS = 6
SLOTS = TOP * TOK // P + EXPERTS
SLOT_DEPTH = 4
GATHER_DEPTH = 8
TURNS = SLOTS // SLOT_DEPTH
LN_EPS, RMS_EPS = 1e-5, 1e-6


def build(nc, a, out):
    with ExitStack() as ctx:
        def sb(name, shape, dt=F32):
            return ctx.enter_context(nc.sbuf_tensor(name, shape, dt))

        def sem(name):
            return ctx.enter_context(nc.semaphore(name))

        g = {"sem": sem}
        g["x"] = sb("x", [P, NT, D])
        g["xn"] = sb("xn", [P, NT, D])
        g["xnT"] = sb("xnT", [P, DC, TOK])
        g["ident"] = sb("ident", [P, P])
        g["mask"] = sb("mask", [P, 2, P], BF16)
        g["halves"] = sb("halves", [P, NT])
        g["ln_stats"] = sb("ln_stats", [P, NT, 6])
        g["loaded_x"] = sem("loaded_x")
        names = {}
        for name in LOADS:
            shape = list(a[name].shape)
            g[name] = sb("w_" + name, shape)
            names[name] = sem("loaded_" + name)
        g["loaded"] = names
        g["norm_sems"] = {name: sem(name) for name in Norm.TOTALS}
        for name, n in (("w_loaded", SLOT_DEPTH), ("x_gathered", SLOT_DEPTH), ("y_stored", SLOT_DEPTH), ("y_gathered", GATHER_DEPTH)):
            g[name] = [sem(f"{name}{j}") for j in range(n)]
        g["xn_dram"] = nc.dram_tensor("xn_rows", (TOK, D), F32, kind="Internal").ap()
        g["y_dram"] = nc.dram_tensor("y_rows", (SLOTS * P, D), F32, kind="Internal").ap()

        with nc.Block() as block:
            @block.sync
            def _(sp):
                sp.dma_start(g["x"][:, :, :], a["x"].rearrange("(n p) d -> p n d", p=P)).then_inc(g["loaded_x"], 16)
                sp.dma_start(g["ident"][:, :], a["ident"]).then_inc(g["loaded_x"], 16)
                sp.dma_start(g["mask"][:, :, :], a["mask"]).then_inc(g["loaded_x"], 16)
                sp.wait_ge(g["loaded_x"], 48)

            @block.gpsimd
            def _(pool):
                pool.memset(g["halves"][:, :], -0.5)

        def load_weights(sp):
            for name in LOADS:
                whole = (slice(None),) * len(a[name].shape)
                sp.dma_start(g[name][whole], a[name][whole]).then_inc(names[name], 16)

        for n, phase in enumerate(PHASES):
            if phase in ("latent", "rotary"):
                attention(nc, g, str(n), n, phase == "latent", load_weights if n == 0 else None)
            else:
                experts(nc, g, a, str(n), n, PHASES[:n].count("experts"), n == len(PHASES) - 1)

        stored = sem("stored")
        with nc.Block() as block:
            @block.sync
            def _(sp):
                sp.dma_start(out.rearrange("(n p) d -> p n d", p=P), g["x"][:, :, :]).then_inc(stored, 16)
                sp.wait_ge(stored, 16)


PHASES = ["latent", "experts", "rotary", "experts"]
EARLY = 7
ALONE = 4
LIST_DEPTH = 4
LOADS = ["wkv_a", "rope_k", "wkT", "wq_nopeT", "kv_w", "rope_q", "wq_rope", "wvT", "wo_a", "gate", "se_up", "se_down",
         "count", "w_rot", "rope_b", "wo_b"]


class Norm:

    TOTALS = {"ln_stats_done": NT, "ln_mv_done": NT, "ln_var_done": 1, "ln_rstd_done": 1, "ln_xn_done": NT,
              "ln_turned": NT // 2}

    def __init__(self, ctx, nc, g, tag, before):
        sb = lambda name, shape: ctx.enter_context(nc.sbuf_tensor(name + tag, shape, F32))
        self.var = sb("ln_var", [P, NT])
        self.rstd = sb("ln_rstd", [P, NT])
        self.mv = sb("ln_mv", [P, NT, 2])
        self.stats = g["ln_stats"]
        self.sems = g["norm_sems"]
        self.before = before

    def sem(self, name):
        return self.sems["ln_" + name]

    def count(self, name, n):
        return self.before * self.TOTALS["ln_" + name] + n

    def sums(self, dve, g, t):
        one = slice(t, t + 1) if isinstance(t, int) else bass.ds(t, 1)
        dve.bn_stats(self.stats[:, one, :].rearrange("p a n -> p (a n)"),
                     g["x"][:, one, :].rearrange("p a d -> p (a d)")).then_inc(self.sem("stats_done"), 1)

    def vector(self, dve, g, meanwhile=None):
        if self.before == 0:
            dve.wait_ge(g["loaded_x"], 48)
            for t in range(NT):
                self.sums(dve, g, t)
        dve.wait_ge(self.sem("stats_done"), self.count("stats_done", NT))
        for t in range(NT):
            dve.bn_aggr(self.mv[:, t, :], self.stats[:, t, :]).then_inc(self.sem("mv_done"), 1)
        dve.wait_ge(self.sem("mv_done"), self.count("mv_done", NT))
        dve.tensor_scalar(self.var[:, :], self.mv[:, :, 1], LN_EPS, None, ALU.add).then_inc(self.sem("var_done"), 1)
        if meanwhile:
            meanwhile()
        dve.wait_ge(self.sem("rstd_done"), self.count("rstd_done", 1))
        for t in range(NT):
            dve.tensor_scalar(g["xn"][:, t, :], g["x"][:, t, :], self.mv[:, t, 0:1], self.rstd[:, t:t + 1],
                              ALU.subtract, ALU.mult).then_inc(self.sem("xn_done"), 1)

    def gpsimd(self, pool, g):
        pool.wait_ge(self.sem("var_done"), self.count("var_done", 1))
        pool.tensor_tensor(self.rstd[:, :], self.var[:, :], g["halves"][:, :], ALU.pow).then_inc(self.sem("rstd_done"), 1)

    def tensor(self, pe, g, banks):
        for m in range(NT // 2):
            pe.wait_ge(self.sem("xn_done"), self.count("xn_done", 2 * m + 2))
            for c in range(DC):
                for t in (2 * m, 2 * m + 1):
                    last = pe.transpose(banks[m][:, c * 256 + (t % 2) * P:c * 256 + (t % 2 + 1) * P],
                                        g["xn"][:, t, c * P:(c + 1) * P], g["ident"][:, :])
            last.then_inc(self.sem("turned"), 1)

    def scalar(self, act, g, banks, done):
        for m in range(NT // 2):
            act.wait_ge(self.sem("turned"), self.count("turned", m + 1))
            act.activation(g["xnT"][:, :, m * 256:(m + 1) * 256],
                           banks[m][:, :].rearrange("p (c n) -> p c n", c=DC), ACT.Copy).then_inc(done, 1)


def attention(nc, g, tag, before, latent, load_weights):
    VW = KVR if latent else 2 * HD
    SCALE = float(NOPE + ROPE) ** -0.5 if latent else float(HD) ** -0.5
    OC = HEADS * VW // P
    loaded = g["loaded"]

    if latent:
        FRONT = [[("Q", 0)], [("Q", 1)], [], [("T", 0), ("Q", 2)], [("T", 1), ("Q", 3)], [], [("T", 2)], [("T", 3)]]
    else:
        FRONT = [[("Q", 0)], [("Q", 1)], [], [("T", 0), ("T", 4), ("T", 1)], [], [("T", 2)], [("T", 3)], []]
    KEYS = ("T", 4)

    T_ORDER, Q_ORDER = [], []
    for p in range(PAIRS):
        T_ORDER.append(("P", p))
        for step in FRONT[p]:
            (T_ORDER if step[0] == "T" else Q_ORDER).append(step)
    Q_ORDER.append("out")
    T_FRONT = [f for f in T_ORDER if f[0] == "T"]
    Q_FRONT = [f for f in Q_ORDER if f[0] == "Q"]

    class Use:

        def __init__(self, kind, b, i, key, nxt):
            order, front = (T_ORDER, T_FRONT) if kind == "T" else (Q_ORDER, Q_FRONT)
            if not nxt:
                order = [k for k in order if k not in front]
            if b is None:
                v, b = front.index(key), 0
            else:
                v = len(front) + len(T_ORDER if kind == "T" else Q_ORDER) * i + order.index(key)
            banks = 2 if kind == "T" else 1
            uses = 2 * len(T_ORDER if kind == "T" else Q_ORDER)
            self.bank = v % banks
            self.before = b * (uses // banks) + v // banks
            self.first = v < banks
            self.written = b * uses + v + 1

    with ExitStack() as ctx:
        def sb(name, shape, dt=F32):
            return ctx.enter_context(nc.sbuf_tensor(name + tag, shape, dt))

        def sem(name):
            return g["sem"](name + tag)

        def psum(name, shape):
            return ctx.enter_context(nc.psum_tensor(name + tag, shape, F32))

        norm = Norm(ctx, nc, g, tag, before)
        next_norm = Norm(ctx, nc, g, tag + "n", before + 1)
        T = [psum(f"T{i}", [P, 512]) for i in range(2)]
        S = [psum(f"S{i}", [P, 512]) for i in range(4)]
        Q = [psum("Q0", [P, 512])]
        O = psum("O0", [P, 512])

        xs = sb("xs", [P, 2, DC, P])
        q = sb("q", [P, 2, HEADS, P])
        qT = sb("qT", [P, 2, HEADS, P])
        rot1 = sb("rot1", [P, 2, 8 * ROPE])
        rot2 = sb("rot2", [P, 2, 8 * ROPE])
        nmax = sb("nmax", [P, 2, HEADS])
        rsum = sb("rsum", [P, 2, HEADS])
        rinv = sb("rinv", [P, 2, HEADS])
        prob = sb("prob", [P, 4, 2, 2 * P])
        probT = sb("probT", [P, 2, 2, 2, 4, P])
        oT = sb("oT", [P, 2, OC, P])
        if latent:
            wqn = sb("wqn", [P, DC, HEADS * KVR])
            wvo = sb("wvo", [P, PAIRS, D])
            kvc = prob[:, 0:2, :, :].rearrange("p a j (t n) -> p (a j t) n", n=P)
            sq = rot1[:, 1, :].rearrange("p (t n) -> p t n", t=NT)
            ms = sb("ms", [P, NT])
            ms2 = sb("ms2", [P, NT])
            rr = sb("rr", [P, NT])
            kv = sb("kv", [P, NT, P])
            kT = sb("kT", [P, TOK])
            vals = sb("vals", [P, 2, KVR])
        else:
            kr = sb("kr", [P, D])
            kT = sb("kT", [P, 2, TOK])
            v = sb("v", [P, 2, D])
            vals = sb("vals", [P, 2, HEADS, VW])

        xnT_done = sem("xnT_done")
        staged = sem("staged")
        projected = sem("projected")
        q_read = [sem("q_read")]
        turned = sem("turned")
        t_read = [sem(f"t_read{i}") for i in range(2)]
        q_ready = sem("q_ready")
        kr_ready = sem("kr_ready")
        vals_ready = sem("vals_ready")
        vals_free = sem("vals_free")
        scored = sem("scored")
        max_done = sem("max_done")
        exp_done = sem("exp_done")
        recip = sem("recip")
        normed = sem("normed")
        summed = sem("summed")
        o_done = sem("o_done")
        pre_pe = sem("pre_pe")
        pre_act = sem("pre_act")
        pre_dve = sem("pre_dve")
        pre_pool = sem("pre_pool")
        WQN_USES = DC * HEADS * KVR // 512
        WVO_USES = PAIRS * D // 512
        START = 2

        def pair(b, i, p):
            return b * 2 * PAIRS + PAIRS * i + p + 1

        def half(b, i, m):
            return b * 4 + 2 * i + m + 1 + START

        def k_slice(b, i, gr):
            if latent:
                return kT[:, bass.ds(b * SEQ, (i + 1) * P)]
            return kT[:, gr, bass.ds(b * SEQ, (i + 1) * P)]

        def run(eng, slot):
            with eng.Fori(0, BATCH - 1) as b:
                slot(b, 0, True)
                slot(b, 1, True)
            slot(BATCH - 1, 0, True)
            slot(BATCH - 1, 1, False)

        def after(b, i):
            return (b, 1) if i == 0 else (b + 1, 0)

        with nc.Block() as block:
            @block.sync
            def _(sp):
                if load_weights:
                    load_weights(sp)

            @block.tensor
            def _(pe):
                pe.sem_inc(summed, START)
                pe.wait_ge(g["loaded_x"], 48)
                norm.tensor(pe, g, [T[0], T[1], S[0], S[1]])
                if latent:
                    pe.wait_ge(loaded["wkv_a"], 16)
                    for m in range(2):
                        pe.wait_ge(xnT_done, 2 * m + 2)
                        for t in range(4):
                            for c in range(DC):
                                last = pe.matmul((Q[0], O)[m][:, t * P:(t + 1) * P],
                                                 g["xnT"][:, c, (4 * m + t) * P:(4 * m + t + 1) * P],
                                                 g["wkv_a"][:, c, :], start=(c == 0), stop=(c == DC - 1))
                        last.then_inc(pre_pe, 1)
                    pe.wait_ge(loaded["wq_nopeT"], 16)
                    pe.wait_ge(loaded["wkT"], 16)
                    for n in range(WQN_USES):
                        if n >= 2:
                            pe.wait_ge(pre_act, n + 1)
                        for k in range(8):
                            h = 8 * (n % 2) + k
                            last = pe.matmul(S[2 + n % 2][:, k * KVR:(k + 1) * KVR],
                                             g["wq_nopeT"][:, h, (n // 2) * P:(n // 2 + 1) * P],
                                             g["wkT"][:, h, :], start=True, stop=True)
                        last.then_inc(pre_pe, 1)
                    pe.wait_ge(pre_act, 2 + WQN_USES)
                    pe.wait_ge(loaded["wq_rope"], 16)
                else:
                    pe.wait_ge(xnT_done, NT // 2)
                    pe.wait_ge(loaded["w_rot"], 16)
                    pe.wait_ge(loaded["wo_b"], 16)

                def turn_keys():
                    pe.wait_ge(pre_dve, 7)
                    for m in range(2):
                        for t in range(4):
                            last = pe.transpose(T[m][:, t * P:(t + 1) * P], kv[:, 4 * m + t, :], g["ident"][:, :])
                        last.then_inc(pre_pe, 1)
                    pe.wait_ge(pre_act, 2 + WQN_USES + 2)

                def values_output():
                    pe.wait_ge(loaded["wvT"], 16)
                    pe.wait_ge(loaded["wo_a"], 16)
                    pe.wait_ge(q_read[0], len(Q_FRONT))
                    for m in range(WVO_USES):
                        if m >= 2:
                            pe.wait_ge(pre_act, 2 + WQN_USES + 2 + m - 1)
                        for j in range(2):
                            for side in range(2):
                                h = 4 * m + 2 * j + side
                                last = pe.matmul((O, Q[0])[m % 2][side * KVR:(side + 1) * KVR, j * D:(j + 1) * D],
                                                 g["wvT"][:, h, :], g["wo_a"][:, h, :], start=True, stop=True)
                        last.then_inc(pre_pe, 1)
                    pe.wait_ge(pre_act, 2 + WQN_USES + 2 + WVO_USES)

                def project(b, i, n, nxt):
                    if latent:
                        w, cols, width = (wqn, g["wq_rope"])[n % 2], 512 * (n // 2), 512
                    else:
                        w, cols, width = g["w_rot"], 512 * n, (512, 256)[n]
                    use = Use("Q", b, i, ("Q", n), nxt)
                    tile = 0 if b is None else 2 * b + i + 1
                    side = 0 if b is None else (i + 1) % 2
                    pe.wait_ge(staged, tile + 1)
                    if not use.first:
                        pe.wait_ge(q_read[use.bank], use.before)
                    for c in range(DC):
                        last = pe.matmul(Q[use.bank][:, 0:width], xs[:, side, c, :], w[:, c, cols:cols + width],
                                         start=(c == 0), stop=(c == DC - 1))
                    last.then_inc(projected, 1)

                def turn_front(b, i, n, nxt):
                    use = Use("T", b, i, ("T", n), nxt)
                    tile = 0 if b is None else 2 * b + i + 1
                    side = 0 if b is None else (i + 1) % 2
                    if not use.first:
                        pe.wait_ge(t_read[use.bank], use.before)
                    if ("T", n) == KEYS:
                        pe.wait_ge(kr_ready, tile + 1)
                        for k in range(2):
                            last = pe.transpose(T[use.bank][:, k * P:(k + 1) * P], kr[:, k * P:(k + 1) * P],
                                                g["ident"][:, :])
                    else:
                        if latent:
                            at = Use("Q", b, i, ("Q", 2 * (n // 2)), nxt)
                            pe.wait_ge(q_read[at.bank], at.before + 1)
                        pe.wait_ge(q_ready, tile * 2 + n // 2 + 1)
                        for k in range(4):
                            last = pe.transpose(T[use.bank][:, k * P:(k + 1) * P], q[:, side, 4 * n + k, :],
                                                g["ident"][:, :])
                    last.then_inc(turned, 1)

                def scores(b, i, p):
                    if not (isinstance(b, int) and b == i == 0 and p < 4):
                        pe.wait_ge(exp_done, pair(b, i, p) - 4)
                    w = (i + 1) * P
                    for j in range(2):
                        h = 2 * p + j
                        to = S[p % 4][:, j * 256:j * 256 + w]
                        pe.matmul(to, qT[:, i, h, :], k_slice(b, i, h // 8), start=True, stop=True)
                        last = pe.matmul(S[p % 4][:, j * 256 + i * P:j * 256 + w], g["mask"][:, 0, :],
                                         g["mask"][:, 1, :], start=False, stop=True, skip_group_check=True)
                    last.then_inc(scored, 1)

                def next_scores(b, i, p, nxt):
                    for key in {0: (("T", 0), KEYS), 2: (("T", 1),)}.get(p, ()):
                        if key in T_FRONT:
                            use = Use("T", b, i, key, nxt)
                            pe.wait_ge(t_read[use.bank], use.before + 1)
                    scores(*after(b, i), p)

                def turn_probs(b, i, p, nxt):
                    use = Use("T", b, i, ("P", p), nxt)
                    pe.wait_ge(normed, pair(b, i, p))
                    pe.wait_ge(t_read[use.bank], use.before)
                    for j in range(2):
                        for kb in range(i + 1):
                            at = (j * (i + 1) + kb) * P
                            last = pe.transpose(T[use.bank][:, at:at + P], prob[:, p % 4, j, kb * P:(kb + 1) * P],
                                                g["ident"][:, :])
                    last.then_inc(turned, 1)

                def values(b, i, m, nxt):
                    use = Use("T", b, i, ("P", 4 * m + 3), nxt)
                    pe.wait_ge(t_read[use.bank], use.before + 1)
                    pe.wait_ge(vals_ready, 2 * b + i + 1)
                    pe.wait_ge(o_done, half(b, i, m) - 1)
                    if latent:
                        for j in range(2):
                            for kb in range(i + 1):
                                last = pe.matmul(O[j * VW:(j + 1) * VW, :], vals[:, kb, :],
                                                 probT[:, m, j, kb, :, :], start=(kb == 0), stop=(kb == i))
                    else:
                        for s in range(4):
                            for j in range(2):
                                h = 8 * m + 2 * s + j
                                for kb in range(i + 1):
                                    last = pe.matmul(O[(h % 4) * VW:(h % 4 + 1) * VW, (s // 2) * P:(s // 2 + 1) * P],
                                                     vals[:, kb, h, :], probT[:, m, j, kb, s, :],
                                                     start=(kb == 0), stop=(kb == i))
                    last.then_inc(summed, 1)

                def output(b, i, nxt):
                    use = Use("Q", b, i, "out", nxt)
                    pe.wait_ge(q_read[use.bank], use.before)
                    pe.wait_ge(o_done, half(b, i, 1))
                    w = wvo if latent else g["wo_b"]
                    for c in range(OC):
                        last = pe.matmul(Q[use.bank][:, 0:D], oT[:, i, c, :], w[:, c, :],
                                         start=(c == 0), stop=(c == OC - 1))
                    last.then_inc(projected, 1)

                def front(b, i, step, nxt):
                    if step[0] == "Q":
                        project(b, i, step[1], nxt)
                    else:
                        turn_front(b, i, step[1], nxt)

                def slot(b, i, nxt):
                    for p in range(PAIRS):
                        turn_probs(b, i, p, nxt)
                        if p < PAIRS - 4:
                            scores(b, i, p + 4)
                        elif nxt:
                            next_scores(b, i, p - 4, nxt)
                        if p == PAIRS - 1:
                            values(b, i, 1, nxt)
                        if nxt:
                            for step in FRONT[p]:
                                front(b, i, step, nxt)
                        if p == 4:
                            values(b, i, 0, nxt)
                    output(b, i, nxt)

                for k, step in enumerate(sum(FRONT, [])):
                    if latent and k == 2:
                        turn_keys()
                    front(None, 0, step, True)
                for k in range(2):
                    pe.wait_ge(t_read[k], len(T_FRONT[k::2]))
                for p in range(4):
                    scores(0, 0, p)
                if latent:
                    values_output()
                run(pe, slot)

            @block.scalar
            def _(act):
                act.sem_inc(o_done, START)
                norm.scalar(act, g, [T[0], T[1], S[0], S[1]], xnT_done)
                if latent:
                    for m in range(2):
                        act.wait_ge(pre_pe, m + 1)
                        act.activation(kvc[:, 4 * m:4 * m + 4, :], (Q[0], O)[m][:, :].rearrange("p (t n) -> p t n", t=4),
                                       ACT.Copy).then_inc(pre_act, 1)
                    for n in range(WQN_USES):
                        act.wait_ge(pre_pe, 2 + n + 1)
                        act.activation(wqn[:, n // 2, (n % 2) * 512:(n % 2 + 1) * 512], S[2 + n % 2][:, :],
                                       ACT.Copy).then_inc(pre_act, 1)

                def copy_keys():
                    for m in range(2):
                        act.wait_ge(pre_pe, 2 + WQN_USES + m + 1)
                        act.activation(kT[:, m * 512:(m + 1) * 512], T[m][:, :], ACT.Copy).then_inc(pre_act, 1)

                def copy_values_output():
                    for m in range(WVO_USES):
                        act.wait_ge(pre_pe, 2 + WQN_USES + 2 + m + 1)
                        act.activation(wvo[:, 2 * m:2 * m + 2, :],
                                       (O, Q[0])[m % 2][:, :].rearrange("p (j d) -> p j d", j=2),
                                       ACT.Copy).then_inc(pre_act, 1)

                def copy_front(b, i, step, nxt):
                    side = 0 if b is None else (i + 1) % 2
                    if latent and step in (("Q", 0), ("Q", 2)):
                        use, h = Use("Q", b, i, step, nxt), 4 * step[1]
                        act.wait_ge(projected, use.written)
                        act.activation(q[:, side, h:h + 8, 0:KVR],
                                       Q[use.bank][:, :].rearrange("p (h n) -> p h n", h=8),
                                       ACT.Copy, scale=SCALE).then_inc(q_read[use.bank], 1)
                    elif not latent and step == ("Q", 1):
                        use = Use("Q", b, i, step, nxt)
                        act.wait_ge(projected, use.written)
                        act.activation(v[:, side, :], Q[use.bank][:, 0:D], ACT.Copy).then_inc(q_read[use.bank], 1)
                    elif step[0] == "T" and step != KEYS:
                        use, gr = Use("T", b, i, step, nxt), step[1]
                        act.wait_ge(turned, use.written)
                        act.activation(qT[:, side, 4 * gr:4 * gr + 4, :],
                                       T[use.bank][:, :].rearrange("p (h n) -> p h n", h=4),
                                       ACT.Copy).then_inc(t_read[use.bank], 1)

                def softmax(b, i, p, nxt):
                    if b is None:
                        b, i = 0, 0
                    elif p >= 4:
                        act.wait_ge(turned, Use("T", b, i, ("P", p - 4), nxt).written)
                    elif i == 1:
                        act.wait_ge(turned, Use("T", b, 0, ("P", p + PAIRS - 4), True).written)
                    else:
                        act.wait_ge(turned, Use("T", b - 1, 1, ("P", p + PAIRS - 4), True).written)
                    if p >= PAIRS:
                        (b, i), p = after(b, i), p - PAIRS
                    act.wait_ge(max_done, pair(b, i, p))
                    w = (i + 1) * P
                    for j in range(2):
                        h = 2 * p + j
                        last = act.activation(prob[:, p % 4, j, 0:w], S[p % 4][:, j * 256:j * 256 + w], ACT.Exp,
                                              bias=nmax[:, i, h:h + 1], scale=1.0, accum_out=rsum[:, i, h:h + 1])
                    last.then_inc(exp_done, 1)

                def outputs(b, i, m):
                    act.wait_ge(summed, half(b, i, m))
                    n = OC // 2
                    act.activation(oT[:, i, n * m:n * (m + 1), :],
                                   O[:, 0:n * P].rearrange("p (c n) -> p c n", c=n), ACT.Copy).then_inc(o_done, 1)

                def slot(b, i, nxt):
                    for p in range(PAIRS):
                        if p + 3 < PAIRS or nxt:
                            softmax(b, i, p + 3, nxt)
                        if nxt:
                            for step in FRONT[p]:
                                copy_front(b, i, step, nxt)
                        if p == 4:
                            outputs(b, i, 0)
                    outputs(b, i, 1)

                for k, step in enumerate(sum(FRONT, [])):
                    if latent and k == 2:
                        copy_keys()
                    copy_front(None, 0, step, True)
                for p in range(3):
                    softmax(None, 0, p, True)
                if latent:
                    copy_values_output()
                run(act, slot)

            @block.gpsimd
            def _(pool):
                if not latent:
                    pool.memset(vals[:, :, :, :], 0.0).then_inc(pre_pool, 1)
                    pool.wait_ge(pre_pool, 1)
                norm.gpsimd(pool, g)
                for i in range(2):
                    pool.wait_ge(xnT_done, 1)
                    pool.tensor_copy(xs[:, i, :, :], g["xnT"][:, :, i * P:(i + 1) * P]).then_inc(staged, 1)
                if latent:
                    pool.wait_ge(pre_dve, 3)
                    pool.tensor_tensor(rr[:, :], ms2[:, :], g["halves"][:, :], ALU.pow).then_inc(pre_pool, 1)
                pool.wait_ge(xnT_done, NT // 2)

                def normalise(b, i, p):
                    pool.wait_ge(recip, pair(b, i, p))
                    w = (i + 1) * P
                    pool.tensor_tensor(prob[:, p % 4, :, 0:w], prob[:, p % 4, :, 0:w],
                                       rinv[:, i, 2 * p:2 * p + 2].unsqueeze(2).broadcast_to([P, 2, w]),
                                       ALU.mult).then_inc(normed, 1)

                def slot(b, i, nxt):
                    more = not isinstance(b, int)
                    for p in range(PAIRS):
                        if p + 1 < PAIRS:
                            normalise(b, i, p + 1)
                        elif nxt:
                            normalise(*after(b, i), 0)
                        if p == 2:
                            pool.wait_ge(summed, half(b, i, 0) - 1)
                            pool.sem_inc(vals_free, 1)
                            if latent:
                                src = kv[:, bass.ds(2 * b + i, 1), 0:KVR].rearrange("p a n -> p (a n)")
                                pool.tensor_copy(vals[:, i, :], src).then_inc(vals_ready, 1)
                            else:
                                pool.tensor_copy(vals[:, i, :, 0:HD],
                                                 v[:, i, :].rearrange("p (h n) -> p h n", h=HEADS)).then_inc(vals_ready, 1)
                        if p == 5 and more:
                            pool.tensor_copy(xs[:, i, :, :],
                                             g["xnT"][:, :, bass.ds(b * SEQ + SEQ + i * P, P)]).then_inc(staged, 1)

                normalise(0, 0, 0)
                run(pool, slot)

            @block.vector
            def _(dve):
                step_n = 0 if latent else 1

                def own(ins):
                    nonlocal step_n
                    ins.then_inc(pre_dve, 1)
                    step_n += 1
                    dve.wait_ge(pre_dve, step_n)

                if latent:
                    norm.vector(dve, g)
                else:
                    norm.vector(dve, g, lambda: dve.memset(q[:, 0, :, :], 0.0).then_inc(pre_dve, 1))
                    own(dve.memset(q[:, 1, :, :], 0.0))
                if latent:
                    dve.wait_ge(pre_act, 2)
                    own(dve.tensor_tensor(sq, kvc[:, :, 0:KVR], kvc[:, :, 0:KVR], ALU.mult))
                    own(dve.tensor_reduce(ms[:, :], sq, AX, ALU.add))
                    own(dve.tensor_scalar(ms2[:, :], ms[:, :], 1.0 / KVR, RMS_EPS, ALU.mult, ALU.add))
                    dve.wait_ge(loaded["rope_k"], 16)
                    raw = kvc[:, :, KVR:P].rearrange("p (b i) n -> p b i n", i=2)
                    r1 = rot1[:, 0, :].rearrange("p (b i n) -> p b i n", b=BATCH, i=2)
                    r2 = rot2[:, 0, :].rearrange("p (b i n) -> p b i n", b=BATCH, i=2)
                    H = ROPE // 2
                    for i in range(2):
                        cos, sin = (g["rope_k"][:, i, s, :].unsqueeze(1) for s in range(2))
                        dve.tensor_tensor(r1[:, :, i, :], raw[:, :, i, :], cos.broadcast_to([P, BATCH, ROPE]), ALU.mult)
                        for lo, hi in ((0, H), (H, 0)):
                            last = dve.tensor_tensor(r2[:, :, i, lo:lo + H], raw[:, :, i, hi:hi + H],
                                                     sin[:, :, lo:lo + H].broadcast_to([P, BATCH, H]), ALU.mult)
                    own(last)
                    own(dve.tensor_tensor(kv[:, :, KVR:P], rot1[:, 0, :].rearrange("p (t n) -> p t n", t=NT),
                                          rot2[:, 0, :].rearrange("p (t n) -> p t n", t=NT), ALU.add))
                    dve.wait_ge(pre_pool, 1)
                    dve.wait_ge(loaded["kv_w"], 16)
                    own(dve.tensor_tensor(sq, kvc[:, :, 0:KVR],
                                          rr[:, :].unsqueeze(2).broadcast_to([P, NT, KVR]), ALU.mult))
                    own(dve.tensor_tensor(kv[:, :, 0:KVR], sq,
                                          g["kv_w"][:, :].unsqueeze(1).broadcast_to([P, NT, KVR]), ALU.mult))
                    dve.wait_ge(loaded["rope_q"], 16)
                else:
                    dve.wait_ge(loaded["rope_b"], 16)

                def rotate_latent(b, i, step, nxt):
                    use, k = Use("Q", b, i, step, nxt), step[1] // 2
                    side = 0 if b is None else (i + 1) % 2
                    dve.wait_ge(projected, use.written)
                    src = Q[use.bank][:, :].rearrange("p (h n) -> p h n", h=8)
                    r1 = rot1[:, k, :].rearrange("p (h n) -> p h n", h=8)
                    r2 = rot2[:, k, :].rearrange("p (h n) -> p h n", h=8)
                    cos, sin = (g["rope_q"][:, side, s, :].unsqueeze(1) for s in range(2))
                    H = ROPE // 2
                    dve.tensor_tensor(r1, src, cos.broadcast_to([P, 8, ROPE]), ALU.mult)
                    for lo, hi in ((0, H), (H, 0)):
                        last = dve.tensor_tensor(r2[:, :, lo:lo + H], src[:, :, hi:hi + H],
                                                 sin[:, :, lo:lo + H].broadcast_to([P, 8, H]), ALU.mult)
                    last.then_inc(q_read[use.bank], 1)
                    dve.wait_ge(q_read[use.bank], use.before + 1)
                    dve.tensor_tensor(q[:, side, 8 * k:8 * k + 8, KVR:P], r1, r2, ALU.add).then_inc(q_ready, 1)

                def rotate_all(b, i, step, nxt):
                    use = Use("Q", b, i, step, nxt)
                    side = 0 if b is None else (i + 1) % 2
                    dve.wait_ge(projected, use.written)
                    src = Q[use.bank][:, :].rearrange("p (s h n) -> p s h n", s=2, h=HEADS)
                    r1 = rot1[:, 0, :].rearrange("p (s h n) -> p s h n", s=2, h=HEADS)
                    r2 = rot2[:, 0, :].rearrange("p (s h n) -> p s h n", s=2, h=HEADS)
                    H = HD // 2
                    for s in range(2):
                        cos, sin = (g["rope_b"][:, side, s, f, :].unsqueeze(1) for f in range(2))
                        dve.tensor_tensor(r1[:, s], src[:, s], cos.broadcast_to([P, HEADS, HD]), ALU.mult)
                        for lo, hi in ((0, H), (H, 0)):
                            last = dve.tensor_tensor(r2[:, s, :, lo:lo + H], src[:, s, :, hi:hi + H],
                                                     sin[:, :, lo:lo + H].broadcast_to([P, HEADS, H]), ALU.mult)
                    last.then_inc(q_read[use.bank], 1)
                    dve.wait_ge(q_read[use.bank], use.before + 1)
                    for k in range(2):
                        start = (side * HEADS + 8 * k) * P
                        diagonal = bass.AP(q, start, [[2 * HEADS * P, P], [P + HD, 8], [1, HD]])
                        at = slice(k * P, (k + 1) * P)
                        dve.tensor_tensor(diagonal, rot1[:, 0, at].rearrange("p (h n) -> p h n", h=8),
                                          rot2[:, 0, at].rearrange("p (h n) -> p h n", h=8),
                                          ALU.add).then_inc(q_ready, 1)
                    dve.tensor_tensor(kr[:, :], rot1[:, 0, D:2 * D], rot2[:, 0, D:2 * D], ALU.add).then_inc(kr_ready, 1)

                def keys(b, i, step, nxt):
                    use = Use("T", b, i, step, nxt)
                    tile = 0 if b is None else 2 * b + i + 1
                    dve.wait_ge(turned, use.written)
                    dve.tensor_copy(kT[:, :, bass.ds(tile * P, P)],
                                    T[use.bank][:, 0:2 * P].rearrange("p (k n) -> p k n", k=2)).then_inc(t_read[use.bank], 1)

                def front(b, i, step, nxt):
                    if latent and step in (("Q", 1), ("Q", 3)):
                        rotate_latent(b, i, step, nxt)
                    elif not latent and step == ("Q", 0):
                        rotate_all(b, i, step, nxt)
                    elif step == KEYS:
                        keys(b, i, step, nxt)

                def maxima(b, i, p):
                    dve.wait_ge(scored, pair(b, i, p))
                    dve.tensor_reduce(nmax[:, i, 2 * p:2 * p + 2],
                                      S[p % 4][:, :].rearrange("p (j n) -> p j n", j=2)[:, :, 0:(i + 1) * P],
                                      AX, ALU.max, negate=True).then_inc(max_done, 1)

                def invert(b, i, p):
                    dve.wait_ge(exp_done, pair(b, i, p))
                    dve.reciprocal(rinv[:, i, 2 * p:2 * p + 2], rsum[:, i, 2 * p:2 * p + 2]).then_inc(recip, 1)

                def probs(b, i, p, nxt):
                    use, m = Use("T", b, i, ("P", p), nxt), p // 4
                    dve.wait_ge(turned, use.written)
                    if p % 4 == 0:
                        dve.wait_ge(summed, half(b, i, m) - 2)
                    w = 2 * (i + 1) * P
                    dve.tensor_copy(probT[:, m, :, 0:i + 1, p % 4, :],
                                    T[use.bank][:, 0:w].rearrange("p (j k n) -> p j k n", j=2, k=i + 1),
                                    ).then_inc(t_read[use.bank], 1)

                def add(b, i, nxt):
                    use = Use("Q", b, i, "out", nxt)
                    dve.wait_ge(projected, use.written)
                    x = g["x"][:, bass.ds(b * 2 + i, 1), :].rearrange("p a d -> p (a d)")
                    dve.tensor_tensor(x, Q[use.bank][:, 0:D], x, ALU.add).then_inc(q_read[use.bank], 1)
                    dve.wait_ge(q_read[use.bank], use.before + 1)
                    next_norm.sums(dve, g, b * 2 + i)

                def slot(b, i, nxt):
                    for p in range(PAIRS):
                        if p + 2 < PAIRS:
                            invert(b, i, p + 2)
                        elif nxt:
                            invert(*after(b, i), p + 2 - PAIRS)
                        probs(b, i, p, nxt)
                        if p + 4 < PAIRS:
                            maxima(b, i, p + 4)
                        elif nxt:
                            maxima(*after(b, i), p + 4 - PAIRS)
                        if nxt:
                            for step in FRONT[p]:
                                front(b, i, step, nxt)
                    add(b, i, nxt)

                for step in sum(FRONT, []):
                    front(None, 0, step, True)
                for p in range(4):
                    maxima(0, 0, p)
                for p in range(2):
                    invert(0, 0, p)
                run(dve, slot)


def experts(nc, g, a, tag, before, run, final):
    with ExitStack() as ctx:
        def sb(name, shape, dt=F32):
            return ctx.enter_context(nc.sbuf_tensor(name + tag, shape, dt))

        def sem(name):
            return g["sem"](name + tag)

        E, K = EXPERTS, TOP
        bank = [ctx.enter_context(nc.psum_tensor(f"bank{i}" + tag, [P, 512], F32)) for i in range(8)]
        norm = Norm(ctx, nc, g, tag, before)
        loaded = g["loaded"]
        ids = sb("ids", [P, SLOTS], U32)
        wts = sb("wts", [P, SLOTS])
        row = sb("row", [1, P], U32)
        place = sb("place", [P, NT * K], I32)
        small = sb("small", [P, 6, NT])
        sg = sb("sg", [P, 2, 512])
        up = sb("up", [P, 2, 512])
        shT = sb("shT", [P, SHARED_CHUNKS, TOK])
        w13 = sb("w13", [P, SLOT_DEPTH, DC, 2 * INTER])
        w2 = sb("w2", [IC, SLOT_DEPTH, 2, D])
        w_loaded = g["w_loaded"]
        gu = sem("gu")
        gu_read = sem("gu_read")
        sh_done = sem("sh_done")
        shared = sem("shared")

        def up_bank(n):
            return 0 if n == EARLY + 1 else 4 + 2 * (n % 2)

        def shared_up(pe, n):
            ch, half = n // 2, n % 2
            if n >= 2:
                pe.wait_ge(gu_read, 2 * (n - 1))
            for s in range(2):
                for c in range(DC):
                    col = (s * SHARED_CHUNKS + ch) * P
                    last = pe.matmul(bank[up_bank(n) + s][:, :], g["se_up"][:, c, col:col + P],
                                     g["xnT"][:, c, half * 512:(half + 1) * 512],
                                     start=(c == 0), stop=(c == DC - 1))
            last.then_inc(gu, 1)

        def shared_silu(act, n):
            act.wait_ge(gu, n + 1)
            if n >= 2:
                act.wait_ge(sh_done, n - 1)
            act.activation(sg[:, n % 2, :], bank[up_bank(n)][:, :], ACT.Silu).then_inc(gu_read, 1)
            act.activation(up[:, n % 2, :], bank[up_bank(n) + 1][:, :], ACT.Copy).then_inc(gu_read, 1)

        def shared_h(eng, n):
            eng.wait_ge(gu_read, 2 * n + 2)
            eng.tensor_tensor(shT[:, n // 2, (n % 2) * 512:(n % 2 + 1) * 512], sg[:, n % 2, :],
                              up[:, n % 2, :], ALU.mult).then_inc(sh_done, 1)

        def load_expert(sp, j, s):
            e = sp.value_load(row[0:1, bass.ds(s, 1)], min_val=0, max_val=EXPERTS - 1)
            sp.dma_start(w13[:, j, :, :], a["w13"][bass.ds(e, 1)].rearrange("a p c n -> p (a c) n")).then_inc(w_loaded[j], 16)
            sp.dma_start(w2[:, j, :, :], a["w2"][bass.ds(e, 1)].rearrange("a p c n -> p (a c) n")).then_inc(w_loaded[j], 16)


        count = g["count"]
        iota, tri, ones = (count[:, n * P:(n + 1) * P] for n in range(3))
        full = count[:, 3 * P:3 * P + 8]
        tokens = count[:, 3 * P + 8:3 * P + 16]
        index = iota_p = count[:, 3 * P + 16:3 * P + 17]

        with ExitStack() as inner:
            def sb(name, shape, dt=F32):
                return inner.enter_context(nc.sbuf_tensor(name + tag, shape, dt))

            lg = sb("lg", [P, NT, E + 1])
            lgs = sb("lgs", [P, NT, E])
            pr = sb("pr", [P, NT, E])
            top = sb("top", [P, NT, 8])
            best = sb("best", [P, NT, 8], U32)
            bestf = sb("bestf", [P, NT * K])
            onehot = sb("onehot", [P, NT * K, E])
            chosen = sb("chosen", [P, NT, E], BF16)
            tri_ones = sb("tri_ones", [P, 2, P], BF16)
            pos = sb("pos", [P, NT, E])
            over = sb("over", [P, E, 8])
            tiles = sb("tiles", [P, E])
            cum = sb("cum", [P, E])
            begin = sb("begin", [P, E])
            junk = sb("junk", [P, E])
            slot_expert = sb("slot_expert", [P, 2])
            placef = sb("placef", [P, NT * K])
            part = sb("part", [P, 2, NT * K], I32)
            partf = sb("partf", [P, 2, NT * K])
            in_row = sb("in_row", [P, LIST_DEPTH, K, P])
            in_slot = sb("in_slot", [P, LIST_DEPTH, 3, K, SLOTS])
            xnT_done = sem("xnT_done")
            stored = sem("xn_stored")
            logits = sem("logits")
            lg_done = sem("lg_done")
            chain = sem("chain")
            ex_done = sem("ex_done")
            chosen_ready = sem("chosen_ready")
            counted = sem("counted")
            expert_ready = sem("expert_ready")
            expert_turned = sem("expert_turned")
            in_ready = sem("in_ready")
            listed = sem("listed")
            row_ready = sem("row_ready")
            in_slot_ready = sem("in_slot_ready")
            weight_ready = sem("weight_ready")

            with nc.Block() as block:
                @block.sync
                def _(sp):
                    sp.wait_ge(norm.sem("xn_done"), norm.count("xn_done", NT))
                    sp.dma_start(g["xn_dram"].rearrange("(n p) d -> p n d", p=P), g["xn"][:, :, :]).then_inc(stored, 16)
                    sp.wait_ge(row_ready, 1)
                    for j in range(SLOT_DEPTH):
                        load_expert(sp, j, j)
                    sp.wait_ge(stored, 16)

                @block.gpsimd
                def _(pool):
                    norm.gpsimd(pool, g)
                    for n in range(ALONE):
                        shared_h(pool, n)
                    for t in range(NT):
                        if ALONE + t < EARLY:
                            shared_h(pool, ALONE + t)
                        pool.wait_ge(in_slot_ready, t + 1)
                        pool.tensor_tensor(in_slot[:, t % LIST_DEPTH, 2], in_slot[:, t % LIST_DEPTH, 0],
                                           top[:, t, 0:K].unsqueeze(2).broadcast_to([P, K, SLOTS]),
                                           ALU.mult).then_inc(weight_ready, 1)

                @block.tensor
                def _(pe):
                    pe.wait_ge(g["loaded_x"], 48)
                    norm.tensor(pe, g, bank[0:4])
                    pe.wait_ge(xnT_done, NT // 2)
                    pe.wait_ge(loaded["gate"], 16)
                    for t in range(NT):
                        for c in range(DC):
                            last = pe.matmul(bank[0][:, t * (E + 1):(t + 1) * (E + 1)],
                                             g["xnT"][:, c, t * P:(t + 1) * P], g["gate"][:, c, :],
                                             start=(c == 0), stop=(c == DC - 1))
                    last.then_inc(logits, 1)

                    pe.wait_ge(loaded["se_up"], 16)
                    pe.wait_ge(loaded["count"], 16)
                    for n in range(3):
                        shared_up(pe, n)
                    pe.wait_ge(chosen_ready, 1)
                    pe.matmul(bank[1][:, 0:NT * E], tri_ones[:, 0, :], chosen[:, :, :], start=True, stop=True)
                    for k in range(1, NT):
                        pe.matmul(bank[1][:, k * E:NT * E], tri_ones[:, 1, :], chosen[:, 0:NT - k, :],
                                  start=False, stop=True, skip_group_check=True)
                    for t in range(NT):
                        last = pe.matmul(bank[2][:, 0:E], tri_ones[:, 1, :], chosen[:, t, :],
                                         start=(t == 0), stop=(t == NT - 1))
                    last.then_inc(counted, 1)
                    for n in range(3, EARLY):
                        if n == EARLY - 2:
                            pe.wait_ge(expert_ready, 1)
                            pe.matmul(bank[0][0:1, 0:P], slot_expert[:, 1:2], g["ident"][:, :],
                                      start=True, stop=True).then_inc(expert_turned, 1)
                        shared_up(pe, n)
                    for t in range(NT):
                        pe.wait_ge(weight_ready, t + 1)
                        pe.wait_ge(in_ready, t + 1)
                        for k in range(K):
                            last = pe.matmul(bank[3][:, 0:2 * SLOTS].rearrange("p (v s) -> p v s", v=2),
                                             in_row[:, t % LIST_DEPTH, k, :], in_slot[:, t % LIST_DEPTH, 1:3, k, :],
                                             start=(t == 0 and k == 0), stop=(t == NT - 1 and k == K - 1))
                        last.then_inc(listed, 1)

                @block.scalar
                def _(act):
                    norm.scalar(act, g, bank[0:4], xnT_done)
                    act.wait_ge(logits, 1)
                    act.activation(lg[:, :, :], bank[0][:, 0:NT * (E + 1)].rearrange("p (t e) -> p t e", t=NT),
                                   ACT.Copy).then_inc(lg_done, 1)
                    act.wait_ge(chain, 3)
                    act.activation(pr[:, :, :], lgs[:, :, :], ACT.Exp).then_inc(ex_done, 1)
                    act.activation(small[:, 3, :], lg[:, :, E], ACT.Exp, scale=-1.0).then_inc(ex_done, 1)
                    for n in range(ALONE):
                        shared_silu(act, n)
                    for t in range(NT):
                        if ALONE + t < EARLY:
                            shared_silu(act, ALONE + t)
                        act.wait_ge(in_slot_ready, t + 1)
                        act.activation(in_slot[:, t % LIST_DEPTH, 1], in_slot[:, t % LIST_DEPTH, 0], ACT.Copy,
                                       scale=tokens[:, t:t + 1]).then_inc(in_ready, 1)

                @block.vector
                def _(dve):
                    norm.vector(dve, g)
                    step = 0

                    def own(ins):
                        nonlocal step
                        ins.then_inc(chain, 1)
                        step += 1
                        dve.wait_ge(chain, step)

                    def over_experts(ap):
                        return ap.unsqueeze(2).broadcast_to([P, NT, E])

                    dve.wait_ge(loaded["count"], 16)
                    own(dve.tensor_copy(tri_ones[:, :, :], count[:, P:3 * P].rearrange("p (a n) -> p a n", a=2)))
                    dve.wait_ge(lg_done, 1)
                    own(dve.tensor_reduce(small[:, 0, :], lg[:, :, 0:E], AX, ALU.max, negate=True))
                    own(dve.tensor_tensor(lgs[:, :, :], lg[:, :, 0:E], over_experts(small[:, 0, :]), ALU.add))
                    dve.wait_ge(ex_done, 2)
                    own(dve.tensor_reduce(small[:, 1, :], pr[:, :, :], AX, ALU.add))
                    own(dve.reciprocal(small[:, 2, :], small[:, 1, :]))
                    own(dve.tensor_tensor(lgs[:, :, :], pr[:, :, :], over_experts(small[:, 2, :]), ALU.mult))
                    own(dve.tensor_scalar(small[:, 4, :], small[:, 3, :], 1.0, None, ALU.add))
                    dve.reciprocal(small[:, 5, :], small[:, 4, :])
                    for t in range(NT):
                        last = dve.max(top[:, t, :], lgs[:, t, :])
                    own(last)
                    for t in range(NT):
                        last = dve.max_index(best[:, t, :], top[:, t, :], lgs[:, t, :])
                    own(last)
                    own(dve.tensor_copy(bestf[:, :].rearrange("p (t k) -> p t k", t=NT), best[:, :, 0:K]))
                    own(dve.tensor_tensor(onehot[:, :, :], iota[:, 0:E].unsqueeze(1).broadcast_to([P, NT * K, E]),
                                          bestf[:, :].unsqueeze(2).broadcast_to([P, NT * K, E]), ALU.is_equal))
                    with nc.allow_low_precision(reason="a sum of 0 and 1"):
                        dve.tensor_reduce(chosen[:, :, :], onehot[:, :, :].rearrange("p (t k) e -> p t e k", t=NT),
                                          AX, ALU.add).then_inc(chosen_ready, 1)
                    dve.wait_ge(counted, 1)
                    own(dve.tensor_tensor(over[:, :, :], bank[2][:, 0:E].unsqueeze(2).broadcast_to([P, E, 8]),
                                          full.unsqueeze(1).broadcast_to([P, E, 8]), ALU.is_gt))
                    own(dve.tensor_reduce(tiles[:, :], over[:, :, :], AX, ALU.add))
                    own(dve.tensor_tensor_scan(cum[:, :], ones[:, 0:E], tiles[:, :], 0.0, ALU.mult, ALU.add))
                    own(dve.tensor_tensor(begin[:, :], cum[:, :], tiles[:, :], ALU.subtract))
                    own(dve.tensor_scalar(junk[:, :], cum[:, :], index, 0.0, ALU.is_le, ALU.add,
                                          accum_out=slot_expert[:, 0:1]))
                    dve.tensor_scalar(slot_expert[:, 1:2], slot_expert[:, 0:1], float(E - 1), None,
                                      ALU.min).then_inc(expert_ready, 1)
                    own(dve.scalar_tensor_tensor(pos[:, :, :], begin[:, :].unsqueeze(1).broadcast_to([P, NT, E]),
                                                 float(P), bank[1][:, 0:NT * E].rearrange("p (t e) -> p t e", t=NT),
                                                 ALU.mult, ALU.add))
                    own(dve.tensor_tensor(onehot[:, :, :].rearrange("p (t k) e -> p t k e", t=NT),
                                          onehot[:, :, :].rearrange("p (t k) e -> p t k e", t=NT),
                                          pos[:, :, :].unsqueeze(2).broadcast_to([P, NT, K, E]), ALU.mult))
                    own(dve.tensor_reduce(placef[:, :], onehot[:, :, :], AX, ALU.add))
                    dve.wait_ge(expert_turned, 1)
                    dve.tensor_copy(row[:, :], bank[0][0:1, 0:P]).then_inc(row_ready, 1)
                    own(dve.tensor_copy(place[:, :], placef[:, :]))
                    dve.tensor_scalar(part[:, 0, :], place[:, :], P - 1, None, ALU.bitwise_and)
                    own(dve.tensor_scalar(part[:, 1, :], place[:, :], 7, None, ALU.logical_shift_right))
                    own(dve.tensor_copy(partf[:, :, :], part[:, :, :]))
                    for t in range(NT):
                        at = slice(t * K, (t + 1) * K)
                        if t >= LIST_DEPTH:
                            dve.wait_ge(listed, t - LIST_DEPTH + 1)
                        dve.tensor_tensor(in_row[:, t % LIST_DEPTH, :, :], iota.unsqueeze(1).broadcast_to([P, K, P]),
                                          partf[:, 0, at].unsqueeze(2).broadcast_to([P, K, P]), ALU.is_equal)
                        dve.tensor_tensor(in_slot[:, t % LIST_DEPTH, 0], iota[:, 0:SLOTS].unsqueeze(1).broadcast_to([P, K, SLOTS]),
                                          partf[:, 1, at].unsqueeze(2).broadcast_to([P, K, SLOTS]),
                                          ALU.is_equal).then_inc(in_slot_ready, 1)
                    dve.wait_ge(listed, NT)
                    dve.tensor_copy(ids[:, :], bank[3][:, 0:SLOTS])
                    dve.tensor_copy(wts[:, :], bank[3][:, SLOTS:2 * SLOTS])

        with ExitStack() as inner:
            def sb(name, shape, dt=F32):
                return inner.enter_context(nc.sbuf_tensor(name + tag, shape, dt))

            DEPTH = SLOT_DEPTH
            assert TURNS * DEPTH == SLOTS
            who = sb("who", [P, DEPTH], U32)
            xg = sb("xg", [P, DEPTH, D])
            xgT = sb("xgT", [P, 2, DC, P])
            act_g = sb("act_g", [P, 2, INTER])
            h = sb("h", [P, 2, 2 * IC])
            hT = sb("hTs", [IC, 2, 2, P])
            y = sb("y", [P, DEPTH, D])
            x_gathered = g["x_gathered"]
            y_stored = g["y_stored"]
            who_ready = sem("who_ready")
            who_seen = sem("who_seen")
            cleared = sem("cleared")
            x_turned = sem("x_turned")
            xgT_done = sem("xgT_done")
            gu_done = sem("gu_done")
            silu_done = sem("silu_done")
            h_done = sem("h_done_s")
            h_turned = sem("h_turned")
            hT_done = sem("hT_done")
            down_done = sem("down_done")
            y_done = sem("y_done")
            TX, TH, G, Y = bank[0:2], bank[2:4], bank[4:6], bank[6:8]

            with nc.Block() as block:
                @block.sync
                def _(sp):
                    def store(turn, j):
                        s = turn * DEPTH + j
                        sp.wait_ge(y_done, s + 1)
                        sp.dma_start(g["y_dram"][bass.ds(s * P, P), :], y[:, j, :]).then_inc(y_stored[j], 16)

                    with sp.Fori(0, TURNS - 1) as turn:
                        for j in range(DEPTH):
                            sp.wait_ge(down_done, turn * DEPTH + j + 1)
                            load_expert(sp, j, turn * DEPTH + DEPTH + j)
                            store(turn, j)
                    for j in range(DEPTH):
                        store(TURNS - 1, j)
                    for j in range(DEPTH):
                        sp.wait_ge(y_stored[j], 16 * TURNS * (run + 1))

                @block.gpsimd
                def _(pool):
                    pool.memset(h[:, :, :], 0.0).then_inc(cleared, 1)

                    def gather(s, j):
                        pool.tensor_copy(who[:, j:j + 1], ids[:, bass.ds(s, 1)]).then_inc(who_ready, 1)
                        pool.wait_ge(who_ready, s + 1)
                        pool.sem_inc(who_seen, 1)
                        pool.indirect_dma_start(xg[:, j, :], None, g["xn_dram"],
                                                bass.IndirectOffsetOnAxis(ap=who[:, j:j + 1], axis=0),
                                                ).then_inc(x_gathered[j], 16)

                    for j in range(DEPTH):
                        gather(j, j)
                    with pool.Fori(0, TURNS - 1) as turn:
                        for j in range(DEPTH):
                            pool.wait_ge(x_turned, turn * DEPTH + j + 1)
                            gather(turn * DEPTH + DEPTH + j, j)

                @block.tensor
                def _(pe):
                    def turn_x(turn, j):
                        s = turn * DEPTH + j
                        pe.wait_ge(x_gathered[j], 16 * (turn + 1 + run * TURNS))
                        if not (isinstance(turn, int) and s < 2):
                            pe.wait_ge(xgT_done, s - 1)
                        for c in range(DC):
                            last = pe.transpose(TX[j % 2][:, c * P:(c + 1) * P], xg[:, j, c * P:(c + 1) * P],
                                                g["ident"][:, :])
                        last.then_inc(x_turned, 1)

                    def gate_up(turn, j):
                        s = turn * DEPTH + j
                        pe.wait_ge(w_loaded[j], 32 * (turn + 1 + run * TURNS))
                        pe.wait_ge(xgT_done, s + 1)
                        if not (isinstance(turn, int) and s < 2):
                            pe.wait_ge(h_done, s - 1)
                        for c in range(DC):
                            last = pe.matmul(G[j % 2][:, 0:2 * INTER], xgT[:, j % 2, c, :], w13[:, j, c, :],
                                             start=(c == 0), stop=(c == DC - 1))
                        last.then_inc(gu_done, 1)

                    def turn_h(turn, j):
                        s = turn * DEPTH + j
                        pe.wait_ge(h_done, s + 1)
                        if not (isinstance(turn, int) and s < 2):
                            pe.wait_ge(hT_done, s - 1)
                        for c in range(2):
                            last = pe.transpose(TH[j % 2][0:IC, c * P:(c + 1) * P], h[:, j % 2, c * IC:(c + 1) * IC],
                                                g["ident"][:, :])
                        last.then_inc(h_turned, 1)

                    def down(turn, j):
                        s = turn * DEPTH + j
                        pe.wait_ge(hT_done, s + 1)
                        if not (isinstance(turn, int) and s < 2):
                            pe.wait_ge(y_done, s - 1)
                        for c in range(2):
                            last = pe.matmul(Y[j % 2][:, 0:D], hT[:, j % 2, c, :], w2[:, j, c, :],
                                             start=(c == 0), stop=(c == 1))
                        last.then_inc(down_done, 1)

                    def slots(turn, first=False, final=False):
                        for j in range(DEPTH):
                            before = (turn, j - 1) if j > 0 else (turn - 1, DEPTH - 1)
                            if j > 0 or not first:
                                turn_h(*before)
                            if j < DEPTH - 1:
                                turn_x(turn, j + 1)
                            elif not final:
                                turn_x(turn + 1, 0)
                            gate_up(turn, j)
                            if first and j == 1:
                                pe.wait_ge(gu_read, 2 * (EARLY + 1))
                            if j > 0 or not first:
                                down(*before)

                    shared_up(pe, EARLY)
                    turn_x(0, 0)
                    slots(0, first=True)
                    with pe.Fori(1, TURNS - 1) as turn:
                        slots(turn)
                    slots(TURNS - 1, final=True)
                    turn_h(TURNS - 1, DEPTH - 1)
                    down(TURNS - 1, DEPTH - 1)
                    shared_up(pe, EARLY + 1)

                @block.scalar
                def _(act):
                    def silu(turn, j):
                        act.wait_ge(gu_done, turn * DEPTH + j + 1)
                        act.activation(act_g[:, j % 2, :], G[j % 2][:, 0:INTER], ACT.Silu).then_inc(silu_done, 1)

                    def weigh(turn, j):
                        s = turn * DEPTH + j
                        act.wait_ge(down_done, s + 1)
                        if not (isinstance(turn, int) and turn + run == 0):
                            act.wait_ge(y_stored[j], 16 * (turn + run * TURNS))
                        act.activation(y[:, j, :], Y[j % 2][:, 0:D], ACT.Copy,
                                       scale=wts[:, bass.ds(s, 1)]).then_inc(y_done, 1)

                    def slots(turn, first=False):
                        for j in range(DEPTH):
                            silu(turn, j)
                            if j > 0:
                                weigh(turn, j - 1)
                            elif not first:
                                weigh(turn - 1, DEPTH - 1)

                    shared_silu(act, EARLY)
                    slots(0, first=True)
                    with act.Fori(1, TURNS) as turn:
                        slots(turn)
                    weigh(TURNS - 1, DEPTH - 1)

                @block.vector
                def _(dve):
                    dve.wait_ge(cleared, 1)

                    def copy_x(turn, j):
                        dve.wait_ge(x_turned, turn * DEPTH + j + 1)
                        dve.tensor_copy(xgT[:, j % 2, :, :],
                                        TX[j % 2][:, 0:D].rearrange("p (c n) -> p c n", c=DC)).then_inc(xgT_done, 1)

                    def gate(turn, j):
                        s = turn * DEPTH + j
                        dve.wait_ge(silu_done, s + 1)
                        dve.tensor_tensor(h[:, j % 2, 0:INTER], G[j % 2][:, INTER:2 * INTER], act_g[:, j % 2, :],
                                          ALU.mult).then_inc(h_done, 1)

                    def copy_h(turn, j):
                        dve.wait_ge(h_turned, turn * DEPTH + j + 1)
                        dve.tensor_copy(hT[:, j % 2, :, :],
                                        TH[j % 2][0:IC, 0:D].rearrange("p (c n) -> p c n", c=2)).then_inc(hT_done, 1)

                    def slots(turn, first=False, final=False):
                        for j in range(DEPTH):
                            if j > 0:
                                copy_h(turn, j - 1)
                            elif not first:
                                copy_h(turn - 1, DEPTH - 1)
                            if j < DEPTH - 1:
                                copy_x(turn, j + 1)
                            elif not final:
                                copy_x(turn + 1, 0)
                            gate(turn, j)

                    copy_x(0, 0)
                    shared_h(dve, EARLY)
                    slots(0, first=True)
                    with dve.Fori(1, TURNS - 1) as turn:
                        slots(turn)
                    slots(TURNS - 1, final=True)
                    copy_h(TURNS - 1, DEPTH - 1)

        with ExitStack() as inner:
            DEPTH = GATHER_DEPTH
            yg = inner.enter_context(nc.sbuf_tensor("yg" + tag, [P, DEPTH, D], F32))
            gathered = g["y_gathered"]
            summed = sem("y_summed")
            x_done = sem("x_done")
            next_norm = Norm(inner, nc, g, tag + "n", before + 1)
            with nc.Block() as block:
                @block.gpsimd
                def _(pool):
                    for n in range(NT * K):
                        if n >= DEPTH:
                            pool.wait_ge(summed, n - DEPTH + 1)
                        pool.indirect_dma_start(yg[:, n % DEPTH, :], None, g["y_dram"],
                                                bass.IndirectOffsetOnAxis(ap=place[:, n:n + 1].bitcast(U32), axis=0),
                                                ).then_inc(gathered[n % DEPTH], 16)

                @block.tensor
                def _(pe):
                    for n in range(EARLY + 2, 2 * SHARED_CHUNKS):
                        shared_up(pe, n)
                    pe.wait_ge(sh_done, 2 * SHARED_CHUNKS)
                    pe.wait_ge(gu_read, 4 * SHARED_CHUNKS)
                    pe.wait_ge(loaded["se_down"], 16)
                    for t in range(NT):
                        for c in range(SHARED_CHUNKS):
                            last = pe.matmul(bank[4 + t // 2][:, (t % 2) * D:(t % 2 + 1) * D],
                                             shT[:, c, t * P:(t + 1) * P], g["se_down"][:, c, :],
                                             start=(c == 0), stop=(c == SHARED_CHUNKS - 1))
                        if t % 2:
                            last.then_inc(shared, 1)

                @block.scalar
                def _(act):
                    for n in range(EARLY + 1, 2 * SHARED_CHUNKS):
                        shared_silu(act, n)

                @block.vector
                def _(dve):
                    def add_shared(m):
                        dve.wait_ge(shared, m + 1)
                        dve.wait_ge(summed, (2 * m + 2) * K)
                        for t in (2 * m, 2 * m + 1):
                            dve.scalar_tensor_tensor(g["x"][:, t, :], bank[4 + m][:, (t % 2) * D:(t % 2 + 1) * D],
                                                     small[:, 5, t:t + 1], g["x"][:, t, :], ALU.mult,
                                                     ALU.add).then_inc(x_done, 1)
                            if not final:
                                dve.wait_ge(x_done, t + 1)
                                next_norm.sums(dve, g, t)

                    late = list(range(EARLY + 1, 2 * SHARED_CHUNKS))
                    for n in range(NT * K):
                        if n % 2 == 0 and late:
                            shared_h(dve, late.pop(0))
                        if n % (2 * K) == 0 and n // (2 * K) >= 2:
                            add_shared(n // (2 * K) - 2)
                        dve.wait_ge(gathered[n % DEPTH], 16 * (n // DEPTH + 1 + run * NT * K // DEPTH))
                        if n % K:
                            dve.wait_ge(summed, n)
                        dve.tensor_tensor(g["x"][:, n // K, :], g["x"][:, n // K, :], yg[:, n % DEPTH, :],
                                          ALU.add).then_inc(summed, 1)
                    add_shared(NT // 2 - 2)
                    add_shared(NT // 2 - 1)


def _rope(dim, scale):
    inv = (1.0 / 10000.0 ** (np.arange(0, dim, 2, dtype=np.float32) / np.float32(dim))).astype(np.float32)
    f = np.outer(np.arange(SEQ, dtype=np.float32), inv).astype(np.float32)
    f = np.concatenate([f, f], axis=1)
    sign = np.where(np.arange(dim) < dim // 2, -1.0, 1.0)
    both = np.stack([np.cos(f), np.sin(f) * sign], axis=1) * scale
    return np.ascontiguousarray(both.reshape(2, P, 2, dim).transpose(1, 0, 2, 3).astype(np.float32))


def _chunks(w):
    return np.ascontiguousarray(w.reshape(-1, P, w.shape[-1]).transpose(1, 0, 2))


def kernel(**inputs):
    import ml_dtypes
    import concourse.bacc as bacc
    from concourse.bass_utils import run_bass_kernel_spmd

    x = {k.replace("L0_", ""): np.asarray(v) for k, v in inputs.items()}
    wq = x["attn_a_wq"].reshape(D, HEADS, NOPE + ROPE)
    wkv = x["attn_a_wkv_b"].reshape(KVR, HEADS, NOPE + VD)
    se_up = np.zeros((D, 2, SHARED_CHUNKS * P), np.float32)
    se_up[:, :, 0:704] = x["ffn_se_gate_up_w"].T.reshape(D, 2, 704)
    se_down = np.zeros((SHARED_CHUNKS * P, D), np.float32)
    se_down[0:704] = x["ffn_se_down_w"].T
    w2 = np.zeros((EXPERTS, 2 * IC, D), np.float32)
    w2[:, 0:INTER] = x["ffn_w2"].transpose(0, 2, 1)
    wo_b = np.zeros((HEADS, 2 * HD, D), np.float32)
    wo_b[:, 0:HD] = x["attn_b_Wo"].T.reshape(HEADS, HD, D)
    p = np.arange(P)
    count = np.concatenate([
        np.broadcast_to(p, (P, P)), p[:, None] < p[None, :], np.ones((P, P)),
        np.broadcast_to(np.arange(8) * P, (P, 8)), np.arange(8) * P + p[:, None], p[:, None],
    ], axis=1).astype(np.float32)
    mask = np.stack([np.eye(P), np.where(p[None, :] > p[:, None], -3e38, 0.0)], axis=1).astype(ml_dtypes.bfloat16)
    arrays = {
        "x": x["attn_a_x"].reshape(TOK, D),
        "ident": np.eye(P, dtype=np.float32),
        "mask": mask,
        "wq_nopeT": wq[:, :, 0:NOPE].transpose(2, 1, 0),
        "wq_rope": _chunks(wq[:, :, NOPE:].reshape(D, HEADS * ROPE)),
        "wkT": wkv[:, :, 0:NOPE].transpose(2, 1, 0),
        "wvT": wkv[:, :, NOPE:].transpose(2, 1, 0),
        "wo_a": x["attn_a_wo"].reshape(HEADS, VD, D).transpose(1, 0, 2),
        "wkv_a": _chunks(x["attn_a_wkv_a"]),
        "kv_w": np.broadcast_to(x["attn_a_kv_norm_w"], (P, KVR)),
        "rope_k": _rope(ROPE, 1.0),
        "rope_q": _rope(ROPE, float(NOPE + ROPE) ** -0.5),
        "gate": _chunks(np.concatenate([x["ffn_gate_w"], x["ffn_shared_gate_w"]]).T),
        "se_up": _chunks(se_up.reshape(D, -1)),
        "se_down": _chunks(se_down),
        "count": count,
        "w_rot": _chunks(np.concatenate([x["attn_b_Wq"], x["attn_b_Wk"], x["attn_b_Wv"]]).T),
        "rope_b": np.stack([_rope(HD, float(HD) ** -0.5), _rope(HD, 1.0)], axis=2),
        "wo_b": wo_b.reshape(4, P, D).transpose(1, 0, 2),
        "w13": x["ffn_w13"].transpose(0, 2, 1).reshape(EXPERTS, DC, P, 2 * INTER).transpose(0, 2, 1, 3),
        "w2": w2.reshape(EXPERTS, 2, IC, D).transpose(0, 2, 1, 3),
    }
    arrays = {k: np.ascontiguousarray(v) for k, v in arrays.items()}
    nc = bacc.Bacc("TRN2", target_bir_lowering=False, num_devices=1)
    aps = {k: nc.dram_tensor(k + "_dram", v.shape, mybir.dt.from_np(v.dtype), kind="ExternalInput").ap()
           for k, v in arrays.items()}
    out = nc.dram_tensor("out_dram", (TOK, D), F32, kind="ExternalOutput").ap()
    build(nc, aps, out)
    r = run_bass_kernel_spmd(nc, [{k + "_dram": v for k, v in arrays.items()}], core_ids=[0])
    return r.results[0]["out_dram"].reshape(BATCH, SEQ, D)
```
